# Optimizing a Trainium2 kernel written in Bass

```python
import numpy as np
import jax
import jax.numpy as jnp

def _softmax(x, axis=-1):
    return jax.nn.softmax(x, axis=axis)

def _gelu(x):
    return jax.nn.gelu(x, approximate=True)

def _silu(x):
    return jax.nn.silu(x)

def _sigmoid(x):
    return jax.nn.sigmoid(x)

def _layernorm(x, axis=-1, eps=1e-05):
    m = jnp.mean(x, axis=axis, keepdims=True)
    v = jnp.var(x, axis=axis, keepdims=True)
    return (x - m) / jnp.sqrt(v + eps)

def _scatter_add(tgt, idx, src, axis=0):
    return tgt.at[idx].add(src)

def _segment_sum(src, seg, n):
    return jax.ops.segment_sum(src, seg, n)
kernel_name = 'mk_macaron_d2_jaxref_r8_820016'

def setup_inputs(seed: int=0):
    np.random.seed(seed)
    _w = jnp.asarray

    def _L0_attn_setup():
        import jax, jax.numpy as jnp
        import numpy as np
        B, S, E, H = (2, 256, 128, 8)
        DH = E // H
        F = DH // 2
        key = jax.random.key(seed)
        ks = jax.random.split(key, 7)
        sc = E ** (-0.5)
        return {'x': jax.random.normal(ks[0], (B, S, E), dtype=jnp.float32), 'Wq': jax.random.normal(ks[1], (E, E), dtype=jnp.float32) * sc, 'Wk': jax.random.normal(ks[2], (E, E), dtype=jnp.float32) * sc, 'Wv': jax.random.normal(ks[3], (E, E), dtype=jnp.float32) * sc, 'norm_w': jnp.ones((H, DH), dtype=jnp.float32), 'Wo': jax.random.normal(ks[4], (E, E), dtype=jnp.float32) * sc, 'bo': jnp.zeros((E,), dtype=jnp.float32), 'diff_weight': jnp.float32(0.2)}
    _L0_attn_in = _L0_attn_setup()

    def _L0_ffn_setup():
        import jax, jax.numpy as jnp
        import numpy as np
        DIM = 128
        DEPTH = 6
        HEADS = 16
        DIM_HEAD = 64
        WINDOW = 32
        INNER = HEADS * DIM_HEAD
        DIM_INNER = int(DIM * 4 * 2 / 3)
        QK_SCALE = 8.0

        def shift_tokens(t):
            a, s = jnp.split(t, 2, -1)
            s = jnp.pad(s, ((0, 0), (1, 0), (0, 0)))[:, :-1]
            return jnp.concatenate([a, s], -1)

        def l2norm(t):
            return t / jnp.maximum(jnp.linalg.norm(t, axis=-1, keepdims=True), 1e-12)

        def rotate_half(x):
            x1, x2 = jnp.split(x, 2, -1)
            return jnp.concatenate([-x2, x1], -1)

        def rotary_tables(n):
            half = jnp.arange(0, DIM_HEAD, 2, dtype=jnp.float32)
            inv_freq = 1.0 / 10000.0 ** (half / DIM_HEAD)
            t = jnp.arange(n, dtype=jnp.float32)
            freqs = t[:, None] * inv_freq[None, :]
            freqs = jnp.concatenate([freqs, freqs], -1)
            base_scale = (half + 0.4 * DIM_HEAD) / (1.4 * DIM_HEAD)
            power = (t - n // 2) / (WINDOW // 2)
            scale = base_scale[None, :] ** power[:, None]
            scale = jnp.concatenate([scale, scale], -1)
            return (freqs, scale)

        def local_attention(q, k, v):
            b, h, n, d = q.shape
            w = WINDOW
            nw = n // w
            bq = q.reshape(b, h, nw, w, d)
            bk = k.reshape(b, h, nw, w, d)
            bv = v.reshape(b, h, nw, w, d)

            def look(t):
                p = jnp.pad(t, ((0, 0), (0, 0), (1, 0), (0, 0), (0, 0)))
                return jnp.concatenate([p[:, :, :nw], p[:, :, 1:]], axis=3)
            bk2, bv2 = (look(bk), look(bv))
            seq = jnp.arange(n).reshape(nw, w)
            seq_p = jnp.pad(seq, ((1, 0), (0, 0)), constant_values=-1)
            jt = jnp.concatenate([seq_p[:nw], seq_p[1:]], axis=1)
            it = seq[:, :, None]
            jb = jt[:, None, :]
            mask = (it < jb) | (it > jb + w) | (jb == -1)
            sim = jnp.einsum('bhwie,bhwje->bhwij', bq, bk2) * QK_SCALE
            sim = jnp.where(mask, -jnp.finfo(sim.dtype).max, sim)
            attn = jax.nn.softmax(sim, -1)
            out = jnp.einsum('bhwij,bhwje->bhwie', attn, bv2)
            return out.reshape(b, h, n, d)

        def attn_layer(x, Wqkv, qs, ksc, Wo):
            b, n, _ = x.shape
            qkv = x @ Wqkv
            q, k, v = jnp.split(qkv, 3, -1)
            sh = lambda t: t.reshape(b, n, HEADS, DIM_HEAD).transpose(0, 2, 1, 3)
            q, k, v = (sh(q), sh(k), sh(v))
            q = l2norm(q) * qs
            k = l2norm(k) * ksc
            freqs, scale = rotary_tables(n)
            cos, sin = (jnp.cos(freqs), jnp.sin(freqs))
            q = q * cos * scale + rotate_half(q) * sin * scale
            inv = 1.0 / scale
            k = k * cos * inv + rotate_half(k) * sin * inv
            out = local_attention(q, k, v)
            out = out.transpose(0, 2, 1, 3).reshape(b, n, INNER)
            return out @ Wo

        def ffn_layer(x, g, bln, W1, b1, W2, b2):
            mu = x.mean(-1, keepdims=True)
            var = ((x - mu) ** 2).mean(-1, keepdims=True)
            xn = (x - mu) / jnp.sqrt(var + 1e-05) * g + bln
            hg = xn @ W1 + b1
            a, gate = jnp.split(hg, 2, -1)
            return a * jax.nn.gelu(gate, approximate=False) @ W2 + b2
        key = jax.random.key(seed)
        ks = jax.random.split(key, 8)
        B, N = (2, 256)
        init = lambda k, shape: jax.random.normal(k, shape, jnp.float32) * 0.02
        return {'x': jax.random.normal(ks[0], (B, N, DIM), jnp.float32), 'Wqkv': init(ks[1], (DEPTH, DIM, 3 * INNER)), 'q_scale': jnp.ones((DEPTH, DIM_HEAD), jnp.float32), 'k_scale': jnp.ones((DEPTH, DIM_HEAD), jnp.float32), 'Wo': init(ks[2], (DEPTH, INNER, DIM)), 'ln_g': jnp.ones((DEPTH, DIM), jnp.float32), 'ln_b': jnp.zeros((DEPTH, DIM), jnp.float32), 'W1': init(ks[3], (DEPTH, DIM, 2 * DIM_INNER)), 'b1': jnp.zeros((DEPTH, 2 * DIM_INNER), jnp.float32), 'W2': init(ks[4], (DEPTH, DIM_INNER, DIM)), 'b2': jnp.zeros((DEPTH, DIM), jnp.float32)}
    _L0_ffn_in = _L0_ffn_setup()

    def _L1_attn_setup():
        import jax, jax.numpy as jnp
        import numpy as np
        B, T, E, H = (4, 256, 128, 16)
        S = E // H
        key = jax.random.key(seed)
        ks = jax.random.split(key, 4)
        x = jax.random.normal(ks[0], (B, T, E), dtype=jnp.float32)
        Wk = jax.random.normal(ks[1], (E, E), dtype=jnp.float32) * E ** (-0.5)
        Wq = jax.random.normal(ks[2], (E, E), dtype=jnp.float32) * E ** (-0.5)
        Wo = jax.random.normal(ks[3], (E, E), dtype=jnp.float32) * E ** (-0.5)
        bo = jnp.zeros((E,), dtype=jnp.float32)
        return {'x': x, 'Wk': Wk, 'Wq': Wq, 'Wo': Wo, 'bo': bo}
    _L1_attn_in = _L1_attn_setup()

    def _L1_ffn_setup():
        import jax, jax.numpy as jnp
        import numpy as np
        DIM = 128
        HIDDEN = 384
        SCALE = 1.0 / 127.0

        def _dequant(w_int, dtype):
            return w_int.astype(dtype) * jnp.asarray(SCALE, dtype)
        key = jax.random.key(seed)
        k_x, k_g, k_u, k_d = jax.random.split(key, 4)
        x = jax.random.normal(k_x, (4, 256, DIM), dtype=jnp.float32)
        w_gate = jax.random.randint(k_g, (HIDDEN, DIM), -127, 128, dtype=jnp.int32)
        w_up = jax.random.randint(k_u, (HIDDEN, DIM), -127, 128, dtype=jnp.int32)
        w_down = jax.random.randint(k_d, (DIM, HIDDEN), -127, 128, dtype=jnp.int32)
        return {'x': x, 'w_gate': w_gate, 'w_up': w_up, 'w_down': w_down}
    _L1_ffn_in = _L1_ffn_setup()
    _d = {'L0_attn_x': _L0_attn_in['x'], 'L0_attn_Wq': _L0_attn_in['Wq'], 'L0_attn_Wk': _L0_attn_in['Wk'], 'L0_attn_Wv': _L0_attn_in['Wv'], 'L0_attn_norm_w': _L0_attn_in['norm_w'], 'L0_attn_Wo': _L0_attn_in['Wo'], 'L0_attn_bo': _L0_attn_in['bo'], 'L0_attn_diff_weight': _L0_attn_in['diff_weight'], 'L0_ffn_Wqkv': _L0_ffn_in['Wqkv'], 'L0_ffn_q_scale': _L0_ffn_in['q_scale'], 'L0_ffn_k_scale': _L0_ffn_in['k_scale'], 'L0_ffn_Wo': _L0_ffn_in['Wo'], 'L0_ffn_ln_g': _L0_ffn_in['ln_g'], 'L0_ffn_ln_b': _L0_ffn_in['ln_b'], 'L0_ffn_W1': _L0_ffn_in['W1'], 'L0_ffn_b1': _L0_ffn_in['b1'], 'L0_ffn_W2': _L0_ffn_in['W2'], 'L0_ffn_b2': _L0_ffn_in['b2'], 'L1_attn_Wk': _L1_attn_in['Wk'], 'L1_attn_Wq': _L1_attn_in['Wq'], 'L1_attn_Wo': _L1_attn_in['Wo'], 'L1_attn_bo': _L1_attn_in['bo'], 'L1_ffn_w_gate': _L1_ffn_in['w_gate'], 'L1_ffn_w_up': _L1_ffn_in['w_up'], 'L1_ffn_w_down': _L1_ffn_in['w_down']}
    _x0 = _d['L0_attn_x']
    _d['L0_attn_x'] = jax.random.normal(jax.random.fold_in(jax.random.key(seed), 1), (8, 256, 128), dtype=_x0.dtype)
    del _x0
    return _d

def reference(L0_attn_x, L0_attn_Wq, L0_attn_Wk, L0_attn_Wv, L0_attn_norm_w, L0_attn_Wo, L0_attn_bo, L0_attn_diff_weight, L0_ffn_Wqkv, L0_ffn_q_scale, L0_ffn_k_scale, L0_ffn_Wo, L0_ffn_ln_g, L0_ffn_ln_b, L0_ffn_W1, L0_ffn_b1, L0_ffn_W2, L0_ffn_b2, L1_attn_Wk, L1_attn_Wq, L1_attn_Wo, L1_attn_bo, L1_ffn_w_gate, L1_ffn_w_up, L1_ffn_w_down):

    def _L0_attn_ref(x, Wq, Wk, Wv, norm_w, Wo, bo, diff_weight):
        import jax, jax.numpy as jnp
        import numpy as np
        B, S, E, H = (2, 256, 128, 8)
        DH = E // H
        F = DH // 2
        b, s, e = x.shape
        qs = (x @ Wq.T).reshape(b, s, H, 2, F)
        ks_ = (x @ Wk.T).reshape(b, s, H, 2, F)
        vs = (x @ Wv.T).reshape(b, s, H, DH)
        scale = F ** (-0.5)
        scores = jnp.einsum('bqhif,bkhif->ibhqk', qs, ks_) * scale
        atts = jax.nn.softmax(scores, axis=-1)
        att = atts[0] - diff_weight * atts[1]
        o = jnp.einsum('bhqk,bkhe->bqhe', att, vs)
        eps = jnp.finfo(o.dtype).eps
        rms = jax.lax.rsqrt(jnp.mean(o * o, axis=(-2, -1), keepdims=True) + eps)
        normed = (o * rms * norm_w).reshape(b, s, e)
        return (normed @ Wo.T + bo) * (1.0 - diff_weight)

    def _L0_ffn_ref(x, Wqkv, q_scale, k_scale, Wo, ln_g, ln_b, W1, b1, W2, b2):
        import jax, jax.numpy as jnp
        import numpy as np
        DIM = 128
        DEPTH = 6
        HEADS = 16
        DIM_HEAD = 64
        WINDOW = 32
        INNER = HEADS * DIM_HEAD
        DIM_INNER = int(DIM * 4 * 2 / 3)
        QK_SCALE = 8.0

        def shift_tokens(t):
            a, s = jnp.split(t, 2, -1)
            s = jnp.pad(s, ((0, 0), (1, 0), (0, 0)))[:, :-1]
            return jnp.concatenate([a, s], -1)

        def l2norm(t):
            return t / jnp.maximum(jnp.linalg.norm(t, axis=-1, keepdims=True), 1e-12)

        def rotate_half(x):
            x1, x2 = jnp.split(x, 2, -1)
            return jnp.concatenate([-x2, x1], -1)

        def rotary_tables(n):
            half = jnp.arange(0, DIM_HEAD, 2, dtype=jnp.float32)
            inv_freq = 1.0 / 10000.0 ** (half / DIM_HEAD)
            t = jnp.arange(n, dtype=jnp.float32)
            freqs = t[:, None] * inv_freq[None, :]
            freqs = jnp.concatenate([freqs, freqs], -1)
            base_scale = (half + 0.4 * DIM_HEAD) / (1.4 * DIM_HEAD)
            power = (t - n // 2) / (WINDOW // 2)
            scale = base_scale[None, :] ** power[:, None]
            scale = jnp.concatenate([scale, scale], -1)
            return (freqs, scale)

        def local_attention(q, k, v):
            b, h, n, d = q.shape
            w = WINDOW
            nw = n // w
            bq = q.reshape(b, h, nw, w, d)
            bk = k.reshape(b, h, nw, w, d)
            bv = v.reshape(b, h, nw, w, d)

            def look(t):
                p = jnp.pad(t, ((0, 0), (0, 0), (1, 0), (0, 0), (0, 0)))
                return jnp.concatenate([p[:, :, :nw], p[:, :, 1:]], axis=3)
            bk2, bv2 = (look(bk), look(bv))
            seq = jnp.arange(n).reshape(nw, w)
            seq_p = jnp.pad(seq, ((1, 0), (0, 0)), constant_values=-1)
            jt = jnp.concatenate([seq_p[:nw], seq_p[1:]], axis=1)
            it = seq[:, :, None]
            jb = jt[:, None, :]
            mask = (it < jb) | (it > jb + w) | (jb == -1)
            sim = jnp.einsum('bhwie,bhwje->bhwij', bq, bk2) * QK_SCALE
            sim = jnp.where(mask, -jnp.finfo(sim.dtype).max, sim)
            attn = jax.nn.softmax(sim, -1)
            out = jnp.einsum('bhwij,bhwje->bhwie', attn, bv2)
            return out.reshape(b, h, n, d)

        def attn_layer(x, Wqkv, qs, ksc, Wo):
            b, n, _ = x.shape
            qkv = x @ Wqkv
            q, k, v = jnp.split(qkv, 3, -1)
            sh = lambda t: t.reshape(b, n, HEADS, DIM_HEAD).transpose(0, 2, 1, 3)
            q, k, v = (sh(q), sh(k), sh(v))
            q = l2norm(q) * qs
            k = l2norm(k) * ksc
            freqs, scale = rotary_tables(n)
            cos, sin = (jnp.cos(freqs), jnp.sin(freqs))
            q = q * cos * scale + rotate_half(q) * sin * scale
            inv = 1.0 / scale
            k = k * cos * inv + rotate_half(k) * sin * inv
            out = local_attention(q, k, v)
            out = out.transpose(0, 2, 1, 3).reshape(b, n, INNER)
            return out @ Wo

        def ffn_layer(x, g, bln, W1, b1, W2, b2):
            mu = x.mean(-1, keepdims=True)
            var = ((x - mu) ** 2).mean(-1, keepdims=True)
            xn = (x - mu) / jnp.sqrt(var + 1e-05) * g + bln
            hg = xn @ W1 + b1
            a, gate = jnp.split(hg, 2, -1)
            return a * jax.nn.gelu(gate, approximate=False) @ W2 + b2
        for i in range(DEPTH):
            x = attn_layer(shift_tokens(x), Wqkv[i], q_scale[i], k_scale[i], Wo[i]) + x
            x = ffn_layer(shift_tokens(x), ln_g[i], ln_b[i], W1[i], b1[i], W2[i], b2[i]) + x
        return x

    def _L1_attn_ref(x, Wk, Wq, Wo, bo):
        import jax, jax.numpy as jnp
        import numpy as np
        B, T, E, H = (4, 256, 128, 16)
        S = E // H
        b, t, e = x.shape
        h, s = (H, E // H)
        scale = e ** (-0.25)
        k = (x @ Wk).reshape(b, t, h, s).transpose(0, 2, 1, 3)
        q = (x @ Wq).reshape(b, t, h, s).transpose(0, 2, 1, 3)
        v = (x @ Wk).reshape(b, t, h, s).transpose(0, 2, 1, 3)
        dot = jnp.einsum('bhqd,bhkd->bhqk', q * scale, k * scale)
        attn = jax.nn.softmax(dot, axis=-1)
        out = jnp.einsum('bhqk,bhkd->bhqd', attn, v)
        out = out.transpose(0, 2, 1, 3).reshape(b, t, e)
        return out @ Wo + bo

    def _L1_ffn_ref(x, w_gate, w_up, w_down):
        import jax, jax.numpy as jnp
        import numpy as np
        DIM = 128
        HIDDEN = 384
        SCALE = 1.0 / 127.0

        def _dequant(w_int, dtype):
            return w_int.astype(dtype) * jnp.asarray(SCALE, dtype)
        wg = _dequant(w_gate, x.dtype)
        wu = _dequant(w_up, x.dtype)
        wd = _dequant(w_down, x.dtype)
        gate = jnp.einsum('bsd,hd->bsh', x, wg)
        up = jnp.einsum('bsd,hd->bsh', x, wu)
        h = jax.nn.silu(gate) * up
        return jnp.einsum('bsh,dh->bsd', h, wd)
    x = L0_attn_x
    x = x + 0.5 * _L0_ffn_ref(_layernorm(x, axis=-1), L0_ffn_Wqkv, L0_ffn_q_scale, L0_ffn_k_scale, L0_ffn_Wo, L0_ffn_ln_g, L0_ffn_ln_b, L0_ffn_W1, L0_ffn_b1, L0_ffn_W2, L0_ffn_b2)
    x = x + _L0_attn_ref(_layernorm(x, axis=-1), L0_attn_Wq, L0_attn_Wk, L0_attn_Wv, L0_attn_norm_w, L0_attn_Wo, L0_attn_bo, L0_attn_diff_weight)
    x = x + 0.5 * _L0_ffn_ref(_layernorm(x, axis=-1), L0_ffn_Wqkv, L0_ffn_q_scale, L0_ffn_k_scale, L0_ffn_Wo, L0_ffn_ln_g, L0_ffn_ln_b, L0_ffn_W1, L0_ffn_b1, L0_ffn_W2, L0_ffn_b2)
    x = x + 0.5 * _L1_ffn_ref(_layernorm(x, axis=-1), L1_ffn_w_gate, L1_ffn_w_up, L1_ffn_w_down)
    x = x + _L1_attn_ref(_layernorm(x, axis=-1), L1_attn_Wk, L1_attn_Wq, L1_attn_Wo, L1_attn_bo)
    x = x + 0.5 * _L1_ffn_ref(_layernorm(x, axis=-1), L1_ffn_w_gate, L1_ffn_w_up, L1_ffn_w_down)
    return x

_drawn_inputs = setup_inputs


def setup_inputs(seed=0):
    import zlib

    import numpy as np

    out = dict(_drawn_inputs(seed))
    spreads = {'L0_attn_norm_w': (1.0, 0.2),
     'L0_attn_bo': (0.0, 0.1),
     'L0_ffn_q_scale': (1.0, 0.6),
     'L0_ffn_k_scale': (1.0, 0.6),
     'L0_ffn_ln_g': (1.0, 0.6),
     'L0_ffn_ln_b': (0.0, 0.8),
     'L0_ffn_b1': (0.0, 0.413),
     'L0_ffn_b2': (0.0, 0.1),
     'L1_attn_bo': (0.0, 0.8)}
    factors = {'L1_attn_Wk': 8.0, 'L1_attn_Wq': 8.0, 'L1_attn_Wo': 8.0}
    for name, (base, spread) in spreads.items():
        noise = np.random.default_rng([zlib.crc32(name.encode()), seed]).standard_normal(out[name].shape)
        drawn = base * np.exp(spread * noise) if base else spread * noise
        out[name] = jnp.asarray(drawn.astype(out[name].dtype))
    for name, factor in factors.items():
        out[name] = (out[name] * factor).astype(out[name].dtype)
    return out
```

```python
import numpy as np
from contextlib import ExitStack

import concourse.bass as bass
from concourse import mybir

P = 128
GROUPS, QUADS, WINDOWS, WIN = 2, 4, 8, 32
SEQS, TOKENS = GROUPS * QUADS, WINDOWS * WIN
TILES = GROUPS * WINDOWS
BATCH = 512
BATCHES = SEQS * TOKENS // BATCH
DEPTH, HEADS, DH = 6, 16, 64
PAIRS = HEADS // 2
INNER = HEADS * DH
FF = int(P * 4 * 2 / 3)
FFC = [128, 128, FF - 256]
QK_SCALE = 8.0
HID = 384
PASSES = 2
MASKED = -1e30


def shape_constants():
    half = np.arange(0, DH, 2, dtype=np.float32)
    inv_freq = (1.0 / 10000.0 ** (half / DH)).astype(np.float32)
    t = np.arange(TOKENS, dtype=np.float32)
    freqs = t[:, None] * inv_freq[None, :]
    freqs = np.concatenate([freqs, freqs], -1).astype(np.float64)
    base = ((half + np.float32(0.4 * DH)) / np.float32(1.4 * DH)).astype(np.float64)
    power = (t.astype(np.float64) - TOKENS // 2) / (WIN // 2)
    scale = base[None, :] ** power[:, None]
    scale = np.concatenate([scale, scale], -1)
    sign = np.where(np.arange(DH) < DH // 2, -1.0, 1.0)[None, :]
    cos, sin = np.cos(freqs), np.sin(freqs) * sign
    tabs = np.stack([cos * scale, sin * scale, cos / scale, sin / scale])
    tabs = tabs.reshape(4, WINDOWS, 1, WIN, DH)
    tabs = np.broadcast_to(tabs, (4, WINDOWS, QUADS, WIN, DH))
    tabs = tabs.reshape(4, WINDOWS, P, DH).transpose(2, 0, 1, 3)
    i = np.arange(P)[:, None] % WIN
    j = np.arange(WIN)[None, :]
    own, prev = np.where(j <= i, 0.0, MASKED), np.where(j >= i, 0.0, MASKED)
    none = np.full((P, WIN), MASKED)
    mask = np.stack([np.concatenate(x, 1) for x in ([own, none], [prev, own], [own, prev])], 1)
    return (np.ascontiguousarray(tabs, np.float32), np.ascontiguousarray(mask, np.float32),
            np.eye(P, dtype=np.float32))


def macaron(nc, x, w, cst, out, stop_after=99):
    fp32, bf16, i32 = mybir.dt.float32, mybir.dt.bfloat16, mybir.dt.int32
    ALU, ACT, AX = mybir.AluOpType, mybir.ActivationFunctionType, mybir.AxisListType

    with ExitStack() as ctx:
        ctx.enter_context(nc.allow_non_contiguous_dma(reason="a layer's vectors, one element a partition"))

        def sb(name, shape, dt=fp32):
            return ctx.enter_context(nc.sbuf_tensor(name, shape, dt))

        def sem(name):
            return ctx.enter_context(nc.semaphore(name))

        X = sb("X", [P, GROUPS, WINDOWS + 1, P])
        Y = sb("Y", [P, GROUPS, WINDOWS + 1, P])
        Y2 = sb("Y2", [P, GROUPS, WINDOWS + 1, P])
        ident = sb("ident", [P, P])
        ident_bf = sb("ident_bf", [P, P], bf16)
        ones = sb("ones", [P, P])
        mean_w = sb("mean_w", [P, P])
        mhalf = sb("mhalf", [P, 1])
        zero_bf = sb("zero_bf", [P, P], bf16)
        mask_bf = sb("mask_bf", [P, 3, DH], bf16)
        tabs = sb("tabs", [P, 4, WINDOWS, DH])
        wqkv = sb("wqkv", [P, 3 * INNER])
        wo = sb("wo", [P, PAIRS, P])
        w1 = sb("w1", [P, 2 * FF])
        w2 = sb("w2", [P, 3, P])
        b1 = sb("b1", [P, 6])
        lnp = sb("lnp", [P, 3])
        qks = sb("qks", [P, 2, DH])
        rot = sb("rot", [P, 4, WINDOWS, DH])
        xst = sb("xst", [P, 2, P])
        sq = sb("sq", [P, 2, BATCH])
        t1 = sb("t1", [P, 2, 4, BATCH])
        t2 = sb("t2", [P, 2, BATCH])
        ss = sb("ss", [P, 2, 32])
        rn = sb("rn", [P, 2, 2, 32])
        qT = sb("qT", [P, PAIRS, P])
        kT = [sb(f"kT{g}", [P, PAIRS, QUADS, 2, WIN]) for g in range(2)]
        mx = sb("mx", [P, 2, 2, PAIRS])
        pr = sb("pr", [P, 2, PAIRS, 2, DH])
        sm = sb("sm", [P, 2, HEADS])
        rs = sb("rs", [P, 2, HEADS])
        pT = sb("pT", [P, PAIRS, P])
        vs = sb("vs", [P, 2, 2, BATCH])
        vj = [sb(f"vj{g}", [P, QUADS, BATCH]) for g in range(2)]
        osb = sb("osb", [P, PAIRS, 2, DH])
        oT = sb("oT", [P, PAIRS, 2, P])
        xs = sb("xs", [P, BATCHES, BATCH])
        cen = sb("cen", [P, BATCHES, BATCH])
        sqd = sb("sqd", [P, BATCHES, BATCH])
        ve = sb("ve", [P, TILES])
        rstd = sb("rstd", [P, TILES])

        wraw = sb("wraw", [P, 7, P])
        iraw = sb("iraw", [P, 3, HID], i32)
        wi = sb("wi", [P, 3, HID])
        vec = sb("vec", [P, 8])
        t1f = t1[:, :, :, :].rearrange("p g c n -> p (g c) n")
        pe_ring = pr[:, :, :, :, :].rearrange("p g m a k -> p (g m a k)").rearrange("p (r t k) -> p r t k", r=4, k=TOKENS)
        pn_ring = t1f[:, 0:2, :].rearrange("p r (t k) -> p r t k", t=2)
        pnT = t1f[:, 2:4, :].rearrange("p r (t k) -> p r t k", t=2)
        qp = t1f[:, 4:6, :].rearrange("p c (r k) -> p (c r) k", k=TOKENS)
        kp = t1f[:, 6:8, :].rearrange("p c (r k) -> p (c r) k", k=TOKENS)
        vpad = osb[:, :, :, :].rearrange("p m a d -> p (m a d)").rearrange("p (t h d) -> p t h d", t=2, d=32)
        oTf = oT[:, :, :, :].rearrange("p m g c -> p (m g c)").rearrange("p (n k) -> p n k", k=TOKENS)
        ys, on, osq, on2, odg, ott = (oTf[:, k, :] for k in range(6))
        rotf = rot[:, :, :, :].rearrange("p a w d -> p (a w d)")
        wqp, wkp = (rotf[:, 512 * k:512 * k + 512].rearrange("p (n d) -> p n d", d=32) for k in range(2))
        wv, wot = (rotf[:, 1024 + P * k:1152 + P * k] for k in range(2))
        nm = sb("nm", [P, HEADS, 2])
        dsum = sb("dsum", [P, HEADS, 2])
        drc = sb("drc", [P, 2, HEADS, 2])
        ave = sb("ave", [P, 2])
        ars = sb("ars", [P, 2])

        gl = sq
        hh = t1[:, :, 0:3, :]

        QB = [ctx.enter_context(nc.psum_tensor(f"QB{i}", [P, BATCH], fp32)) for i in range(2)]
        TB = [ctx.enter_context(nc.psum_tensor(f"TB{i}", [P, BATCH], fp32)) for i in range(2)]
        SB = [ctx.enter_context(nc.psum_tensor(f"SB{i}", [P, BATCH], fp32)) for i in range(2)]
        OB = [ctx.enter_context(nc.psum_tensor(f"OB{i}", [P, BATCH], fp32)) for i in range(2)]
        LNB = [QB[0], QB[1], TB[0], TB[1]]
        FFB = [SB[0], SB[1], OB[0], OB[1]]

        names = """cst_ld cst_done mask_done ln_xn x_ld xt_done xt_ev
            ln_mean ln_cen ln_sqd ln_ss ln_ve ln_rs ln_dg ln_bc ln_out
            wqkv_ld wo_ld ff_ld qs_ld tab_done xst_done
            qkv_done sq_done ss_done rot_done add_done nrm_max nrm_pow qk_done v_done vj_ld0 vj_ld1
            qkt_done qkt_ev sc_done mx_done sub_done exp_done sum_done rs_done
            pt_done pt_ev pv_done on_done ot_done ot_ev y_done y2_done
            xs_done h_done gelu_done hm_done f_done y_ready x_done
            raw_ld int_ld vec_done wt_done wt_ev wdup_done wi_cv wi_done wi_ev n_out
            ys_done aqk_done aqk_ev av_done av_ev as_done am_done ae_done ac_done ad_done an_half an_done at_done at_ev apv_done
            a_on a_sq a_ss a_ve a_rs a_dg a_bc a_on2 a_y a_yt
            on_T on_ev out_st""".split()
        S = {n: sem(n) for n in names}

        def batch(b, t):
            g, h = divmod(b, 2)
            return t[:, g, 1 + 4 * h:5 + 4 * h, :].rearrange("p w c -> p (w c)")

        def natural(ap):
            return [ap[s].rearrange("(w i) e -> i w e", i=WIN) for s in range(SEQS)]

        PHASES = [("stack", 0), ("attend", 0), ("stack", 1), ("ffn", 0), ("attend", 1), ("ffn", 1)]
        X_BEFORE = [0, 4, 12, 16, 20, 28, 32]
        NORM_NO = [0, 1 + DEPTH, 2 + DEPTH, 3 + 2 * DEPTH, 4 + 2 * DEPTH, 5 + 2 * DEPTH]

        def run(stack, attention, ffn):
            for k, (kind, p) in enumerate(PHASES[:stop_after]):
                {"stack": stack, "attend": attention, "ffn": ffn}[kind](p, NORM_NO[k], X_BEFORE[k])

        X_TOTAL = X_BEFORE[min(stop_after, len(PHASES))]

        DIFF = 0
        DHS = [16, 8]
        QS = [8.0 ** -0.5, float(P) ** -0.5]
        UNITS = [8, 16]
        ROWS = 16

        def unit_ready(kind, i):
            if not 0 <= i < ROWS:
                return None
            return i if kind else (i // 2 if i % 2 else None)

        def seq_cols(t, gq, jq):
            return t[:, bass.ds(gq, 1), 1:1 + WINDOWS, bass.ds(jq * WIN, WIN)].rearrange("p g w i -> p (g w) i")

        nat = xs[:, :, :].rearrange("p b (t e) -> p (b t) e", e=P)
        block = ctx.enter_context(nc.Block())

        CREDIT = 2
        PER_PASS = DEPTH * TILES

        def tile0(p, l):
            return l * TILES + (CREDIT + p * PER_PASS)

        def layer0(p, l):
            return l + p * DEPTH

        def ln_no(p, l):
            return l + ((DEPTH + 2) * p + 1)

        @block.sync
        def _(sp):
            sp.sem_inc(S["vj_ld0"], 128)
            sp.sem_inc(S["vj_ld1"], 128)
            for k, (dst, src) in enumerate(((tabs[:, :, :, :], cst[0]), (ident[:, :], cst[2]))):
                sp.dma_start(dst, src).then_inc(S["cst_ld"], 16)
            sp.dma_start(xs[:, 3, 0:3 * DH], cst[1].rearrange("p a b -> p (a b)")).then_inc(S["cst_ld"], 16)
            sp.wait_ge(S["mask_done"], 1)
            for s, src in enumerate(natural(x)):
                g, j = divmod(s, QUADS)
                sp.dma_start(nat[32 * j:32 * j + 32, g * WINDOWS:(g + 1) * WINDOWS, :], src).then_inc(S["x_ld"], 16)

            for k, n in enumerate(("L0_attn_Wq", "L0_attn_Wk", "L0_attn_Wv", "L0_attn_Wo", "L1_attn_Wq", "L1_attn_Wk", "L1_attn_Wo")):
                sp.dma_start(wraw[:, k, :], w[n]).then_inc(S["raw_ld"], 16)
            for k, src in ((0, w["L0_attn_diff_weight"].unsqueeze(0).to_broadcast([P, 1])),
                           (3, w["L0_attn_norm_w"].rearrange("h (d o) -> (h d) o", o=1)),
                           (4, w["L0_attn_bo"].rearrange("(p o) -> p o", o=1)), (6, w["L1_attn_bo"].rearrange("(p o) -> p o", o=1))):
                sp.dma_start(vec[:, k:k + 1], src).then_inc(S["raw_ld"], 16)
            for k, n in enumerate(("L1_ffn_w_gate", "L1_ffn_w_up")):
                sp.dma_start(iraw[:, k, :].rearrange("p (c d) -> p c d", d=P), w[n].rearrange("(c p) d -> p c d", p=P)).then_inc(S["int_ld"], 16)
            sp.dma_start(iraw[:, 2, :], w["L1_ffn_w_down"]).then_inc(S["int_ld"], 16)

            def stack(p, N0, xb):
                with sp.Fori(0, DEPTH) as l:
                    G, L = tile0(p, l), layer0(p, l)
                    sp.wait_ge(S["qkv_done"], G * 6)
                    sp.dma_start(wqkv[:, :], w["L0_ffn_Wqkv"][bass.ds(l, 1), :, :].rearrange("a p n -> p (a n)"),
                                 max_dma_last_dim=16384).then_inc(S["wqkv_ld"], 16)
                    sp.wait_ge(S["tab_done"], L * 4 + 4)
                    for k, n in enumerate(("L0_ffn_q_scale", "L0_ffn_k_scale")):
                        sp.dma_start(qks[:, k, :], w[n][bass.ds(l, 1), :].to_broadcast([P, DH])).then_inc(S["qs_ld"], 16)
                    sp.wait_ge(S["y_done"], L * WINDOWS + 1)
                    sp.dma_start(wo[:, :, :], w["L0_ffn_Wo"][bass.ds(l, 1), :, :].rearrange("a (m p) n -> p (a m) n", p=P)).then_inc(S["wo_ld"], 16)
                    sp.wait_ge(S["y_ready"], (L + (p + 1)) * BATCHES)
                    sp.dma_start(w1[:, :], w["L0_ffn_W1"][bass.ds(l, 1), :, :].rearrange("a p n -> p (a n)")).then_inc(S["ff_ld"], 16)
                    sp.dma_start(w2[:, 0:2, :], w["L0_ffn_W2"][bass.ds(l, 1), 0:256, :].rearrange("a (m p) n -> p (a m) n", p=P)).then_inc(S["ff_ld"], 16)
                    sp.dma_start(w2[0:FFC[2], 2, :], w["L0_ffn_W2"][bass.ds(l, 1), 256:FF, :].rearrange("a p n -> p (a n)")).then_inc(S["ff_ld"], 16)
                    for half in range(2):
                        o = half * FF
                        sp.dma_start(b1[:, 3 * half:3 * half + 2], w["L0_ffn_b1"][bass.ds(l, 1), o:o + 256].rearrange("a (m p) -> p (a m)", p=P)).then_inc(S["ff_ld"], 16)
                        sp.dma_start(b1[0:FFC[2], 3 * half + 2:3 * half + 3], w["L0_ffn_b1"][bass.ds(l, 1), o + 256:o + FF].rearrange("a p -> p a")).then_inc(S["ff_ld"], 16)
                    for k, n in enumerate(("L0_ffn_ln_g", "L0_ffn_ln_b", "L0_ffn_b2")):
                        sp.dma_start(lnp[:, k:k + 1], w[n][bass.ds(l, 1), :].rearrange("a p -> p a")).then_inc(S["ff_ld"], 16)

                    def spread(G, w_par, g):
                        sp.wait_ge(S["v_done"], G * 2 + 2)
                        for j in range(QUADS):
                            for h2 in range(2):
                                sp.dma_start(vj[g][64 * h2 + 32 * w_par:64 * h2 + 32 * w_par + 32, j, :],
                                             vs[32 * j:32 * j + 32, g, h2, :]).then_inc(S[f"vj_ld{g}"], 16)

                    with sp.Fori(0, WINDOWS // 2) as wp:
                        for k in range(4):
                            spread(G + wp * 4 + k, k // 2, k % 2)

            run(stack, lambda *a: None, lambda *a: None)
            sp.wait_ge(S["on_ev"], 4)
            for s, dst in enumerate(natural(out)):
                g, j = divmod(s, QUADS)
                sp.dma_start(dst, nat[32 * j:32 * j + 32, g * WINDOWS:(g + 1) * WINDOWS, :]).then_inc(S["out_st"], 16)
            sp.wait_ge(S["out_st"], 16 * SEQS)

        @block.gpsimd
        def _(gp):
            gp.memset(ones[:, :], 1.0).then_inc(S["cst_done"], 1)

            gp.wait_ge(S["cst_done"], 5)

            def power(N):
                gp.wait_ge(S["ln_ve"], N + 1)
                gp.tensor_tensor(rstd[:, :], ve[:, :], mhalf[:, 0:1].to_broadcast([P, TILES]), ALU.pow).then_inc(S["ln_rs"], 1)

            def project(G, g):
                for c in range(4):
                    gp.wait_ge(S["rot_done"], G * 8 + 2 * c + 2)
                    gp.tensor_tensor(t1[:, g, c, :], t1[:, g, c, :], t2[:, c % 2, :], ALU.add).then_inc(S["add_done"], 1)
                gp.wait_ge(S["nrm_max"], G + 1)
                gp.wait_ge(S["qk_done"], (G - 1) * 2)
                gp.tensor_tensor(rn[:, g, 1, :], rn[:, g, 0, :], mhalf[:, 0:1].to_broadcast([P, 32]), ALU.pow).then_inc(S["nrm_pow"], 1)
                gp.wait_ge(S["nrm_pow"], G + 1)
                gp.wait_ge(S["add_done"], G * 4 + 4)
                for k in range(2):
                    t = t1[:, g, 2 * k:2 * k + 2, :].rearrange("p c (h d) -> p (c h) d", d=DH)
                    r = rn[:, g, 1, 16 * k:16 * k + 16].unsqueeze(2).to_broadcast([P, 16, DH])
                    gp.tensor_tensor(t, t, r, ALU.mult).then_inc(S["qk_done"], 1)

            gp.sem_inc(S["nrm_pow"], CREDIT)
            gp.sem_inc(S["tab_done"], 4)
            gp.sem_inc(S["a_rs"], 1)
            gp.sem_inc(S["add_done"], 4 * CREDIT)
            gp.sem_inc(S["qk_done"], 2 * CREDIT)

            def attention(kind, N0, xb):
                power(N0)
                if kind == DIFF:
                    with gp.Fori(0, SEQS) as q:
                        gp.wait_ge(S["a_ve"], q + 2)
                        gp.tensor_tensor(ars[:, :], ave[:, :], mhalf[:, 0:1].to_broadcast([P, 2]), ALU.pow).then_inc(S["a_rs"], 1)

            def ffn(q, N0, xb):
                power(N0)

            def stack(p, N0, xb):
                power(N0)
                with gp.Fori(0, DEPTH) as l:
                    G, L = tile0(p, l), layer0(p, l)
                    gp.wait_ge(S["qs_ld"], L * 32 + 32)
                    gp.wait_ge(S["rot_done"], G * 8)
                    gp.wait_ge(S["cst_ld"], 48)
                    for k in range(4):
                        s = qks[:, k // 2, :].rearrange("p (w t d) -> p w t d", w=1, t=2)
                        if k % 2:
                            s = s[:, :, ::-1, :]
                        gp.tensor_tensor(rot[:, k, :, :].rearrange("p w (t d) -> p w t d", t=2),
                                         tabs[:, k, :, :].rearrange("p w (t d) -> p w t d", t=2),
                                         s.to_broadcast([P, WINDOWS, 2, DH // 2]), ALU.mult).then_inc(S["tab_done"], 1)
                    with gp.Fori(0, WINDOWS) as v:
                        for g in range(2):
                            project(G + v * 2 + g, g)
                    power(ln_no(p, l))

            run(stack, attention, ffn)

        @block.tensor
        def _(pe):
            for n, k in (("qkv_done", 6), ("qkt_done", 4), ("sc_done", 1), ("pt_done", 2), ("pv_done", 1), ("ot_done", 2)):
                pe.sem_inc(S[n], k * CREDIT)
            for n, k in (("y_done", 1), ("aqk_done", 4), ("av_done", 1), ("as_done", ROWS), ("at_done", UNITS[0]), ("apv_done", 1),
                         ("a_ss", 1), ("a_bc", 1), ("a_y", 1)):
                pe.sem_inc(S[n], k)
            pe.wait_ge(S["cst_ld"], 48)
            pe.wait_ge(S["cst_done"], 5)
            pe.wait_ge(S["mask_done"], 1)
            pe.wait_ge(S["x_ld"], 16 * SEQS)

            def to_features():
                for b in range(BATCHES):
                    for t in range(4):
                        last = pe.transpose(LNB[b][:, P * t:P * t + P], nat[:, 4 * b + t, :], ident[:, :])
                    last.then_inc(S["xt_done"], 1)

            def norm(N, src, ready):
                for b in range(BATCHES):
                    ready(b)
                    pe.matmul(LNB[b][:, :], mean_w[:, :], src(b), start=True, stop=True).then_inc(S["ln_mean"], 1)
                for b in range(BATCHES):
                    pe.wait_ge(S["ln_sqd"], N * BATCHES + b + 1)
                    for t in range(4):
                        last = pe.matmul(SB[0][:, 4 * b + t:4 * b + t + 1], sqd[:, b, P * t:P * t + P], mean_w[:, 0:1],
                                         start=(b == 0 and t == 0), stop=True, skip_group_check=True)
                    last.then_inc(S["ln_ss"], 1)
                for b in range(BATCHES):
                    pe.wait_ge(S["ln_dg"], N * TILES + 4 * b + 4)
                    pe.wait_ge(S["ln_cen"], N * BATCHES + b + 1)
                    pe.matmul(LNB[b][:, :], ones[:, :], sqd[:, b, :], start=True, stop=True).then_inc(S["ln_bc"], 1)

            def qkv(G, g, chunks):
                for c in chunks:
                    if c < 2:
                        pe.wait_ge(S["v_done"], G * 2 - 2 + c + 1)
                    else:
                        pe.wait_ge(S["rot_done"], G * 8 + 2 * (c - 2) + 2)
                    pe.matmul(QB[c % 2][:, :], xst[:, g, :], wqkv[:, BATCH * c:BATCH * c + BATCH],
                              start=True, stop=True).then_inc(S["qkv_done"], 1)

            def p_transposes(G, g):
                pe.wait_ge(S["exp_done"], G + 1)
                for b in range(2):
                    if b == 0:
                        pe.wait_ge(S["ot_ev"], G * 2)
                    for m in range(4):
                        mm = 4 * b + m
                        last = pe.transpose(TB[b][:, P * m:P * m + P],
                                            pr[:, g, mm, :, :].rearrange("p a b -> p (a b)"), ident[:, :])
                    last.then_inc(S["pt_done"], 1)

            def o_transposes(G):
                pe.wait_ge(S["on_done"], G * 2 + 2)
                for b in range(2):
                    for m in range(4):
                        mm = 4 * b + m
                        last = pe.transpose(TB[b][:, P * m:P * m + P],
                                            osb[:, mm, :, :].rearrange("p a b -> p (a b)"), ident[:, :])
                    last.then_inc(S["ot_done"], 1)

            def output(G):
                pe.wait_ge(S["ot_ev"], G * 2 + 2)
                for m in range(PAIRS):
                    last = pe.matmul(OB[0][:, 0:2 * P], wo[:, m, :], oT[:, m, :, :].rearrange("p g c -> p (g c)"),
                                     start=(m == 0), stop=(m == PAIRS - 1))
                last.then_inc(S["y_done"], 1)

            def qk_transposes(G, g):
                for b in range(4):
                    pe.wait_ge(S["qk_done"], G * 2 + 1 + b // 2)
                    if b >= 2:
                        pe.wait_ge(S["qkt_ev"], G * 4 + b - 1)
                    for m in range(4):
                        last = pe.transpose(TB[b % 2][:, P * m:P * m + P], t1[:, g, b, P * m:P * m + P], ident[:, :])
                    last.then_inc(S["qkt_done"], 1)

            def scores(G, g, mask):
                pe.wait_ge(S["sub_done"], G * 2)
                for h2 in range(2):
                    if h2:
                        pe.wait_ge(S["qkt_ev"], G * 4 + 4)
                    pe.matmul(SB[h2][:, :].rearrange("p (m k) -> p m k", k=DH), ident_bf[:, :],
                              mask_bf[:, mask:mask + 1, :].to_broadcast([P, PAIRS, DH]),
                              start=True, stop=True)
                for m in range(PAIRS):
                    for h2 in range(2):
                        for j in range(QUADS):
                            last = pe.matmul(SB[h2][32 * j:32 * j + 32, DH * m:DH * m + DH],
                                             qT[64 * h2:64 * h2 + 64, m, 32 * j:32 * j + 32],
                                             kT[g][64 * h2:64 * h2 + 64, m, j, :, :].rearrange("p s k -> p (s k)"),
                                             start=False, stop=True, skip_group_check=True)
                last.then_inc(S["sc_done"], 1)

            def attend(G0, n, base, first, run=None):
                a, b, c = run or (True, True, True)
                g = n % 2
                G = base + n
                if a:
                    if n == 0 and first:
                        pe.wait_ge(S["wqkv_ld"], G0[1] * 16 + 16)
                    pe.wait_ge(S["xst_done"], G * 3 + 3)
                    qkv(G, g, range(0, 3))
                if c:
                    p_transposes(G - 2, g)
                if a:
                    qkv(G, g, range(3, 6))
                if c:
                    pe.wait_ge(S["y2_done"], G0[2] + (n - 2 - g) // 2 + 1)
                    pe.wait_ge(S["pt_ev"], (G - 2) * 2 + 2)
                    pe.wait_ge(S[f"vj_ld{g}"], (G0[2] + ((n - 2) // 2 + 2)) * 128)
                    pe.wait_ge(S["on_done"], (G - 2) * 2)
                    for h2 in range(2):
                        pe.matmul(OB[h2][:, 0:DH], zero_bf[:, :], zero_bf[:, 0:DH], start=True, stop=True)
                    for m in range(PAIRS):
                        for h2 in range(2):
                            for j in range(QUADS):
                                last = pe.matmul(OB[h2][32 * j:32 * j + 32, DH * m:DH * m + DH],
                                                 pT[64 * h2:64 * h2 + 64, m, 32 * j:32 * j + 32],
                                                 vj[g][64 * h2:64 * h2 + 64, j, DH * m:DH * m + DH],
                                                 start=False, stop=True, skip_group_check=True)
                    last.then_inc(S["pv_done"], 1)
                if b:
                    qk_transposes(G - 1, 1 - g)
                    w_ = (n - 1) // 2
                    mask = 0 if (first and n - 1 < 2) else (1 if w_ % 2 else 2)
                    scores(G - 1, 1 - g, mask)
                if c:
                    o_transposes(G - 2)
                    if g == 1:
                        if n == 3 and first:
                            pe.wait_ge(S["wo_ld"], G0[1] * 16 + 16)
                        output(G - 2)

            def feed_forward(p, L, N):
                pe.wait_ge(S["ff_ld"], (L + 1) * 160)
                K = L * (BATCHES * 3) + CREDIT

                def up(b):
                    pe.wait_ge(S["ln_out"], L * BATCHES + b + 1)
                    for k in range(6):
                        i, c = 6 * b + k, k // 2
                        pe.wait_ge(S["hm_done" if k % 2 else "gelu_done"], K + (i // 2 - 2 + 1))
                        col = P * c + (0 if k % 2 else FF)
                        pe.matmul(FFB[i % 4][0:FFC[c], :], w1[:, col:col + FFC[c]], cen[:, b, :],
                                  start=True, stop=True).then_inc(S["h_done"], 1)

                def down(b):
                    pe.wait_ge(S["hm_done"], K + 3 * b + 3)
                    pe.wait_ge(S["ln_out"], (L + 1) * BATCHES)
                    if b >= 2:
                        pe.wait_ge(S["y_ready"], (L + p + 1) * BATCHES + b - 1)
                    for c in range(3):
                        last = pe.matmul(TB[b % 2][:, :], w2[0:FFC[c], c, :], hh[0:FFC[c], b % 2, c, :],
                                         start=(c == 0), stop=(c == 2))
                    last.then_inc(S["f_done"], 1)

                up(0)
                for b in range(1, BATCHES):
                    up(b)
                    down(b - 1)
                down(BATCHES - 1)

            def x_ready(xb):
                if xb == 0:
                    return lambda b: pe.wait_ge(S["xt_ev"], b + 1)
                return lambda b: pe.wait_ge(S["x_done"], xb)

            def ffn(q, N0, xb):
                if q == 0:
                    pe.wait_ge(S["wi_cv"], 3)
                    for m in range(3):
                        for c in range(3):
                            last = pe.transpose(FFB[m][:, P * c:P * c + P], wqkv[:, HID * m + P * c:HID * m + P * c + P], ident[:, :])
                        last.then_inc(S["wi_done"], 1)
                    pe.wait_ge(S["wi_ev"], 3)
                norm(N0, lambda b: batch(b, X), x_ready(xb))
                L = PASSES * DEPTH + q
                K = L * (BATCHES * 3) + CREDIT

                def up(b):
                    pe.wait_ge(S["n_out"], (1 + 2 * q) * BATCHES + b + 1)
                    for k in range(6):
                        i, c = 6 * b + k, k // 2
                        pe.wait_ge(S["hm_done" if k % 2 else "gelu_done"], K + (i // 2 - 2 + 1))
                        pe.matmul(FFB[i % 4][:, :], wi[:, k % 2, P * c:P * c + P], cen[:, b, :], start=True, stop=True).then_inc(S["h_done"], 1)

                def down(b):
                    pe.wait_ge(S["hm_done"], K + 3 * b + 3)
                    pe.wait_ge(S["n_out"], (1 + 2 * q) * BATCHES + BATCHES)
                    if b >= 2:
                        pe.wait_ge(S["x_done"], xb + b - 1)
                    for c in range(3):
                        last = pe.matmul(TB[b % 2][:, :], wi[:, 2, P * c:P * c + P], hh[:, b % 2, c, :], start=(c == 0), stop=(c == 2))
                    last.then_inc(S["f_done"], 1)

                up(0)
                for b in range(1, BATCHES):
                    up(b)
                    down(b - 1)
                down(BATCHES - 1)

            def attention(kind, N0, xb):
                if kind == DIFF:
                    pe.wait_ge(S["raw_ld"], 16 * 11)
                    for k in range(4):
                        last = pe.transpose(SB[0][:, P * k:P * k + P], wraw[:, k, :], ident[:, :])
                    last.then_inc(S["wt_done"], 1)
                    pe.wait_ge(S["wt_ev"], 2)
                pe.wait_ge(S["wdup_done"], 4 * kind + 4)
                norm(N0, lambda b: batch(b, X), x_ready(xb))
                wvv = wv if kind == DIFF else wraw[:, 5, :]
                woo = wot if kind == DIFF else wraw[:, 6, :]
                dh = DHS[kind]
                per = 32 // dh
                units = UNITS[kind]
                with pe.Fori(0, SEQS) as s:
                    Q = s + (SEQS * kind + 1)
                    U = s * units + (SEQS * UNITS[0] * kind + UNITS[0])
                    pe.wait_ge(S["ys_done"], Q + 1)
                    pe.wait_ge(S["ae_done"], Q * ROWS)
                    for k, wp in enumerate((wqp, wkp)):
                        for h in range(2):
                            for r_ in range(2):
                                c = 4 * (2 * h + r_)
                                last = pe.matmul(LNB[2 * k + h][:, TOKENS * r_:TOKENS * r_ + TOKENS],
                                                 wp[:, c:c + 4, :].rearrange("p n d -> p (n d)"), ys, start=True, stop=True, skip_group_check=True)
                            last.then_inc(S["aqk_done"], 1)
                    pe.wait_ge(S["at_ev"], U)
                    for t in range(2):
                        last = pe.matmul(SB[0][:, P * t:P * t + P], ys[:, P * t:P * t + P], wvv, start=True, stop=True, skip_group_check=True)
                    last.then_inc(S["av_done"], 1)
                    pe.wait_ge(S["aqk_ev"], Q * 4 + 4)
                    for i in range(ROWS + 5):
                        if i < ROWS:
                            a, r_ = i % 4, i // 4
                            if i >= 4:
                                pe.wait_ge(S["ae_done"], Q * ROWS + i - 3)
                            for t in range(2):
                                last = pe.matmul(LNB[a][:, TOKENS * t:TOKENS * t + TOKENS],
                                                 qp[32 * a:32 * a + 8, r_, P * t:P * t + P], kp[32 * a:32 * a + 8, r_, :],
                                                 start=True, stop=True, skip_group_check=True)
                            last.then_inc(S["as_done"], 1)
                        u = unit_ready(kind, i - 3)
                        if u is not None:
                            pe.wait_ge(S["an_done"], U + u + 1)
                            if u < 2:
                                pe.wait_ge(S["av_ev"], Q + 1)
                            else:
                                pe.wait_ge(S["at_ev"], U + u - 1)
                            for kb in range(2):
                                for t in range(2):
                                    last = pe.transpose(SB[u % 2][:, TOKENS * kb + P * t:TOKENS * kb + P * t + P],
                                                        pn_ring[:, u % 2, t, P * kb:P * kb + P], ident[:, :])
                            last.then_inc(S["at_done"], 1)
                        u = unit_ready(kind, i - 4)
                        if u is not None:
                            if u == 0:
                                pe.wait_ge(S["x_done"], xb + s)
                            pe.wait_ge(S["at_ev"], U + u + 1)
                            c = 32 * (u // per)
                            for kb in range(2):
                                last = pe.matmul(OB[0][c:c + 32, 0:TOKENS], vpad[:, kb, u, :], pnT[:, u % 2, kb, :],
                                                 start=(u % per == 0 and kb == 0), stop=(u % per == per - 1 and kb == 1))
                    last.then_inc(S["apv_done"], 1)
                    if kind == DIFF:
                        pe.wait_ge(S["a_sq"], Q + 1)
                        for t in range(2):
                            last = pe.matmul(OB[1][:, t:t + 1], osq[:, P * t:P * t + P], mean_w[:, 0:1], start=(t == 0), stop=True, skip_group_check=True)
                        last.then_inc(S["a_ss"], 1)
                        pe.wait_ge(S["a_dg"], Q * 2 + 2)
                        pe.matmul(OB[1][:, 0:TOKENS], ones[:, :], odg, start=True, stop=True).then_inc(S["a_bc"], 1)
                        pe.wait_ge(S["a_on2"], Q + 1)
                        pe.matmul(OB[0][:, 0:TOKENS], woo, on2, start=True, stop=True).then_inc(S["a_y"], 1)
                    else:
                        pe.wait_ge(S["a_on"], Q + 1)
                        pe.matmul(OB[0][:, 0:TOKENS], woo, on, start=True, stop=True).then_inc(S["a_y"], 1)

            def stack(p, N0, xb):
                norm(N0, lambda b: batch(b, X), x_ready(xb))
                with pe.Fori(0, DEPTH) as l:
                    G, L, N = tile0(p, l), layer0(p, l), ln_no(p, l)
                    G0 = (G, L, L * WINDOWS)
                    for n in range(4):
                        attend(G0, n, G, True, (True, n >= 1, n >= 2))
                    with pe.Fori(1, WINDOWS // 2) as v:
                        Gv = (G, L, L * WINDOWS + v * 2)
                        for n in range(4):
                            attend(Gv, n, G + v * 4, False)
                    Ge = (G, L, L * WINDOWS + WINDOWS)
                    attend(Ge, 0, G + TILES, False, (False, True, True))
                    attend(Ge, 1, G + TILES, False, (False, False, True))

                    def staged(b):
                        pe.wait_ge(S["xs_done"], L * 12 + 3 * b + 3)
                    norm(N, lambda b: xs[:, b, :], staged)
                    feed_forward(p, L, N)

            to_features()
            run(stack, attention, ffn)

            def to_tokens():
                for b in range(BATCHES):
                    pe.wait_ge(S["x_done"], X_TOTAL)
                    for t in range(4):
                        last = pe.transpose(LNB[b][:, P * t:P * t + P], batch(b, X)[:, P * t:P * t + P], ident[:, :])
                    last.then_inc(S["on_T"], 1)
            to_tokens()

        @block.scalar
        def _(act):
            act.sem_inc(S["sq_done"], 4 * CREDIT)
            act.sem_inc(S["xst_done"], 3 * CREDIT)
            act.sem_inc(S["v_done"], 2 * CREDIT)
            act.sem_inc(S["qkt_ev"], 4 * CREDIT)
            act.sem_inc(S["exp_done"], CREDIT)
            act.sem_inc(S["pt_ev"], 2 * CREDIT)
            act.sem_inc(S["ot_ev"], 2 * CREDIT)
            act.sem_inc(S["gelu_done"], CREDIT)
            for n, k in (("aqk_ev", 4), ("ae_done", ROWS), ("at_ev", UNITS[0]), ("a_sq", 1)):
                act.sem_inc(S[n], k)
            for b in range(BATCHES):
                act.wait_ge(S["xt_done"], b + 1)
                act.activation(batch(b, X), LNB[b][:, :], ACT.Copy).then_inc(S["xt_ev"], 1)

            def squares(N):
                for b in range(BATCHES):
                    act.wait_ge(S["ln_cen"], N * BATCHES + b + 1)
                    act.activation(sqd[:, b, :], cen[:, b, :], ACT.Square).then_inc(S["ln_sqd"], 1)

            def stage(G, wx, g):
                act.wait_ge(S["qkv_done"], (G - 1) * 6)
                yt = Y[:, g, bass.ds(wx, 2), :].rearrange("p a (j i) -> p a j i", i=WIN)
                xt = xst[:, g, :].rearrange("p (a j i) -> p a j i", a=1, i=WIN)
                act.activation(xt[0:64], yt[0:64, 1:2], ACT.Copy).then_inc(S["xst_done"], 1)
                act.activation(xt[64:P, :, :, 1:WIN], yt[64:P, 1:2, :, 0:WIN - 1], ACT.Copy).then_inc(S["xst_done"], 1)
                act.activation(xt[64:P, :, :, 0:1], yt[64:P, 0:1, :, WIN - 1:WIN], ACT.Copy).then_inc(S["xst_done"], 1)

            def softmax_exp(G, g):
                act.wait_ge(S["sub_done"], G * 2 + 2)
                t = pr[:, g, :, :, :].rearrange("p m a k -> p (m a k)")
                act.activation(t, t, ACT.Exp, scale=QK_SCALE).then_inc(S["exp_done"], 1)

            def attend(base, n, w0, run=(True, True, True)):
                a, b, c = run
                g, G = n % 2, base + n
                if a and n == 0:
                    stage(G, w0, 0)
                if a and n < 3:
                    stage(G + 1, w0 + (n + 1) // 2, 1 - g)
                if c:
                    softmax_exp(G - 2, g)

                def square(c4):
                    act.wait_ge(S["qkv_done"], G * 6 + c4 + 1)
                    act.wait_ge(S["ss_done"], G * 4 + c4 - 1)
                    act.activation(sq[:, c4 % 2, :], QB[c4 % 2][:, :], ACT.Square).then_inc(S["sq_done"], 1)

                if a:
                    for c4 in range(3):
                        square(c4)
                if c:
                    act.wait_ge(S["pv_done"], G - 2)
                    for k in range(2):
                        act.wait_ge(S["pt_done"], (G - 2) * 2 + k + 1)
                        act.activation(pT[:, 4 * k:4 * k + 4, :].rearrange("p m q -> p (m q)"), TB[k][:, :], ACT.Copy).then_inc(S["pt_ev"], 1)
                if a:
                    square(3)
                    act.wait_ge(S[f"vj_ld{g}"], (ynow[0] + 2) * 128)
                    act.wait_ge(S["pv_done"], G - 1)
                    for k in range(2):
                        act.wait_ge(S["qkv_done"], G * 6 + 5 + k)
                        act.activation(vs[:, g, :, 256 * k:256 * k + 256].rearrange("p a (m d) -> p m a d", d=DH),
                                       QB[k][:, :].rearrange("p (m a d) -> p m a d", a=2, d=DH), ACT.Copy).then_inc(S["v_done"], 1)
                if b:
                    slot = ((n - 1) // 2) % 2
                    act.wait_ge(S["sc_done"], G - 1)
                    for k in range(4):
                        act.wait_ge(S["qkt_done"], (G - 1) * 4 + k + 1)
                        if k < 2:
                            dst = qT[:, 4 * k:4 * k + 4, :]
                            src = TB[k % 2][:, :].rearrange("p (m q) -> p m q", m=4)
                        else:
                            dst = kT[1 - g][:, 4 * k - 8:4 * k - 4, :, slot, :]
                            src = TB[k % 2][:, :].rearrange("p (m j q) -> p m j q", m=4, q=WIN)
                        act.activation(dst, src, ACT.Copy).then_inc(S["qkt_ev"], 1)
                if c:
                    act.wait_ge(S["y_done"], ynow[0] + 1)
                    for k in range(2):
                        act.wait_ge(S["ot_done"], (G - 2) * 2 + k + 1)
                        act.activation(oT[:, 4 * k:4 * k + 4, g, :], TB[k][:, :].rearrange("p (m q) -> p m q", m=4), ACT.Copy).then_inc(S["ot_ev"], 1)

            ynow = [None]

            def ffn(q, N0, xb):
                squares(N0)
                L = PASSES * DEPTH + q
                K = L * (BATCHES * 3) + CREDIT
                for i in range(3 * BATCHES):
                    act.wait_ge(S["h_done"], L * (BATCHES * 6) + 2 * i + 1)
                    act.wait_ge(S["hm_done"], K + (i - 2 + 1))
                    act.activation(gl[:, i % 2, :], FFB[(2 * i) % 4][:, :], ACT.Silu).then_inc(S["gelu_done"], 1)

            def attention(kind, N0, xb):
                squares(N0)
                units = UNITS[kind]
                with act.Fori(0, SEQS) as s:
                    Q = s + (SEQS * kind + 1)
                    U = s * units + (SEQS * UNITS[0] * kind + UNITS[0])
                    act.wait_ge(S["as_done"], Q * ROWS)
                    for k in range(4):
                        act.wait_ge(S["aqk_done"], Q * 4 + k + 1)
                        dst = (qp if k < 2 else kp)[:, 2 * (k % 2):2 * (k % 2) + 2, :]
                        act.activation(dst, LNB[k][:, :].rearrange("p (r n) -> p r n", n=TOKENS), ACT.Copy,
                                       scale=QS[kind] if k < 2 else 1.0).then_inc(S["aqk_ev"], 1)
                    for i in range(ROWS + 3):
                        if i < ROWS:
                            act.wait_ge(S["am_done"], Q * ROWS + i + 1)
                            if i < 4:
                                act.wait_ge(S["an_done"], U)
                            elif kind != DIFF:
                                act.wait_ge(S["an_done"], U + i - 3)
                            else:
                                act.wait_ge(S["an_done" if i % 2 else "an_half"], U + (i - 4) // 2 + 1)
                            for t in range(2):
                                last = act.activation(pe_ring[:, i % 4, t, :], LNB[i % 4][:, TOKENS * t:TOKENS * t + TOKENS], ACT.Exp,
                                                      bias=nm[:, i, t:t + 1], accum_out=dsum[:, i, t:t + 1])
                            last.then_inc(S["ae_done"], 1)
                        u = unit_ready(kind, i - 3)
                        if u is not None:
                            act.wait_ge(S["at_done"], U + u + 1)
                            act.activation(pnT[:, u % 2, :, :], SB[u % 2][:, :].rearrange("p (t k) -> p t k", t=2), ACT.Copy).then_inc(S["at_ev"], 1)
                    if kind == DIFF:
                        act.wait_ge(S["a_on"], Q + 1)
                        act.activation(osq, OB[0][:, 0:TOKENS], ACT.Square).then_inc(S["a_sq"], 1)

            def stack(p, N0, xb):
                squares(N0)
                with act.Fori(0, DEPTH) as l:
                    G, L, N = tile0(p, l), layer0(p, l), ln_no(p, l)
                    act.wait_ge(S["y_ready"], (L + p + 1) * BATCHES)
                    for n in range(4):
                        ynow[0] = L * WINDOWS + (n - 2) // 2
                        attend(G, n, 0, (True, n >= 1, n >= 2))
                    with act.Fori(1, WINDOWS // 2) as v:
                        for n in range(4):
                            ynow[0] = L * WINDOWS + v * 2 + (n - 2) // 2
                            attend(G + v * 4, n, v * 2)
                    for n in range(2):
                        ynow[0] = L * WINDOWS + WINDOWS + (n - 2) // 2
                        attend(G + TILES, n, 0, (False, n == 0, True))
                    squares(N)
                    K = L * (BATCHES * 3) + CREDIT
                    act.wait_ge(S["ff_ld"], (L + 1) * 160)
                    for i in range(3 * BATCHES):
                        b, c = divmod(i, 3)
                        act.wait_ge(S["h_done"], L * (BATCHES * 6) + 2 * i + 1)
                        act.wait_ge(S["hm_done"], K + (i - 2 + 1))
                        r = slice(0, FFC[c])
                        act.activation(gl[r, i % 2, :], FFB[(2 * i) % 4][r, :], ACT.Gelu, bias=b1[r, 3 + c:4 + c]).then_inc(S["gelu_done"], 1)

            run(stack, attention, ffn)
            for b in range(BATCHES):
                act.wait_ge(S["on_T"], b + 1)
                act.activation(nat[:, 4 * b:4 * b + 4, :].rearrange("p t e -> p (t e)"), LNB[b][:, :], ACT.Copy).then_inc(S["on_ev"], 1)

        @block.vector
        def _(dve):
            dve.sem_inc(S["rot_done"], 8 * CREDIT)
            dve.sem_inc(S["ss_done"], 4 * CREDIT)
            dve.sem_inc(S["mx_done"], 2 * CREDIT)
            dve.sem_inc(S["nrm_max"], CREDIT)
            dve.sem_inc(S["sub_done"], 2 * CREDIT)
            dve.sem_inc(S["sum_done"], CREDIT)
            dve.sem_inc(S["rs_done"], CREDIT)
            dve.sem_inc(S["on_done"], 2 * CREDIT)
            dve.sem_inc(S["hm_done"], CREDIT)
            for n, k in (("y2_done", 1), ("ys_done", 1), ("av_ev", 1), ("am_done", ROWS), ("ac_done", ROWS), ("ad_done", UNITS[0]),
                         ("an_half", UNITS[0]), ("an_done", UNITS[0]), ("a_on", 1), ("a_ve", 1), ("a_dg", 2), ("a_on2", 1), ("a_yt", 1)):
                dve.sem_inc(S[n], k)
            dve.wait_ge(S["cst_ld"], 48)
            dve.tensor_copy(mask_bf[:, :, :].rearrange("p a b -> p (a b)"), xs[:, 3, 0:3 * DH]).then_inc(S["mask_done"], 1)
            dve.tensor_copy(ident_bf[:, :], ident[:, :]).then_inc(S["cst_done"], 1)
            dve.memset(mean_w[:, :], 1.0 / P).then_inc(S["cst_done"], 1)
            dve.memset(mhalf[:, :], -0.5).then_inc(S["cst_done"], 1)
            dve.memset(zero_bf[:, :], 0.0)
            dve.memset(kT[0][:, :, :, 1, :], 0.0)
            dve.memset(kT[1][:, :, :, 1, :], 0.0)
            dve.memset(vj[0][:, :, :], 0.0)
            dve.memset(vj[1][:, :, :], 0.0)
            dve.memset(Y[:, :, 0, :], 0.0)
            dve.memset(Y2[:, :, 0, :], 0.0).then_inc(S["cst_done"], 1)

            def norm(N, src, ready, dst, affine, done):
                for b in range(BATCHES):
                    dve.wait_ge(S["ln_mean"], N * BATCHES + b + 1)
                    ready(b)
                    dve.tensor_tensor(cen[:, b, :], src(b), LNB[b][:, :], ALU.subtract).then_inc(S["ln_cen"], 1)
                dve.wait_ge(S["ln_ss"], (N + 1) * BATCHES)
                dve.tensor_scalar(ve[:, :], SB[0][:, 0:TILES], 1e-5, None, ALU.add).then_inc(S["ln_ve"], 1)
                dve.wait_ge(S["ln_rs"], N + 1)
                for t in range(TILES):
                    b, k = divmod(t, 4)
                    dve.tensor_scalar(sqd[:, b, P * k:P * k + P], ident[:, :], rstd[:, t:t + 1], None, ALU.mult).then_inc(S["ln_dg"], 1)
                for b in range(BATCHES):
                    dve.wait_ge(S["ln_bc"], N * BATCHES + b + 1)
                    o = dve.tensor_tensor(dst(b), cen[:, b, :], LNB[b][:, :], ALU.mult)
                    if not affine:
                        o.then_inc(S[done], 1)
                    else:
                        o.then_inc(S["ln_xn"], 1)
                if affine:
                    for b in range(BATCHES):
                        dve.wait_ge(S["ln_xn"], affine(b))
                        dve.tensor_scalar(dst(b), dst(b), lnp[:, 0:1], lnp[:, 1:2], ALU.mult, ALU.add).then_inc(S["ln_out"], 1)

            def attend(base, n, L, mrun, ybase, run=(True, True)):
                a, c = run
                g, G = n % 2, base + n
                if c:
                    Gc = G - 2
                    dve.wait_ge(S["sc_done"], Gc + 1)
                    dve.wait_ge(S["pt_done"], (Gc - 1) * 2)
                    for h2 in range(2):
                        s = SB[h2][:, :].rearrange("p (m k) -> p m k", k=DH)
                        dve.tensor_reduce(mx[:, g, h2, :], s, AX.X, ALU.max).then_inc(S["mx_done"], 1)
                    for h2 in range(2):
                        s = SB[h2][:, :].rearrange("p (m k) -> p m k", k=DH)
                        dve.wait_ge(S["mx_done"], Gc * 2 + h2 + 1)
                        dve.tensor_tensor(pr[:, g, :, h2, :], s, mx[:, g, h2, :].unsqueeze(2).to_broadcast([P, PAIRS, DH]),
                                          ALU.subtract).then_inc(S["sub_done"], 1)
                if a:
                    w_ = mrun
                    dve.wait_ge(S["qkt_done"], (G - 1) * 4)
                    for c4 in range(4):
                        k = 2 * (c4 // 2)
                        dve.wait_ge(S["sq_done"], G * 4 + c4 + 1)
                        dve.wait_ge(S["add_done"], G * 4 + c4 - 1)
                        q = QB[c4 % 2][:, :].rearrange("p (h t d) -> p h t d", t=2, d=DH // 2)
                        cos = rot[:, k, bass.ds(w_, 1), :]
                        sin = rot[:, k + 1, bass.ds(w_, 1), :]
                        dve.tensor_tensor(t1[:, g, c4, :].rearrange("p (h d) -> p h d", d=DH), QB[c4 % 2][:, :].rearrange("p (h d) -> p h d", d=DH),
                                          cos.to_broadcast([P, 8, DH]), ALU.mult).then_inc(S["rot_done"], 1)
                        dve.tensor_tensor(t2[:, c4 % 2, :].rearrange("p (h t d) -> p h t d", t=2, d=DH // 2), q[:, :, ::-1, :],
                                          sin.rearrange("p w (t d) -> p w t d", t=2).to_broadcast([P, 8, 2, DH // 2]),
                                          ALU.mult).then_inc(S["rot_done"], 1)
                        dve.tensor_reduce(ss[:, g, 8 * c4:8 * c4 + 8], sq[:, c4 % 2, :].rearrange("p (h d) -> p h d", d=DH),
                                          AX.X, ALU.add).then_inc(S["ss_done"], 1)
                    dve.wait_ge(S["ss_done"], G * 4 + 4)
                    dve.tensor_scalar(rn[:, g, 0, :], ss[:, g, :], 1e-24, None, ALU.max).then_inc(S["nrm_max"], 1)
                if c:
                    dve.wait_ge(S["exp_done"], Gc + 1)
                    dve.tensor_reduce(sm[:, g, :].rearrange("p (m a) -> p m a", a=2), pr[:, g, :, :, :], AX.X, ALU.add).then_inc(S["sum_done"], 1)
                    dve.wait_ge(S["sum_done"], Gc + 1)
                    dve.reciprocal(rs[:, g, :], sm[:, g, :]).then_inc(S["rs_done"], 1)
                    dve.wait_ge(S["rs_done"], Gc + 1)
                    dve.wait_ge(S["pv_done"], Gc + 1)
                    dve.wait_ge(S["ot_done"], Gc * 2)
                    for h2 in range(2):
                        r = rs[:, g, :].rearrange("p (m a) -> p m a", a=2)[:, :, h2:h2 + 1].to_broadcast([P, PAIRS, DH])
                        dve.tensor_tensor(osb[:, :, h2, :], OB[h2][:, :].rearrange("p (m d) -> p m d", d=DH), r, ALU.mult).then_inc(S["on_done"], 1)
                    if g == 1:
                        wx, ycount = ybase
                        dve.wait_ge(S["y_done"], ycount + 2)
                        dve.tensor_tensor(Y2[:, :, bass.ds(wx + 1, 1), :], OB[0][:, 0:2 * P].rearrange("p (g w c) -> p g w c", g=2, w=1),
                                          Y[:, :, bass.ds(wx + 1, 1), :], ALU.add).then_inc(S["y2_done"], 1)

            def x_ready(xb):
                if xb == 0:
                    return lambda b: dve.wait_ge(S["xt_ev"], b + 1)
                return lambda b: dve.wait_ge(S["x_done"], xb)

            def ffn(q, N0, xb):
                if q == 0:
                    dve.wait_ge(S["int_ld"], 48)
                    for m in range(3):
                        dve.tensor_scalar(wqkv[:, HID * m:HID * m + HID], iraw[:, m, :], float(np.float32(1.0 / 127.0)), None, ALU.mult).then_inc(S["wi_cv"], 1)
                    for m in range(3):
                        dve.wait_ge(S["wi_done"], m + 1)
                        dve.tensor_copy(wi[:, m, :], FFB[m][:, 0:HID]).then_inc(S["wi_ev"], 1)
                norm(N0, lambda b: batch(b, X), x_ready(xb), lambda b: cen[:, b, :], None, "n_out")
                L = PASSES * DEPTH + q
                K = L * (BATCHES * 3) + CREDIT

                def join(b):
                    dve.wait_ge(S["f_done"], L * BATCHES + b + 1)
                    dve.scalar_tensor_tensor(batch(b, X), TB[b % 2][:, :], 0.5, batch(b, X), ALU.mult, ALU.add).then_inc(S["x_done"], 1)

                for i in range(3 * BATCHES):
                    b, c = divmod(i, 3)
                    dve.wait_ge(S["h_done"], L * (BATCHES * 6) + 2 * i + 2)
                    dve.wait_ge(S["gelu_done"], K + i + 1)
                    if c == 0 and b >= 2:
                        dve.wait_ge(S["f_done"], L * BATCHES + b - 1)
                    dve.tensor_tensor(hh[:, b % 2, c, :], FFB[(2 * i + 1) % 4][:, :], gl[:, i % 2, :], ALU.mult).then_inc(S["hm_done"], 1)
                    if c == 2 and b >= 1:
                        join(b - 1)
                join(BATCHES - 1)

            def attention(kind, N0, xb):
                dh = DHS[kind]
                units = UNITS[kind]
                if kind == DIFF:
                    dve.wait_ge(S["raw_ld"], 16 * 11)
                    dve.tensor_scalar(vec[:, 1:2], vec[:, 0:1], -1.0, None, ALU.mult).then_inc(S["vec_done"], 1)
                    dve.tensor_scalar(vec[:, 2:3], vec[:, 0:1], -1.0, 1.0, ALU.mult, ALU.add).then_inc(S["vec_done"], 1)
                    dve.wait_ge(S["vec_done"], 2)
                    dve.tensor_tensor(vec[:, 5:6], vec[:, 4:5], vec[:, 2:3], ALU.mult).then_inc(S["vec_done"], 1)
                    dve.wait_ge(S["vec_done"], 3)
                    dve.wait_ge(S["wt_done"], 1)
                    for k, dst in ((2, wv), (3, wot)):
                        dve.tensor_copy(dst, SB[0][:, P * k:P * k + P]).then_inc(S["wt_ev"], 1)
                dve.memset(rotf[:, 0:1024], 0.0).then_inc(S["wdup_done"], 1)
                dve.memset(vpad[:, :, :, :], 0.0).then_inc(S["wdup_done"], 1)
                dve.wait_ge(S["wdup_done"], 4 * kind + 2)
                for k, dst in ((0, wqp), (1, wkp)):
                    src = SB[0][:, P * k:P * k + P] if kind == DIFF else wraw[:, 4 + k, :]
                    dve.tensor_copy(dst[:, :, 0:8], src.rearrange("p (n d) -> p n d", d=8)).then_inc(S["wdup_done"], 1)
                norm(N0, lambda b: batch(b, X), x_ready(xb), lambda b: cen[:, b, :], None, "n_out")
                norms = (1 if kind == DIFF else 3)
                dve.wait_ge(S["n_out"], norms * BATCHES)
                ycen = cen[:, :, :].rearrange("p (g h) (w c) -> p g (h w) c", g=GROUPS, w=4)
                per = 32 // dh
                with dve.Fori(0, GROUPS) as gq, dve.Fori(0, QUADS) as jq:
                    s = gq * QUADS + jq
                    Q = s + (SEQS * kind + 1)
                    U = s * units + (SEQS * UNITS[0] * kind + UNITS[0])
                    dve.wait_ge(S["av_done"], Q)
                    dve.tensor_copy(ys.rearrange("p (w i) -> p w i", i=WIN),
                                    ycen[:, bass.ds(gq, 1), :, bass.ds(jq * WIN, WIN)].rearrange("p g w i -> p (g w) i")).then_inc(S["ys_done"], 1)
                    dve.wait_ge(S["av_done"], Q + 1)
                    dve.wait_ge(S["apv_done"], Q)
                    for h in range(per):
                        src = SB[0][:, 0:TOKENS].rearrange("p (t c h d) -> p t c h d", t=2, h=per, d=dh)
                        dst = vpad[:, :, 0:units, :].rearrange("p t (c h) d -> p t c h d", h=per)
                        o = dve.tensor_copy(dst[:, :, :, h, dh * h:dh * h + dh], src[:, :, :, h, :])
                    o.then_inc(S["av_ev"], 1)

                    def finish(i):
                        dve.wait_ge(S["ae_done"], Q * ROWS + i + 1)
                        dve.reciprocal(drc[:, 0, i, :], dsum[:, i, :]).then_inc(S["ac_done"], 1)
                        dve.wait_ge(S["ac_done"], Q * ROWS + i + 1)
                        u = i if kind else i // 2
                        if kind or i % 2 == 0:
                            if u >= 2:
                                dve.wait_ge(S["at_done"], U + u - 1)
                            for t in range(2):
                                o = dve.tensor_scalar(pn_ring[:, u % 2, t, :], pe_ring[:, i % 4, t, :], drc[:, 0, i, t:t + 1], None, ALU.mult)
                            o.then_inc(S["an_done" if kind else "an_half"], 1)
                        else:
                            dve.tensor_scalar(drc[:, 1, i, :], drc[:, 0, i, :], vec[:, 1:2], None, ALU.mult).then_inc(S["ad_done"], 1)
                            dve.wait_ge(S["ad_done"], U + u + 1)
                            dve.wait_ge(S["an_half"], U + u + 1)
                            for t in range(2):
                                o = dve.scalar_tensor_tensor(pn_ring[:, u % 2, t, :], pe_ring[:, i % 4, t, :], drc[:, 1, i, t:t + 1],
                                                             pn_ring[:, u % 2, t, :], ALU.mult, ALU.add)
                            o.then_inc(S["an_done"], 1)

                    for i in range(ROWS + 2):
                        if i < ROWS:
                            dve.wait_ge(S["as_done"], Q * ROWS + i + 1)
                            dve.tensor_reduce(nm[:, i, :], LNB[i % 4][:, :].rearrange("p (t k) -> p t k", t=2), AX.X, ALU.max, negate=True).then_inc(S["am_done"], 1)
                        if i >= 2:
                            finish(i - 2)
                    dve.wait_ge(S["apv_done"], Q + 1)
                    o = seq_cols(X, gq, jq)
                    if kind == DIFF:
                        dve.tensor_scalar(on, OB[0][:, 0:TOKENS], vec[:, 3:4], None, ALU.mult).then_inc(S["a_on"], 1)
                        dve.wait_ge(S["a_ss"], Q + 1)
                        dve.tensor_scalar(ave[:, :], OB[1][:, 0:2], float(np.finfo(np.float32).eps), None, ALU.add).then_inc(S["a_ve"], 1)
                        dve.wait_ge(S["a_rs"], Q + 1)
                        for t in range(2):
                            dve.tensor_scalar(odg[:, P * t:P * t + P], ident[:, :], ars[:, t:t + 1], None, ALU.mult).then_inc(S["a_dg"], 1)
                        dve.wait_ge(S["a_bc"], Q + 1)
                        dve.tensor_tensor(on2, on, OB[1][:, 0:TOKENS], ALU.mult).then_inc(S["a_on2"], 1)
                        dve.wait_ge(S["a_y"], Q + 1)
                        dve.tensor_scalar(ott, OB[0][:, 0:TOKENS], vec[:, 2:3], vec[:, 5:6], ALU.mult, ALU.add).then_inc(S["a_yt"], 1)
                        dve.wait_ge(S["a_yt"], Q + 1)
                        dve.tensor_tensor(o, ott.rearrange("p (w i) -> p w i", i=WIN), o, ALU.add).then_inc(S["x_done"], 1)
                    else:
                        dve.tensor_copy(on, OB[0][:, 0:TOKENS]).then_inc(S["a_on"], 1)
                        dve.wait_ge(S["a_y"], Q + 1)
                        dve.scalar_tensor_tensor(o, OB[0][:, 0:TOKENS].rearrange("p (w i) -> p w i", i=WIN), vec[:, 6:7], o, ALU.add, ALU.add).then_inc(S["x_done"], 1)

            def stack(p, N0, xb):
                norm(N0, lambda b: batch(b, X), x_ready(xb), lambda b: batch(b, Y), None, "y_ready")
                with dve.Fori(0, DEPTH) as l:
                    G, L, N = tile0(p, l), layer0(p, l), ln_no(p, l)
                    dve.wait_ge(S["tab_done"], L * 4 + 8)
                    dve.wait_ge(S["y_ready"], (L + p + 1) * BATCHES)
                    for n in range(4):
                        attend(G, n, L, n // 2, ((n - 2) // 2, L * WINDOWS + (n - 2) // 2), (True, n >= 2))
                    with dve.Fori(1, WINDOWS // 2) as v:
                        for n in range(4):
                            wy = v * 2 + (n - 2) // 2
                            attend(G + v * 4, n, L, v * 2 + n // 2, (wy, L * WINDOWS + wy))
                    for n in range(2):
                        attend(G + TILES, n, L, 0, (WINDOWS - 1, L * WINDOWS + WINDOWS - 1), (False, True))
                    dve.wait_ge(S["y2_done"], L * WINDOWS + (WINDOWS + 1))
                    for b in range(BATCHES):
                        gg, h = divmod(b, 2)
                        src = Y2[:, gg, :, :].rearrange("p w (j i) -> p w j i", i=WIN)
                        own = src[:, 1 + 4 * h:5 + 4 * h]
                        bef = src[:, 4 * h:4 * h + 4]
                        dst = xs[:, b, :].rearrange("p (w j i) -> p w j i", j=QUADS, i=WIN)
                        dve.tensor_copy(dst[0:64], own[0:64]).then_inc(S["xs_done"], 1)
                        dve.tensor_copy(dst[64:P, :, :, 1:WIN], own[64:P, :, :, 0:WIN - 1]).then_inc(S["xs_done"], 1)
                        dve.tensor_copy(dst[64:P, :, :, 0:1], bef[64:P, :, :, WIN - 1:WIN]).then_inc(S["xs_done"], 1)
                    dve.wait_ge(S["ff_ld"], (L + 1) * 160)

                    def staged(b):
                        dve.wait_ge(S["xs_done"], L * 12 + 3 * b + 3)
                    norm(N, lambda b: xs[:, b, :], staged, lambda b: cen[:, b, :],
                         lambda b: L * BATCHES + b + 1, None)
                    K = L * (BATCHES * 3) + CREDIT

                    def join(b):
                        dve.wait_ge(S["f_done"], L * BATCHES + b + 1)
                        dve.scalar_tensor_tensor(batch(b, Y), TB[b % 2][:, :], lnp[:, 2:3], batch(b, Y2), ALU.add, ALU.add).then_inc(S["y_ready"], 1)

                    for i in range(3 * BATCHES):
                        b, c = divmod(i, 3)
                        dve.wait_ge(S["h_done"], L * (BATCHES * 6) + 2 * i + 2)
                        dve.wait_ge(S["gelu_done"], K + i + 1)
                        if c == 0 and b >= 2:
                            dve.wait_ge(S["f_done"], L * BATCHES + b - 1)
                        r = slice(0, FFC[c])
                        dve.scalar_tensor_tensor(hh[r, b % 2, c, :], FFB[(2 * i + 1) % 4][r, :], b1[r, c:c + 1], gl[r, i % 2, :],
                                                 ALU.add, ALU.mult).then_inc(S["hm_done"], 1)
                        if c == 2 and b >= 1:
                            join(b - 1)
                    join(BATCHES - 1)
                for b in range(BATCHES):
                    dve.wait_ge(S["y_ready"], (DEPTH * (p + 1) + p) * BATCHES + b + 1)
                    dve.scalar_tensor_tensor(batch(b, X), batch(b, Y), 0.5, batch(b, X), ALU.mult, ALU.add).then_inc(S["x_done"], 1)

            run(stack, attention, ffn)


INPUTS = ["L0_attn_Wq", "L0_attn_Wk", "L0_attn_Wv", "L0_attn_norm_w", "L0_attn_Wo", "L0_attn_bo",
          "L0_attn_diff_weight", "L0_ffn_Wqkv", "L0_ffn_q_scale", "L0_ffn_k_scale", "L0_ffn_Wo", "L0_ffn_ln_g",
          "L0_ffn_ln_b", "L0_ffn_W1", "L0_ffn_b1", "L0_ffn_W2", "L0_ffn_b2", "L1_attn_Wk", "L1_attn_Wq",
          "L1_attn_Wo", "L1_attn_bo", "L1_ffn_w_gate", "L1_ffn_w_up", "L1_ffn_w_down"]


def build_program(nc, inputs, stop_after=99):
    fp32 = mybir.dt.float32
    arrays, aps = {}, {}
    for name in ["L0_attn_x"] + INPUTS:
        a = np.ascontiguousarray(inputs[name])
        if a.ndim == 0:
            a = a.reshape(1)
        arrays[name] = a
        aps[name] = nc.dram_tensor(name, a.shape, mybir.dt.from_np(a.dtype), kind="ExternalInput").ap()
    cst = []
    for name, a in zip(("rotary", "mask", "identity"), shape_constants()):
        arrays[name] = a
        cst.append(nc.dram_tensor(name, a.shape, fp32, kind="ExternalInput").ap())
    out = nc.dram_tensor("out", (SEQS, TOKENS, P), fp32, kind="ExternalOutput").ap()
    macaron(nc, aps["L0_attn_x"], aps, cst, out, stop_after)
    return arrays


def kernel(**inputs):
    import concourse.bacc as bacc
    from concourse.bass_utils import run_bass_kernel_spmd

    nc = bacc.Bacc("TRN2", target_bir_lowering=False, num_devices=1)
    arrays = build_program(nc, inputs)
    r = run_bass_kernel_spmd(nc, [arrays], core_ids=[0])
    return r.results[0]["out"]
```

```python
import numpy as np
from contextlib import ExitStack

import concourse.bass as bass
from concourse import mybir

P = 128
GROUPS, QUADS, WINDOWS, WIN = 2, 4, 8, 32
SEQS, TOKENS = GROUPS * QUADS, WINDOWS * WIN
TILES = GROUPS * WINDOWS
BATCH = 512
BATCHES = SEQS * TOKENS // BATCH
DEPTH, HEADS, DH = 6, 16, 64
PAIRS = HEADS // 2
INNER = HEADS * DH
FF = int(P * 4 * 2 / 3)
FFC = [128, 128, FF - 256]
QK_SCALE = 8.0
HID = 384
PASSES = 2
MASKED = -1e30


def shape_constants():
    half = np.arange(0, DH, 2, dtype=np.float32)
    inv_freq = (1.0 / 10000.0 ** (half / DH)).astype(np.float32)
    t = np.arange(TOKENS, dtype=np.float32)
    freqs = t[:, None] * inv_freq[None, :]
    freqs = np.concatenate([freqs, freqs], -1).astype(np.float64)
    base = ((half + np.float32(0.4 * DH)) / np.float32(1.4 * DH)).astype(np.float64)
    power = (t.astype(np.float64) - TOKENS // 2) / (WIN // 2)
    scale = base[None, :] ** power[:, None]
    scale = np.concatenate([scale, scale], -1)
    sign = np.where(np.arange(DH) < DH // 2, -1.0, 1.0)[None, :]
    cos, sin = np.cos(freqs), np.sin(freqs) * sign
    tabs = np.stack([cos * scale, sin * scale, cos / scale, sin / scale])
    tabs = tabs.reshape(4, WINDOWS, 1, WIN, DH)
    tabs = np.broadcast_to(tabs, (4, WINDOWS, QUADS, WIN, DH))
    tabs = tabs.reshape(4, WINDOWS, P, DH).transpose(2, 0, 1, 3)
    i = np.arange(P)[:, None] % WIN
    j = np.arange(WIN)[None, :]
    own, prev = np.where(j <= i, 0.0, MASKED), np.where(j >= i, 0.0, MASKED)
    none = np.full((P, WIN), MASKED)
    mask = np.stack([np.concatenate(x, 1) for x in ([own, none], [prev, own], [own, prev])], 1)
    return (np.ascontiguousarray(tabs, np.float32), np.ascontiguousarray(mask, np.float32),
            np.eye(P, dtype=np.float32))


def macaron(nc, x, w, cst, out, stop_after=99):
    fp32, bf16, i32 = mybir.dt.float32, mybir.dt.bfloat16, mybir.dt.int32
    ALU, ACT, AX = mybir.AluOpType, mybir.ActivationFunctionType, mybir.AxisListType

    with ExitStack() as ctx:
        ctx.enter_context(nc.allow_non_contiguous_dma(reason="a layer's vectors, one element a partition"))

        def sb(name, shape, dt=fp32):
            return ctx.enter_context(nc.sbuf_tensor(name, shape, dt))

        def sem(name):
            return ctx.enter_context(nc.semaphore(name))

        X = sb("X", [P, GROUPS, WINDOWS + 1, P])
        Y = sb("Y", [P, GROUPS, WINDOWS + 1, P])
        ident = sb("ident", [P, P])
        ident_bf = sb("ident_bf", [P, P], bf16)
        ones = sb("ones", [P, P])
        mean_w = sb("mean_w", [P, P])
        mhalf = sb("mhalf", [P, 1])
        zero_bf = sb("zero_bf", [P, P], bf16)
        mask_bf = sb("mask_bf", [P, 3, DH], bf16)
        tabs = sb("tabs", [P, 4, WINDOWS, DH])
        wqkv = sb("wqkv", [P, 3 * INNER])
        wo = sb("wo", [P, PAIRS, P])
        w1 = sb("w1", [P, 2 * FF])
        w2 = sb("w2", [P, 3, P])
        b1 = sb("b1", [P, 6])
        lnp = sb("lnp", [P, 3])
        qks = sb("qks", [P, 2, DH])
        rot = sb("rot", [P, 4, WINDOWS, DH])
        xst = sb("xst", [P, 2, P])
        sq = sb("sq", [P, 2, BATCH])
        t1 = sb("t1", [P, 2, 4, BATCH])
        t2 = sb("t2", [P, 2, BATCH])
        ss = sb("ss", [P, 2, 32])
        rn = sb("rn", [P, 2, 2, 32])
        qT = sb("qT", [P, PAIRS, P])
        kT = [sb(f"kT{g}", [P, PAIRS, QUADS, 2, 2, WIN]) for g in range(2)]
        mx = sb("mx", [P, 2, HEADS])
        pr = sb("pr", [P, 2, PAIRS, 2, DH])
        sm = sb("sm", [P, 2, HEADS])
        rs = sb("rs", [P, 2, HEADS])
        pT = sb("pT", [P, PAIRS, P])
        vj = [sb(f"vj{g}", [P, QUADS, 2, BATCH]) for g in range(2)]
        osb = sb("osb", [P, PAIRS, 2, DH])
        oT = sb("oT", [P, PAIRS, 2, P])
        xs = sb("xs", [P, BATCHES, BATCH])
        vs = xs[:, :, :].rearrange("p (g a) n -> p g a n", g=2)
        cen = sb("cen", [P, BATCHES, BATCH])
        sqd = sb("sqd", [P, BATCHES, BATCH])
        ve = sb("ve", [P, TILES])
        rstd = sb("rstd", [P, TILES])

        wraw = sb("wraw", [P, 7, P])
        iraw = tabs[:, :, :, :].rearrange("p a w d -> p (a w d)")[:, 0:3 * HID].rearrange("p (m n) -> p m n", m=3).bitcast(i32)
        wi = vj[0][:, :, :, :].rearrange("p j a n -> p (j a n)")[:, 0:3 * HID].rearrange("p (m n) -> p m n", m=3)
        vec = sb("vec", [P, 8])
        t1f = t1[:, :, :, :].rearrange("p g c n -> p (g c) n")
        pe_ring = pr[:, :, :, :, :].rearrange("p g m a k -> p (g m a k)").rearrange("p (r t k) -> p r t k", r=4, k=TOKENS)
        pn_ring = t1f[:, 0:2, :].rearrange("p r (t k) -> p r t k", t=2)
        pnT = t1f[:, 2:4, :].rearrange("p r (t k) -> p r t k", t=2)
        qp = t1f[:, 4:6, :].rearrange("p c (r k) -> p (c r) k", k=TOKENS)
        kp = t1f[:, 6:8, :].rearrange("p c (r k) -> p (c r) k", k=TOKENS)
        vpad = osb[:, :, :, :].rearrange("p m a d -> p (m a d)").rearrange("p (t h d) -> p t h d", t=2, d=32)
        oTf = oT[:, :, :, :].rearrange("p m g c -> p (m g c)").rearrange("p (n k) -> p n k", k=TOKENS)
        ys, on, osq, on2, odg, ott = (oTf[:, k, :] for k in range(6))
        rotf = rot[:, :, :, :].rearrange("p a w d -> p (a w d)")
        wqp, wkp = (rotf[:, 512 * k:512 * k + 512].rearrange("p (n d) -> p n d", d=32) for k in range(2))
        wv, wot = (rotf[:, 1024 + P * k:1152 + P * k] for k in range(2))
        nm = sb("nm", [P, HEADS, 2])
        dsum = sb("dsum", [P, HEADS, 2])
        drc = sb("drc", [P, 2, HEADS, 2])
        ave = sb("ave", [P, 2])
        ars = sb("ars", [P, 2])

        gl = sq
        hh = t1[:, :, 0:3, :]

        QB = [ctx.enter_context(nc.psum_tensor(f"QB{i}", [P, BATCH], fp32)) for i in range(2)]
        TB = [ctx.enter_context(nc.psum_tensor(f"TB{i}", [P, BATCH], fp32)) for i in range(2)]
        SB = [ctx.enter_context(nc.psum_tensor(f"SB{i}", [P, BATCH], fp32)) for i in range(2)]
        OB = [ctx.enter_context(nc.psum_tensor(f"OB{i}", [P, BATCH], fp32)) for i in range(2)]
        LNB = [QB[0], QB[1], TB[0], TB[1]]
        FFB = [SB[0], SB[1], OB[0], OB[1]]

        names = """cst_ld cst_done mask_done ln_xn x_ld xt_done xt_ev
            ln_mean ln_cen ln_sqd ln_ss ln_ve ln_rs ln_dg ln_bc ln_out
            wqkv_ld wo_ld ff_ld qs_ld tab_done xst_done
            qkv_done sq_done ss_done rot_done add_done nrm_max nrm_pow qn_done kn_done v_done vj_ld0 vj_ld1
            qkt_done qkt_ev sc_done mx_done sub_done exp_done sum_done rs_done
            pt_done pt_ev pv_done on_done ot_done ot_ev y_done y_add
            xs_done h_done gelu_done hm_done f_done y_ready x_done
            raw_ld int_ld vec_done wt_done wt_ev wdup_done wi_cv wi_done wi_ev n_out
            ys_done aqk_done aqk_ev av_done av_ev as_done am_done ae_done ac_done ad_done an_half an_done at_done at_ev apv_done
            a_on a_sq a_ss a_ve a_rs a_dg a_bc a_on2 a_y a_yt
            on_T on_ev out_st""".split()
        S = {n: sem(n) for n in names}

        def batch(b, t):
            g, h = divmod(b, 2)
            return t[:, g, 1 + 4 * h:5 + 4 * h, :].rearrange("p w c -> p (w c)")

        def natural(ap):
            return [ap[s].rearrange("(w i) e -> i w e", i=WIN) for s in range(SEQS)]

        PHASES = [("stack", 0), ("attend", 0), ("stack", 1), ("ffn", 0), ("attend", 1), ("ffn", 1)]
        X_BEFORE = [0, 4, 12, 16, 20, 28, 32]
        NORM_NO = [0, 1 + DEPTH, 2 + DEPTH, 3 + 2 * DEPTH, 4 + 2 * DEPTH, 5 + 2 * DEPTH]

        def run(stack, attention, ffn):
            for k, (kind, p) in enumerate(PHASES[:stop_after]):
                {"stack": stack, "attend": attention, "ffn": ffn}[kind](p, NORM_NO[k], X_BEFORE[k])

        X_TOTAL = X_BEFORE[min(stop_after, len(PHASES))]

        DIFF = 0
        DHS = [16, 8]
        QS = [8.0 ** -0.5, float(P) ** -0.5]
        UNITS = [8, 16]
        ROWS = 16

        def unit_ready(kind, i):
            if not 0 <= i < ROWS:
                return None
            return i if kind else (i // 2 if i % 2 else None)

        def seq_cols(t, gq, jq):
            return t[:, bass.ds(gq, 1), 1:1 + WINDOWS, bass.ds(jq * WIN, WIN)].rearrange("p g w i -> p (g w) i")

        nat = xs[:, :, :].rearrange("p b (t e) -> p (b t) e", e=P)
        block = ctx.enter_context(nc.Block())

        CREDIT = 2
        PER_PASS = DEPTH * TILES

        def tile0(p, l):
            return l * TILES + (CREDIT + p * PER_PASS)

        def layer0(p, l):
            return l + p * DEPTH

        def ln_no(p, l):
            return l + ((DEPTH + 2) * p + 1)

        @block.sync
        def _(sp):
            sp.sem_inc(S["vj_ld0"], 128)
            sp.sem_inc(S["vj_ld1"], 128)
            for k, (dst, src) in enumerate(((tabs[:, :, :, :], cst[0]), (ident[:, :], cst[2]))):
                sp.dma_start(dst, src).then_inc(S["cst_ld"], 16)
            sp.dma_start(xs[:, 3, 0:3 * DH], cst[1].rearrange("p a b -> p (a b)")).then_inc(S["cst_ld"], 16)
            sp.wait_ge(S["mask_done"], 1)
            for s, src in enumerate(natural(x)):
                g, j = divmod(s, QUADS)
                sp.dma_start(nat[32 * j:32 * j + 32, g * WINDOWS:(g + 1) * WINDOWS, :], src).then_inc(S["x_ld"], 16)

            for k, n in enumerate(("L0_attn_Wq", "L0_attn_Wk", "L0_attn_Wv", "L0_attn_Wo", "L1_attn_Wq", "L1_attn_Wk", "L1_attn_Wo")):
                sp.dma_start(wraw[:, k, :], w[n]).then_inc(S["raw_ld"], 16)
            for k, src in ((0, w["L0_attn_diff_weight"].unsqueeze(0).to_broadcast([P, 1])),
                           (3, w["L0_attn_norm_w"].rearrange("h (d o) -> (h d) o", o=1)),
                           (4, w["L0_attn_bo"].rearrange("(p o) -> p o", o=1)), (6, w["L1_attn_bo"].rearrange("(p o) -> p o", o=1))):
                sp.dma_start(vec[:, k:k + 1], src).then_inc(S["raw_ld"], 16)
            def stack(p, N0, xb):
                with sp.Fori(0, DEPTH) as l:
                    G, L = tile0(p, l), layer0(p, l)
                    sp.wait_ge(S["qkv_done"], G * 6)
                    sp.dma_start(wqkv[:, :], w["L0_ffn_Wqkv"][bass.ds(l, 1), :, :].rearrange("a p n -> p (a n)"),
                                 max_dma_last_dim=16384).then_inc(S["wqkv_ld"], 16)
                    sp.wait_ge(S["tab_done"], L * 4 + 4)
                    for k, n in enumerate(("L0_ffn_q_scale", "L0_ffn_k_scale")):
                        sp.dma_start(qks[:, k, :], w[n][bass.ds(l, 1), :].to_broadcast([P, DH])).then_inc(S["qs_ld"], 16)
                    sp.wait_ge(S["y_done"], L * WINDOWS + 1)
                    sp.dma_start(wo[:, :, :], w["L0_ffn_Wo"][bass.ds(l, 1), :, :].rearrange("a (m p) n -> p (a m) n", p=P)).then_inc(S["wo_ld"], 16)
                    sp.wait_ge(S["y_ready"], (L + (p + 1)) * BATCHES)
                    sp.dma_start(w1[:, :], w["L0_ffn_W1"][bass.ds(l, 1), :, :].rearrange("a p n -> p (a n)")).then_inc(S["ff_ld"], 16)
                    sp.dma_start(w2[:, 0:2, :], w["L0_ffn_W2"][bass.ds(l, 1), 0:256, :].rearrange("a (m p) n -> p (a m) n", p=P)).then_inc(S["ff_ld"], 16)
                    sp.dma_start(w2[0:FFC[2], 2, :], w["L0_ffn_W2"][bass.ds(l, 1), 256:FF, :].rearrange("a p n -> p (a n)")).then_inc(S["ff_ld"], 16)
                    for half in range(2):
                        o = half * FF
                        sp.dma_start(b1[:, 3 * half:3 * half + 2], w["L0_ffn_b1"][bass.ds(l, 1), o:o + 256].rearrange("a (m p) -> p (a m)", p=P)).then_inc(S["ff_ld"], 16)
                        sp.dma_start(b1[0:FFC[2], 3 * half + 2:3 * half + 3], w["L0_ffn_b1"][bass.ds(l, 1), o + 256:o + FF].rearrange("a p -> p a")).then_inc(S["ff_ld"], 16)
                    for k, n in enumerate(("L0_ffn_ln_g", "L0_ffn_ln_b", "L0_ffn_b2")):
                        sp.dma_start(lnp[:, k:k + 1], w[n][bass.ds(l, 1), :].rearrange("a p -> p a")).then_inc(S["ff_ld"], 16)

                    def spread(G, w_par, g):
                        sp.wait_ge(S["v_done"], G * 2 + 2)
                        for j in range(QUADS):
                            for h2 in range(2):
                                sp.dma_start(vj[g][64 * h2 + 32 * w_par:64 * h2 + 32 * w_par + 32, j, h2, :],
                                             vs[32 * j:32 * j + 32, g, h2, :]).then_inc(S[f"vj_ld{g}"], 16)

                    with sp.Fori(0, WINDOWS // 2) as wp:
                        for k in range(4):
                            spread(G + wp * 4 + k, k // 2, k % 2)

            run(stack, lambda *a: None, lambda *a: None)
            if stop_after > 3:
                sp.wait_ge(S["tab_done"], 4 * DEPTH * PASSES + 4)
                for k, n in enumerate(("L1_ffn_w_gate", "L1_ffn_w_up")):
                    sp.dma_start(iraw[:, k, :].rearrange("p (c d) -> p c d", d=P), w[n].rearrange("(c p) d -> p c d", p=P)).then_inc(S["int_ld"], 16)
                sp.dma_start(iraw[:, 2, :], w["L1_ffn_w_down"]).then_inc(S["int_ld"], 16)
            sp.wait_ge(S["on_ev"], 4)
            for s, dst in enumerate(natural(out)):
                g, j = divmod(s, QUADS)
                sp.dma_start(dst, nat[32 * j:32 * j + 32, g * WINDOWS:(g + 1) * WINDOWS, :]).then_inc(S["out_st"], 16)
            sp.wait_ge(S["out_st"], 16 * SEQS)

        @block.gpsimd
        def _(gp):
            gp.memset(ones[:, :], 1.0).then_inc(S["cst_done"], 1)

            gp.wait_ge(S["cst_done"], 5)

            def power(N):
                gp.wait_ge(S["ln_ve"], N + 1)
                gp.tensor_tensor(rstd[:, :], ve[:, :], mhalf[:, 0:1].to_broadcast([P, TILES]), ALU.pow).then_inc(S["ln_rs"], 1)

            def project(G, g):
                for k in range(2):
                    for c in (2 * k, 2 * k + 1):
                        gp.wait_ge(S["rot_done"], G * 8 + 2 * c + 2)
                        gp.tensor_tensor(t1[:, g, c, :], t1[:, g, c, :], t2[:, c % 2, :], ALU.add).then_inc(S["add_done"], 1)
                    gp.wait_ge(S["nrm_max"], G * 2 + k + 1)
                    if k == 0:
                        gp.wait_ge(S["qn_done"], G - 1)
                    else:
                        gp.wait_ge(S["kn_done"], G - 1)
                    gp.tensor_tensor(rn[:, g, 1, 16 * k:16 * k + 16], rn[:, g, 0, 16 * k:16 * k + 16],
                                     mhalf[:, 0:1].to_broadcast([P, 16]), ALU.pow).then_inc(S["nrm_pow"], 1)
                gp.wait_ge(S["nrm_pow"], G * 2 + 2)
                gp.wait_ge(S["add_done"], G * 4 + 4)
                t = t1[:, g, 2:4, :].rearrange("p c (h d) -> p (c h) d", d=DH)
                r = rn[:, g, 1, 16:32].unsqueeze(2).to_broadcast([P, 16, DH])
                gp.tensor_tensor(t, t, r, ALU.mult).then_inc(S["kn_done"], 1)

            gp.sem_inc(S["nrm_pow"], 2 * CREDIT)
            gp.sem_inc(S["tab_done"], 4)
            gp.sem_inc(S["a_rs"], 1)
            gp.sem_inc(S["add_done"], 4 * CREDIT)
            gp.sem_inc(S["kn_done"], CREDIT)

            def attention(kind, N0, xb):
                power(N0)
                if kind == DIFF:
                    with gp.Fori(0, SEQS) as q:
                        gp.wait_ge(S["a_ve"], q + 2)
                        gp.tensor_tensor(ars[:, :], ave[:, :], mhalf[:, 0:1].to_broadcast([P, 2]), ALU.pow).then_inc(S["a_rs"], 1)

            def ffn(q, N0, xb):
                power(N0)

            def stack(p, N0, xb):
                power(N0)
                with gp.Fori(0, DEPTH) as l:
                    G, L = tile0(p, l), layer0(p, l)
                    gp.wait_ge(S["qs_ld"], L * 32 + 32)
                    gp.wait_ge(S["rot_done"], G * 8)
                    gp.wait_ge(S["cst_ld"], 48)
                    for k in range(4):
                        s = qks[:, k // 2, :].rearrange("p (w t d) -> p w t d", w=1, t=2)
                        if k % 2:
                            s = s[:, :, ::-1, :]
                        gp.tensor_tensor(rot[:, k, :, :].rearrange("p w (t d) -> p w t d", t=2),
                                         tabs[:, k, :, :].rearrange("p w (t d) -> p w t d", t=2),
                                         s.to_broadcast([P, WINDOWS, 2, DH // 2]), ALU.mult).then_inc(S["tab_done"], 1)
                    with gp.Fori(0, WINDOWS) as v:
                        for g in range(2):
                            project(G + v * 2 + g, g)
                    power(ln_no(p, l))

            run(stack, attention, ffn)

        @block.tensor
        def _(pe):
            for n, k in (("qkv_done", 6), ("qkt_done", 4), ("sc_done", 2), ("pt_done", 2), ("pv_done", 2), ("ot_done", 2)):
                pe.sem_inc(S[n], k * CREDIT)
            for n, k in (("y_done", 1), ("aqk_done", 4), ("av_done", 1), ("as_done", ROWS), ("at_done", UNITS[0]), ("apv_done", 1),
                         ("a_ss", 1), ("a_bc", 1), ("a_y", 1)):
                pe.sem_inc(S[n], k)
            pe.wait_ge(S["cst_ld"], 48)
            pe.wait_ge(S["cst_done"], 5)
            pe.wait_ge(S["mask_done"], 1)
            pe.wait_ge(S["x_ld"], 16 * SEQS)

            def to_features():
                for b in range(BATCHES):
                    for t in range(4):
                        last = pe.transpose(LNB[b][:, P * t:P * t + P], nat[:, 4 * b + t, :], ident[:, :])
                    last.then_inc(S["xt_done"], 1)

            def norm(N, src, ready):
                for b in range(BATCHES):
                    ready(b)
                    pe.matmul(LNB[b][:, :], mean_w[:, :], src(b), start=True, stop=True).then_inc(S["ln_mean"], 1)
                for b in range(BATCHES):
                    pe.wait_ge(S["ln_sqd"], N * BATCHES + b + 1)
                    for t in range(4):
                        last = pe.matmul(SB[0][:, 4 * b + t:4 * b + t + 1], sqd[:, b, P * t:P * t + P], mean_w[:, 0:1],
                                         start=(b == 0 and t == 0), stop=True, skip_group_check=True)
                    last.then_inc(S["ln_ss"], 1)
                for b in range(BATCHES):
                    pe.wait_ge(S["ln_dg"], N * TILES + 4 * b + 4)
                    pe.wait_ge(S["ln_cen"], N * BATCHES + b + 1)
                    pe.matmul(LNB[b][:, :], ones[:, :], sqd[:, b, :], start=True, stop=True).then_inc(S["ln_bc"], 1)

            def qkv(G, g, chunks):
                for c in chunks:
                    if c < 2:
                        pe.wait_ge(S["v_done"], G * 2 - 1 + c)
                    else:
                        pe.wait_ge(S["rot_done"], G * 8 + 2 * c - 2)
                    pe.matmul(QB[c % 2][:, :], xst[:, g, :], wqkv[:, BATCH * c:BATCH * c + BATCH],
                              start=True, stop=True).then_inc(S["qkv_done"], 1)

            def transposes(src, free, done):
                for k in range(2):
                    free(k)
                    for m in range(4):
                        last = pe.transpose(TB[k][:, P * m:P * m + P], src(4 * k + m), ident[:, :])
                    last.then_inc(S[done], 1)

            def q_transposes(G, g):
                pe.wait_ge(S["qn_done"], G + 1)
                transposes(lambda m: t1[:, g, m // 4, P * (m % 4):P * (m % 4) + P],
                           lambda k: pe.wait_ge(S["pt_ev"], G * 2 - 1 + k), "qkt_done")

            def k_transposes(G, g):
                pe.wait_ge(S["kn_done"], G + 1)
                transposes(lambda m: t1[:, g, 2 + m // 4, P * (m % 4):P * (m % 4) + P],
                           lambda k: pe.wait_ge(S["qkt_ev"], G * 6 + k + 1), "qkt_done")

            def scores(G, g, mask):
                pe.wait_ge(S["sub_done"], G * 2)
                for k in range(2):
                    if k:
                        pe.wait_ge(S["qkt_ev"], G * 6 + 6)
                    pe.matmul(SB[k][:, :].rearrange("p (m k) -> p m k", k=DH), ident_bf[:, :],
                              mask_bf[:, mask:mask + 1, :].to_broadcast([P, 8, DH]), start=True, stop=True)
                for m in range(PAIRS):
                    for j in range(QUADS):
                        last = pe.matmul(SB[m // 4][32 * j:32 * j + 32, P * (m % 4):P * (m % 4) + P],
                                         qT[:, m, 32 * j:32 * j + 32],
                                         kT[g][:, m, j, :, :, :].rearrange("p a s k -> p (a s k)"),
                                         start=False, stop=True, skip_group_check=True)
                    if m % 4 == 3:
                        last.then_inc(S["sc_done"], 1)

            def p_transposes(G, g):
                def free(k):
                    pe.wait_ge(S["exp_done"], G * 2 + k + 1)
                    pe.wait_ge(S["ot_ev"], G * 2 - 1 + k)
                transposes(lambda m: pr[:, g, m, :, :].rearrange("p a b -> p (a b)"), free, "pt_done")

            def values(G, g, v_no, y_no):
                pe.wait_ge(S["y_add"], y_no)
                pe.wait_ge(S["on_done"], G * 2)
                pe.wait_ge(S[f"vj_ld{g}"], v_no * 128)
                pe.wait_ge(S["pt_ev"], G * 2 + 2)
                for m in range(PAIRS):
                    for j in range(QUADS):
                        last = pe.matmul(OB[m // 4][32 * j:32 * j + 32, P * (m % 4):P * (m % 4) + P],
                                         pT[:, m, 32 * j:32 * j + 32], vj[g][:, j, :, DH * m:DH * m + DH],
                                         start=True, stop=True, skip_group_check=True)
                    if m % 4 == 3:
                        last.then_inc(S["pv_done"], 1)

            def o_transposes(G, b):
                def free(k):
                    pe.wait_ge(S["on_done"], G * 2 + k + 1)
                    if b:
                        pe.wait_ge(S["qkt_ev"], G * 6 + 10 + 2 * k)
                transposes(lambda m: osb[:, m, :, :].rearrange("p a b -> p (a b)"), free, "ot_done")

            def output(G):
                pe.wait_ge(S["ot_ev"], G * 2 + 2)
                for m in range(PAIRS):
                    last = pe.matmul(OB[0][:, 0:2 * P], wo[:, m, :], oT[:, m, :, :].rearrange("p g c -> p (g c)"),
                                     start=(m == 0), stop=(m == PAIRS - 1))
                last.then_inc(S["y_done"], 1)

            def attend(G0, n, base, first, parts=(True, True, True)):
                a, b, c = parts
                g = n % 2
                G = base + n
                if a:
                    if n == 0 and first:
                        pe.wait_ge(S["wqkv_ld"], G0[1] * 16 + 16)
                    pe.wait_ge(S["xst_done"], G * 3 + 3)
                    qkv(G, g, (0, 1))
                if b:
                    q_transposes(G - 1, 1 - g)
                if c:
                    values(G - 2, g, G0[2] + (n - 2) // 2 + 2, G0[2] + (n - 2 - g) // 2 + 1)
                if b:
                    k_transposes(G - 1, 1 - g)
                if a:
                    qkv(G, g, (2,))
                if c:
                    o_transposes(G - 2, b)
                if a:
                    qkv(G, g, (3,))
                if b:
                    mask = 0 if (first and n - 1 < 2) else (1 if (n - 1) // 2 % 2 else 2)
                    scores(G - 1, 1 - g, mask)
                if c and g == 1:
                    if n == 3 and first:
                        pe.wait_ge(S["wo_ld"], G0[1] * 16 + 16)
                    output(G - 2)
                if a:
                    qkv(G, g, (4, 5))
                if b:
                    p_transposes(G - 1, 1 - g)

            def feed_forward(p, L, N):
                pe.wait_ge(S["ff_ld"], (L + 1) * 160)
                K = L * (BATCHES * 3) + CREDIT

                def up(b):
                    pe.wait_ge(S["ln_out"], L * BATCHES + b + 1)
                    for k in range(6):
                        i, c = 6 * b + k, k // 2
                        pe.wait_ge(S["hm_done" if k % 2 else "gelu_done"], K + (i // 2 - 2 + 1))
                        col = P * c + (0 if k % 2 else FF)
                        pe.matmul(FFB[i % 4][0:FFC[c], :], w1[:, col:col + FFC[c]], cen[:, b, :],
                                  start=True, stop=True).then_inc(S["h_done"], 1)

                def down(b):
                    pe.wait_ge(S["hm_done"], K + 3 * b + 3)
                    pe.wait_ge(S["ln_out"], (L + 1) * BATCHES)
                    if b >= 2:
                        pe.wait_ge(S["y_ready"], (L + p + 1) * BATCHES + b - 1)
                    for c in range(3):
                        last = pe.matmul(TB[b % 2][:, :], w2[0:FFC[c], c, :], hh[0:FFC[c], b % 2, c, :],
                                         start=(c == 0), stop=(c == 2))
                    last.then_inc(S["f_done"], 1)

                up(0)
                for b in range(1, BATCHES):
                    up(b)
                    down(b - 1)
                down(BATCHES - 1)

            def x_ready(xb):
                if xb == 0:
                    return lambda b: pe.wait_ge(S["xt_ev"], b + 1)
                return lambda b: pe.wait_ge(S["x_done"], xb)

            def ffn(q, N0, xb):
                if q == 0:
                    pe.wait_ge(S["wi_cv"], 3)
                    for m in range(3):
                        for c in range(3):
                            last = pe.transpose(FFB[m][:, P * c:P * c + P], wqkv[:, HID * m + P * c:HID * m + P * c + P], ident[:, :])
                        last.then_inc(S["wi_done"], 1)
                    pe.wait_ge(S["wi_ev"], 3)
                norm(N0, lambda b: batch(b, X), x_ready(xb))
                L = PASSES * DEPTH + q
                K = L * (BATCHES * 3) + CREDIT

                def up(b):
                    pe.wait_ge(S["n_out"], (1 + 2 * q) * BATCHES + b + 1)
                    for k in range(6):
                        i, c = 6 * b + k, k // 2
                        pe.wait_ge(S["hm_done" if k % 2 else "gelu_done"], K + (i // 2 - 2 + 1))
                        pe.matmul(FFB[i % 4][:, :], wi[:, k % 2, P * c:P * c + P], cen[:, b, :], start=True, stop=True).then_inc(S["h_done"], 1)

                def down(b):
                    pe.wait_ge(S["hm_done"], K + 3 * b + 3)
                    pe.wait_ge(S["n_out"], (1 + 2 * q) * BATCHES + BATCHES)
                    if b >= 2:
                        pe.wait_ge(S["x_done"], xb + b - 1)
                    for c in range(3):
                        last = pe.matmul(TB[b % 2][:, :], wi[:, 2, P * c:P * c + P], hh[:, b % 2, c, :], start=(c == 0), stop=(c == 2))
                    last.then_inc(S["f_done"], 1)

                up(0)
                for b in range(1, BATCHES):
                    up(b)
                    down(b - 1)
                down(BATCHES - 1)

            def attention(kind, N0, xb):
                if kind == DIFF:
                    pe.wait_ge(S["raw_ld"], 16 * 11)
                    for k in range(4):
                        last = pe.transpose(SB[0][:, P * k:P * k + P], wraw[:, k, :], ident[:, :])
                    last.then_inc(S["wt_done"], 1)
                    pe.wait_ge(S["wt_ev"], 2)
                pe.wait_ge(S["wdup_done"], 4 * kind + 4)
                norm(N0, lambda b: batch(b, X), x_ready(xb))
                wvv = wv if kind == DIFF else wraw[:, 5, :]
                woo = wot if kind == DIFF else wraw[:, 6, :]
                dh = DHS[kind]
                per = 32 // dh
                units = UNITS[kind]
                with pe.Fori(0, SEQS) as s:
                    Q = s + (SEQS * kind + 1)
                    U = s * units + (SEQS * UNITS[0] * kind + UNITS[0])
                    pe.wait_ge(S["ys_done"], Q + 1)
                    pe.wait_ge(S["ae_done"], Q * ROWS)
                    for k, wp in enumerate((wqp, wkp)):
                        for h in range(2):
                            for r_ in range(2):
                                c = 4 * (2 * h + r_)
                                last = pe.matmul(LNB[2 * k + h][:, TOKENS * r_:TOKENS * r_ + TOKENS],
                                                 wp[:, c:c + 4, :].rearrange("p n d -> p (n d)"), ys, start=True, stop=True, skip_group_check=True)
                            last.then_inc(S["aqk_done"], 1)
                    pe.wait_ge(S["at_ev"], U)
                    for t in range(2):
                        last = pe.matmul(SB[0][:, P * t:P * t + P], ys[:, P * t:P * t + P], wvv, start=True, stop=True, skip_group_check=True)
                    last.then_inc(S["av_done"], 1)
                    pe.wait_ge(S["aqk_ev"], Q * 4 + 4)
                    for i in range(ROWS + 5):
                        if i < ROWS:
                            a, r_ = i % 4, i // 4
                            if i >= 4:
                                pe.wait_ge(S["ae_done"], Q * ROWS + i - 3)
                            for t in range(2):
                                last = pe.matmul(LNB[a][:, TOKENS * t:TOKENS * t + TOKENS],
                                                 qp[32 * a:32 * a + 8, r_, P * t:P * t + P], kp[32 * a:32 * a + 8, r_, :],
                                                 start=True, stop=True, skip_group_check=True)
                            last.then_inc(S["as_done"], 1)
                        u = unit_ready(kind, i - 3)
                        if u is not None:
                            pe.wait_ge(S["an_done"], U + u + 1)
                            if u < 2:
                                pe.wait_ge(S["av_ev"], Q + 1)
                            else:
                                pe.wait_ge(S["at_ev"], U + u - 1)
                            for kb in range(2):
                                for t in range(2):
                                    last = pe.transpose(SB[u % 2][:, TOKENS * kb + P * t:TOKENS * kb + P * t + P],
                                                        pn_ring[:, u % 2, t, P * kb:P * kb + P], ident[:, :])
                            last.then_inc(S["at_done"], 1)
                        u = unit_ready(kind, i - 4)
                        if u is not None:
                            if u == 0:
                                pe.wait_ge(S["x_done"], xb + s)
                            pe.wait_ge(S["at_ev"], U + u + 1)
                            c = 32 * (u // per)
                            for kb in range(2):
                                last = pe.matmul(OB[0][c:c + 32, 0:TOKENS], vpad[:, kb, u, :], pnT[:, u % 2, kb, :],
                                                 start=(u % per == 0 and kb == 0), stop=(u % per == per - 1 and kb == 1))
                    last.then_inc(S["apv_done"], 1)
                    if kind == DIFF:
                        pe.wait_ge(S["a_sq"], Q + 1)
                        for t in range(2):
                            last = pe.matmul(OB[1][:, t:t + 1], osq[:, P * t:P * t + P], mean_w[:, 0:1], start=(t == 0), stop=True, skip_group_check=True)
                        last.then_inc(S["a_ss"], 1)
                        pe.wait_ge(S["a_dg"], Q * 2 + 2)
                        pe.matmul(OB[1][:, 0:TOKENS], ones[:, :], odg, start=True, stop=True).then_inc(S["a_bc"], 1)
                        pe.wait_ge(S["a_on2"], Q + 1)
                        pe.matmul(OB[0][:, 0:TOKENS], woo, on2, start=True, stop=True).then_inc(S["a_y"], 1)
                    else:
                        pe.wait_ge(S["a_on"], Q + 1)
                        pe.matmul(OB[0][:, 0:TOKENS], woo, on, start=True, stop=True).then_inc(S["a_y"], 1)

            def stack(p, N0, xb):
                norm(N0, lambda b: batch(b, X), x_ready(xb))
                with pe.Fori(0, DEPTH) as l:
                    G, L, N = tile0(p, l), layer0(p, l), ln_no(p, l)
                    G0 = (G, L, L * WINDOWS)
                    for n in range(4):
                        attend(G0, n, G, True, (True, n >= 1, n >= 2))
                    with pe.Fori(1, WINDOWS // 2) as v:
                        Gv = (G, L, L * WINDOWS + v * 2)
                        for n in range(4):
                            attend(Gv, n, G + v * 4, False)
                    Ge = (G, L, L * WINDOWS + WINDOWS)
                    attend(Ge, 0, G + TILES, False, (False, True, True))
                    attend(Ge, 1, G + TILES, False, (False, False, True))

                    def staged(b):
                        pe.wait_ge(S["xs_done"], L * 12 + 3 * b + 3)
                    norm(N, lambda b: xs[:, b, :], staged)
                    feed_forward(p, L, N)

            to_features()
            run(stack, attention, ffn)

            def to_tokens():
                for b in range(BATCHES):
                    pe.wait_ge(S["x_done"], X_TOTAL)
                    for t in range(4):
                        last = pe.transpose(LNB[b][:, P * t:P * t + P], batch(b, X)[:, P * t:P * t + P], ident[:, :])
                    last.then_inc(S["on_T"], 1)
            to_tokens()

        @block.scalar
        def _(act):
            act.sem_inc(S["sq_done"], 4 * CREDIT)
            act.sem_inc(S["xst_done"], 3 * CREDIT)
            act.sem_inc(S["v_done"], 2 * CREDIT)
            act.sem_inc(S["qkt_ev"], 6 * CREDIT)
            act.sem_inc(S["exp_done"], 2 * CREDIT)
            act.sem_inc(S["pt_ev"], 2 * CREDIT)
            act.sem_inc(S["ot_ev"], 2 * CREDIT)
            act.sem_inc(S["gelu_done"], CREDIT)
            for n, k in (("aqk_ev", 4), ("ae_done", ROWS), ("at_ev", UNITS[0]), ("a_sq", 1)):
                act.sem_inc(S[n], k)
            for b in range(BATCHES):
                act.wait_ge(S["xt_done"], b + 1)
                act.activation(batch(b, X), LNB[b][:, :], ACT.Copy).then_inc(S["xt_ev"], 1)

            def squares(N):
                for b in range(BATCHES):
                    act.wait_ge(S["ln_cen"], N * BATCHES + b + 1)
                    act.activation(sqd[:, b, :], cen[:, b, :], ACT.Square).then_inc(S["ln_sqd"], 1)

            def stage(G, wx, g):
                act.wait_ge(S["qkv_done"], (G - 1) * 6)
                yt = Y[:, g, bass.ds(wx, 2), :].rearrange("p a (j i) -> p a j i", i=WIN)
                xt = xst[:, g, :].rearrange("p (a j i) -> p a j i", a=1, i=WIN)
                act.activation(xt[0:64], yt[0:64, 1:2], ACT.Copy).then_inc(S["xst_done"], 1)
                act.activation(xt[64:P, :, :, 1:WIN], yt[64:P, 1:2, :, 0:WIN - 1], ACT.Copy).then_inc(S["xst_done"], 1)
                act.activation(xt[64:P, :, :, 0:1], yt[64:P, 0:1, :, WIN - 1:WIN], ACT.Copy).then_inc(S["xst_done"], 1)

            def attend(base, n, w0, y_no, parts=(True, True, True)):
                a, b, c = parts
                g, G = n % 2, base + n

                def square(c4):
                    act.wait_ge(S["qkv_done"], G * 6 + c4 + 1)
                    act.wait_ge(S["ss_done"], G * 4 + c4 - 1)
                    act.activation(sq[:, c4 % 2, :], QB[c4 % 2][:, :], ACT.Square).then_inc(S["sq_done"], 1)

                if a:
                    if n == 0:
                        stage(G, w0, 0)
                    square(0)
                    square(1)
                    if n < 3:
                        stage(G + 1, w0 + (n + 1) // 2, 1 - g)
                if b:
                    slot = ((n - 1) // 2) % 2
                    act.wait_ge(S["sc_done"], (G - 1) * 2)
                    for k in range(4):
                        act.wait_ge(S["qkt_done"], (G - 1) * 4 + k + 1)
                        if k < 2:
                            act.activation(qT[:, 4 * k:4 * k + 4, :], TB[k][:, :].rearrange("p (m q) -> p m q", m=4), ACT.Copy).then_inc(S["qkt_ev"], 1)
                        else:
                            for h2 in range(2):
                                r = slice(64 * h2, 64 * h2 + 64)
                                act.activation(kT[1 - g][r, 4 * k - 8:4 * k - 4, :, h2, slot, :],
                                               TB[k % 2][r, :].rearrange("p (m j q) -> p m j q", m=4, q=WIN), ACT.Copy).then_inc(S["qkt_ev"], 1)
                if a:
                    square(2)
                if c:
                    act.wait_ge(S["y_done"], y_no + 1)
                    for k in range(2):
                        act.wait_ge(S["ot_done"], (G - 2) * 2 + k + 1)
                        act.activation(oT[:, 4 * k:4 * k + 4, g, :], TB[k][:, :].rearrange("p (m q) -> p m q", m=4), ACT.Copy).then_inc(S["ot_ev"], 1)
                if a:
                    square(3)
                    act.wait_ge(S[f"vj_ld{g}"], (y_no + 2) * 128)
                    act.wait_ge(S["pv_done"], G * 2 - 2)
                    for k in range(2):
                        act.wait_ge(S["qkv_done"], G * 6 + 5 + k)
                        act.activation(vs[:, g, :, 256 * k:256 * k + 256].rearrange("p a (m d) -> p m a d", d=DH),
                                       QB[k][:, :].rearrange("p (m a d) -> p m a d", a=2, d=DH), ACT.Copy).then_inc(S["v_done"], 1)
                if b:
                    for k in range(2):
                        act.wait_ge(S["sub_done"], (G - 1) * 2 + k + 1)
                        t = pr[:, 1 - g, 4 * k:4 * k + 4, :, :].rearrange("p m a k -> p (m a k)")
                        act.activation(t, t, ACT.Exp, scale=QK_SCALE).then_inc(S["exp_done"], 1)
                    act.wait_ge(S["pv_done"], G * 2 - 2)
                    for k in range(2):
                        act.wait_ge(S["pt_done"], (G - 1) * 2 + k + 1)
                        act.activation(pT[:, 4 * k:4 * k + 4, :].rearrange("p m q -> p (m q)"), TB[k][:, :], ACT.Copy).then_inc(S["pt_ev"], 1)
                    if n == 3:
                        pass

            def ffn(q, N0, xb):
                squares(N0)
                L = PASSES * DEPTH + q
                K = L * (BATCHES * 3) + CREDIT
                for i in range(3 * BATCHES):
                    act.wait_ge(S["h_done"], L * (BATCHES * 6) + 2 * i + 1)
                    act.wait_ge(S["hm_done"], K + (i - 2 + 1))
                    act.activation(gl[:, i % 2, :], FFB[(2 * i) % 4][:, :], ACT.Silu).then_inc(S["gelu_done"], 1)

            def attention(kind, N0, xb):
                squares(N0)
                units = UNITS[kind]
                with act.Fori(0, SEQS) as s:
                    Q = s + (SEQS * kind + 1)
                    U = s * units + (SEQS * UNITS[0] * kind + UNITS[0])
                    act.wait_ge(S["as_done"], Q * ROWS)
                    for k in range(4):
                        act.wait_ge(S["aqk_done"], Q * 4 + k + 1)
                        dst = (qp if k < 2 else kp)[:, 2 * (k % 2):2 * (k % 2) + 2, :]
                        act.activation(dst, LNB[k][:, :].rearrange("p (r n) -> p r n", n=TOKENS), ACT.Copy,
                                       scale=QS[kind] if k < 2 else 1.0).then_inc(S["aqk_ev"], 1)
                    for i in range(ROWS + 3):
                        if i < ROWS:
                            act.wait_ge(S["am_done"], Q * ROWS + i + 1)
                            if i < 4:
                                act.wait_ge(S["an_done"], U)
                            elif kind != DIFF:
                                act.wait_ge(S["an_done"], U + i - 3)
                            else:
                                act.wait_ge(S["an_done" if i % 2 else "an_half"], U + (i - 4) // 2 + 1)
                            for t in range(2):
                                last = act.activation(pe_ring[:, i % 4, t, :], LNB[i % 4][:, TOKENS * t:TOKENS * t + TOKENS], ACT.Exp,
                                                      bias=nm[:, i, t:t + 1], accum_out=dsum[:, i, t:t + 1])
                            last.then_inc(S["ae_done"], 1)
                        u = unit_ready(kind, i - 3)
                        if u is not None:
                            act.wait_ge(S["at_done"], U + u + 1)
                            act.activation(pnT[:, u % 2, :, :], SB[u % 2][:, :].rearrange("p (t k) -> p t k", t=2), ACT.Copy).then_inc(S["at_ev"], 1)
                    if kind == DIFF:
                        act.wait_ge(S["a_on"], Q + 1)
                        act.activation(osq, OB[0][:, 0:TOKENS], ACT.Square).then_inc(S["a_sq"], 1)

            def stack(p, N0, xb):
                squares(N0)
                with act.Fori(0, DEPTH) as l:
                    G, L, N = tile0(p, l), layer0(p, l), ln_no(p, l)
                    act.wait_ge(S["y_ready"], (L + p + 1) * BATCHES)
                    W = L * WINDOWS
                    for n in range(4):
                        attend(G, n, 0, W + (n - 2) // 2, (True, n >= 1, n >= 2))
                    with act.Fori(1, WINDOWS // 2) as v:
                        for n in range(4):
                            attend(G + v * 4, n, v * 2, W + v * 2 + (n - 2) // 2)
                    for n in range(2):
                        attend(G + TILES, n, 0, W + WINDOWS + (n - 2) // 2, (False, n == 0, True))
                    squares(N)
                    K = L * (BATCHES * 3) + CREDIT
                    act.wait_ge(S["ff_ld"], (L + 1) * 160)
                    for i in range(3 * BATCHES):
                        b, c = divmod(i, 3)
                        act.wait_ge(S["h_done"], L * (BATCHES * 6) + 2 * i + 1)
                        act.wait_ge(S["hm_done"], K + (i - 2 + 1))
                        r = slice(0, FFC[c])
                        act.activation(gl[r, i % 2, :], FFB[(2 * i) % 4][r, :], ACT.Gelu, bias=b1[r, 3 + c:4 + c]).then_inc(S["gelu_done"], 1)

            run(stack, attention, ffn)
            for b in range(BATCHES):
                act.wait_ge(S["on_T"], b + 1)
                act.activation(nat[:, 4 * b:4 * b + 4, :].rearrange("p t e -> p (t e)"), LNB[b][:, :], ACT.Copy).then_inc(S["on_ev"], 1)

        @block.vector
        def _(dve):
            dve.sem_inc(S["rot_done"], 8 * CREDIT)
            dve.sem_inc(S["ss_done"], 4 * CREDIT)
            dve.sem_inc(S["mx_done"], 2 * CREDIT)
            dve.sem_inc(S["nrm_max"], 2 * CREDIT)
            dve.sem_inc(S["qn_done"], CREDIT)
            dve.sem_inc(S["sub_done"], 2 * CREDIT)
            dve.sem_inc(S["sum_done"], CREDIT)
            dve.sem_inc(S["rs_done"], CREDIT)
            dve.sem_inc(S["on_done"], 2 * CREDIT)
            dve.sem_inc(S["hm_done"], CREDIT)
            for n, k in (("y_add", 1), ("ys_done", 1), ("av_ev", 1), ("am_done", ROWS), ("ac_done", ROWS), ("ad_done", UNITS[0]),
                         ("an_half", UNITS[0]), ("an_done", UNITS[0]), ("a_on", 1), ("a_ve", 1), ("a_dg", 2), ("a_on2", 1), ("a_yt", 1)):
                dve.sem_inc(S[n], k)
            dve.wait_ge(S["cst_ld"], 48)
            dve.tensor_copy(mask_bf[:, :, :].rearrange("p a b -> p (a b)"), xs[:, 3, 0:3 * DH]).then_inc(S["mask_done"], 1)
            dve.tensor_copy(ident_bf[:, :], ident[:, :]).then_inc(S["cst_done"], 1)
            dve.memset(mean_w[:, :], 1.0 / P).then_inc(S["cst_done"], 1)
            dve.memset(mhalf[:, :], -0.5).then_inc(S["cst_done"], 1)
            dve.memset(zero_bf[:, :], 0.0)
            for g in range(2):
                dve.memset(kT[g][:, :, :, :, :, :], 0.0)
                dve.memset(vj[g][:, :, :, :], 0.0)
            dve.memset(Y[:, :, 0, :], 0.0).then_inc(S["cst_done"], 1)

            def norm(N, src, ready, dst, affine, done):
                for b in range(BATCHES):
                    dve.wait_ge(S["ln_mean"], N * BATCHES + b + 1)
                    ready(b)
                    dve.tensor_tensor(cen[:, b, :], src(b), LNB[b][:, :], ALU.subtract).then_inc(S["ln_cen"], 1)
                dve.wait_ge(S["ln_ss"], (N + 1) * BATCHES)
                dve.tensor_scalar(ve[:, :], SB[0][:, 0:TILES], 1e-5, None, ALU.add).then_inc(S["ln_ve"], 1)
                dve.wait_ge(S["ln_rs"], N + 1)
                for t in range(TILES):
                    b, k = divmod(t, 4)
                    dve.tensor_scalar(sqd[:, b, P * k:P * k + P], ident[:, :], rstd[:, t:t + 1], None, ALU.mult).then_inc(S["ln_dg"], 1)
                for b in range(BATCHES):
                    dve.wait_ge(S["ln_bc"], N * BATCHES + b + 1)
                    o = dve.tensor_tensor(dst(b), cen[:, b, :], LNB[b][:, :], ALU.mult)
                    if not affine:
                        o.then_inc(S[done], 1)
                    else:
                        o.then_inc(S["ln_xn"], 1)
                if affine:
                    for b in range(BATCHES):
                        dve.wait_ge(S["ln_xn"], affine(b))
                        dve.tensor_scalar(dst(b), dst(b), lnp[:, 0:1], lnp[:, 1:2], ALU.mult, ALU.add).then_inc(S["ln_out"], 1)

            def attend(base, n, w_a, w_c, y_no, parts=(True, True, True)):
                a, b, c = parts
                g, G = n % 2, base + n

                def rotate(c4):
                    k = 2 * (c4 // 2)
                    dve.wait_ge(S["sq_done"], G * 4 + c4 + 1)
                    dve.wait_ge(S["add_done"], G * 4 + c4 - 1)
                    q = QB[c4 % 2][:, :].rearrange("p (h t d) -> p h t d", t=2, d=DH // 2)
                    cos = rot[:, k, bass.ds(w_a, 1), :]
                    sin = rot[:, k + 1, bass.ds(w_a, 1), :]
                    dve.tensor_tensor(t1[:, g, c4, :].rearrange("p (h d) -> p h d", d=DH), QB[c4 % 2][:, :].rearrange("p (h d) -> p h d", d=DH),
                                      cos.to_broadcast([P, 8, DH]), ALU.mult).then_inc(S["rot_done"], 1)
                    dve.tensor_tensor(t2[:, c4 % 2, :].rearrange("p (h t d) -> p h t d", t=2, d=DH // 2), q[:, :, ::-1, :],
                                      sin.rearrange("p w (t d) -> p w t d", t=2).to_broadcast([P, 8, 2, DH // 2]),
                                      ALU.mult).then_inc(S["rot_done"], 1)
                    dve.tensor_reduce(ss[:, g, 8 * c4:8 * c4 + 8], sq[:, c4 % 2, :].rearrange("p (h d) -> p h d", d=DH),
                                      AX.X, ALU.add).then_inc(S["ss_done"], 1)

                def guard(k):
                    dve.wait_ge(S["ss_done"], G * 4 + 2 * k + 2)
                    dve.wait_ge(S["nrm_pow"], G * 2 - 2)
                    dve.tensor_scalar(rn[:, g, 0, 16 * k:16 * k + 16], ss[:, g, 16 * k:16 * k + 16], 1e-24, None, ALU.max).then_inc(S["nrm_max"], 1)

                if a:
                    dve.wait_ge(S["qkt_done"], G * 4 - 4)
                    rotate(0)
                    rotate(1)
                    guard(0)
                if c:
                    Gc = G - 2
                    dve.wait_ge(S["rs_done"], Gc + 1)
                    dve.wait_ge(S["ot_done"], Gc * 2)
                    for k in range(2):
                        dve.wait_ge(S["pv_done"], Gc * 2 + k + 1)
                        dve.tensor_tensor(osb[:, 4 * k:4 * k + 4, :, :].rearrange("p m a d -> p (m a) d"),
                                          OB[k][:, :].rearrange("p (h d) -> p h d", d=DH),
                                          rs[:, g, 8 * k:8 * k + 8].unsqueeze(2).to_broadcast([P, 8, DH]), ALU.mult).then_inc(S["on_done"], 1)
                if a:
                    rotate(2)
                    rotate(3)
                    guard(1)
                    dve.wait_ge(S["nrm_pow"], G * 2 + 1)
                    dve.wait_ge(S["add_done"], G * 4 + 2)
                    t = t1[:, g, 0:2, :].rearrange("p c (h d) -> p (c h) d", d=DH)
                    dve.tensor_tensor(t, t, rn[:, g, 1, 0:16].unsqueeze(2).to_broadcast([P, 16, DH]), ALU.mult).then_inc(S["qn_done"], 1)
                if b:
                    Gb, gb = G - 1, 1 - g
                    dve.wait_ge(S["pt_done"], (Gb - 1) * 2)
                    for k in range(2):
                        dve.wait_ge(S["sc_done"], Gb * 2 + k + 1)
                        dve.tensor_reduce(mx[:, gb, 8 * k:8 * k + 8], SB[k][:, :].rearrange("p (h k) -> p h k", k=DH), AX.X, ALU.max).then_inc(S["mx_done"], 1)
                    for k in range(2):
                        dve.wait_ge(S["mx_done"], Gb * 2 + k + 1)
                        dve.tensor_tensor(pr[:, gb, 4 * k:4 * k + 4, :, :].rearrange("p m a k -> p (m a) k"),
                                          SB[k][:, :].rearrange("p (h k) -> p h k", k=DH),
                                          mx[:, gb, 8 * k:8 * k + 8].unsqueeze(2).to_broadcast([P, 8, DH]), ALU.subtract).then_inc(S["sub_done"], 1)
                if c and g == 1:
                    dve.wait_ge(S["y_done"], y_no + 2)
                    y = Y[:, :, bass.ds(w_c + 1, 1), :]
                    dve.tensor_tensor(y, OB[0][:, 0:2 * P].rearrange("p (g w c) -> p g w c", g=2, w=1), y, ALU.add).then_inc(S["y_add"], 1)
                if b:
                    dve.wait_ge(S["exp_done"], Gb * 2 + 2)
                    dve.tensor_reduce(sm[:, gb, :], pr[:, gb, :, :, :].rearrange("p m a k -> p (m a) k"), AX.X, ALU.add).then_inc(S["sum_done"], 1)
                    dve.wait_ge(S["sum_done"], Gb + 1)
                    dve.reciprocal(rs[:, gb, :], sm[:, gb, :]).then_inc(S["rs_done"], 1)

            def x_ready(xb):
                if xb == 0:
                    return lambda b: dve.wait_ge(S["xt_ev"], b + 1)
                return lambda b: dve.wait_ge(S["x_done"], xb)

            def ffn(q, N0, xb):
                if q == 0:
                    dve.wait_ge(S["int_ld"], 48)
                    for m in range(3):
                        dve.tensor_scalar(wqkv[:, HID * m:HID * m + HID], iraw[:, m, :], float(np.float32(1.0 / 127.0)), None, ALU.mult).then_inc(S["wi_cv"], 1)
                    for m in range(3):
                        dve.wait_ge(S["wi_done"], m + 1)
                        dve.tensor_copy(wi[:, m, :], FFB[m][:, 0:HID]).then_inc(S["wi_ev"], 1)
                norm(N0, lambda b: batch(b, X), x_ready(xb), lambda b: cen[:, b, :], None, "n_out")
                L = PASSES * DEPTH + q
                K = L * (BATCHES * 3) + CREDIT

                def join(b):
                    dve.wait_ge(S["f_done"], L * BATCHES + b + 1)
                    dve.scalar_tensor_tensor(batch(b, X), TB[b % 2][:, :], 0.5, batch(b, X), ALU.mult, ALU.add).then_inc(S["x_done"], 1)

                for i in range(3 * BATCHES):
                    b, c = divmod(i, 3)
                    dve.wait_ge(S["h_done"], L * (BATCHES * 6) + 2 * i + 2)
                    dve.wait_ge(S["gelu_done"], K + i + 1)
                    if c == 0 and b >= 2:
                        dve.wait_ge(S["f_done"], L * BATCHES + b - 1)
                    dve.tensor_tensor(hh[:, b % 2, c, :], FFB[(2 * i + 1) % 4][:, :], gl[:, i % 2, :], ALU.mult).then_inc(S["hm_done"], 1)
                    if c == 2 and b >= 1:
                        join(b - 1)
                join(BATCHES - 1)

            def attention(kind, N0, xb):
                dh = DHS[kind]
                units = UNITS[kind]
                if kind == DIFF:
                    dve.wait_ge(S["raw_ld"], 16 * 11)
                    dve.tensor_scalar(vec[:, 1:2], vec[:, 0:1], -1.0, None, ALU.mult).then_inc(S["vec_done"], 1)
                    dve.tensor_scalar(vec[:, 2:3], vec[:, 0:1], -1.0, 1.0, ALU.mult, ALU.add).then_inc(S["vec_done"], 1)
                    dve.wait_ge(S["vec_done"], 2)
                    dve.tensor_tensor(vec[:, 5:6], vec[:, 4:5], vec[:, 2:3], ALU.mult).then_inc(S["vec_done"], 1)
                    dve.wait_ge(S["vec_done"], 3)
                    dve.wait_ge(S["wt_done"], 1)
                    for k, dst in ((2, wv), (3, wot)):
                        dve.tensor_copy(dst, SB[0][:, P * k:P * k + P]).then_inc(S["wt_ev"], 1)
                dve.memset(rotf[:, 0:1024], 0.0).then_inc(S["wdup_done"], 1)
                dve.memset(vpad[:, :, :, :], 0.0).then_inc(S["wdup_done"], 1)
                dve.wait_ge(S["wdup_done"], 4 * kind + 2)
                for k, dst in ((0, wqp), (1, wkp)):
                    src = SB[0][:, P * k:P * k + P] if kind == DIFF else wraw[:, 4 + k, :]
                    dve.tensor_copy(dst[:, :, 0:8], src.rearrange("p (n d) -> p n d", d=8)).then_inc(S["wdup_done"], 1)
                norm(N0, lambda b: batch(b, X), x_ready(xb), lambda b: cen[:, b, :], None, "n_out")
                norms = (1 if kind == DIFF else 3)
                dve.wait_ge(S["n_out"], norms * BATCHES)
                ycen = cen[:, :, :].rearrange("p (g h) (w c) -> p g (h w) c", g=GROUPS, w=4)
                per = 32 // dh
                with dve.Fori(0, GROUPS) as gq, dve.Fori(0, QUADS) as jq:
                    s = gq * QUADS + jq
                    Q = s + (SEQS * kind + 1)
                    U = s * units + (SEQS * UNITS[0] * kind + UNITS[0])
                    dve.wait_ge(S["av_done"], Q)
                    dve.tensor_copy(ys.rearrange("p (w i) -> p w i", i=WIN),
                                    ycen[:, bass.ds(gq, 1), :, bass.ds(jq * WIN, WIN)].rearrange("p g w i -> p (g w) i")).then_inc(S["ys_done"], 1)
                    dve.wait_ge(S["av_done"], Q + 1)
                    dve.wait_ge(S["apv_done"], Q)
                    for h in range(per):
                        src = SB[0][:, 0:TOKENS].rearrange("p (t c h d) -> p t c h d", t=2, h=per, d=dh)
                        dst = vpad[:, :, 0:units, :].rearrange("p t (c h) d -> p t c h d", h=per)
                        o = dve.tensor_copy(dst[:, :, :, h, dh * h:dh * h + dh], src[:, :, :, h, :])
                    o.then_inc(S["av_ev"], 1)

                    def finish(i):
                        dve.wait_ge(S["ae_done"], Q * ROWS + i + 1)
                        dve.reciprocal(drc[:, 0, i, :], dsum[:, i, :]).then_inc(S["ac_done"], 1)
                        dve.wait_ge(S["ac_done"], Q * ROWS + i + 1)
                        u = i if kind else i // 2
                        if kind or i % 2 == 0:
                            if u >= 2:
                                dve.wait_ge(S["at_done"], U + u - 1)
                            for t in range(2):
                                o = dve.tensor_scalar(pn_ring[:, u % 2, t, :], pe_ring[:, i % 4, t, :], drc[:, 0, i, t:t + 1], None, ALU.mult)
                            o.then_inc(S["an_done" if kind else "an_half"], 1)
                        else:
                            dve.tensor_scalar(drc[:, 1, i, :], drc[:, 0, i, :], vec[:, 1:2], None, ALU.mult).then_inc(S["ad_done"], 1)
                            dve.wait_ge(S["ad_done"], U + u + 1)
                            dve.wait_ge(S["an_half"], U + u + 1)
                            for t in range(2):
                                o = dve.scalar_tensor_tensor(pn_ring[:, u % 2, t, :], pe_ring[:, i % 4, t, :], drc[:, 1, i, t:t + 1],
                                                             pn_ring[:, u % 2, t, :], ALU.mult, ALU.add)
                            o.then_inc(S["an_done"], 1)

                    for i in range(ROWS + 2):
                        if i < ROWS:
                            dve.wait_ge(S["as_done"], Q * ROWS + i + 1)
                            dve.tensor_reduce(nm[:, i, :], LNB[i % 4][:, :].rearrange("p (t k) -> p t k", t=2), AX.X, ALU.max, negate=True).then_inc(S["am_done"], 1)
                        if i >= 2:
                            finish(i - 2)
                    dve.wait_ge(S["apv_done"], Q + 1)
                    o = seq_cols(X, gq, jq)
                    if kind == DIFF:
                        dve.tensor_scalar(on, OB[0][:, 0:TOKENS], vec[:, 3:4], None, ALU.mult).then_inc(S["a_on"], 1)
                        dve.wait_ge(S["a_ss"], Q + 1)
                        dve.tensor_scalar(ave[:, :], OB[1][:, 0:2], float(np.finfo(np.float32).eps), None, ALU.add).then_inc(S["a_ve"], 1)
                        dve.wait_ge(S["a_rs"], Q + 1)
                        for t in range(2):
                            dve.tensor_scalar(odg[:, P * t:P * t + P], ident[:, :], ars[:, t:t + 1], None, ALU.mult).then_inc(S["a_dg"], 1)
                        dve.wait_ge(S["a_bc"], Q + 1)
                        dve.tensor_tensor(on2, on, OB[1][:, 0:TOKENS], ALU.mult).then_inc(S["a_on2"], 1)
                        dve.wait_ge(S["a_y"], Q + 1)
                        dve.tensor_scalar(ott, OB[0][:, 0:TOKENS], vec[:, 2:3], vec[:, 5:6], ALU.mult, ALU.add).then_inc(S["a_yt"], 1)
                        dve.wait_ge(S["a_yt"], Q + 1)
                        dve.tensor_tensor(o, ott.rearrange("p (w i) -> p w i", i=WIN), o, ALU.add).then_inc(S["x_done"], 1)
                    else:
                        dve.tensor_copy(on, OB[0][:, 0:TOKENS]).then_inc(S["a_on"], 1)
                        dve.wait_ge(S["a_y"], Q + 1)
                        dve.scalar_tensor_tensor(o, OB[0][:, 0:TOKENS].rearrange("p (w i) -> p w i", i=WIN), vec[:, 6:7], o, ALU.add, ALU.add).then_inc(S["x_done"], 1)

            def stack(p, N0, xb):
                norm(N0, lambda b: batch(b, X), x_ready(xb), lambda b: batch(b, Y), None, "y_ready")
                with dve.Fori(0, DEPTH) as l:
                    G, L, N = tile0(p, l), layer0(p, l), ln_no(p, l)
                    dve.wait_ge(S["tab_done"], L * 4 + 8)
                    dve.wait_ge(S["y_ready"], (L + p + 1) * BATCHES)
                    W = L * WINDOWS
                    for n in range(4):
                        attend(G, n, n // 2, (n - 2) // 2, W + (n - 2) // 2, (True, n >= 1, n >= 2))
                    with dve.Fori(1, WINDOWS // 2) as v:
                        for n in range(4):
                            wc = v * 2 + (n - 2) // 2
                            attend(G + v * 4, n, v * 2 + n // 2, wc, W + wc)
                    for n in range(2):
                        attend(G + TILES, n, 0, WINDOWS - 1, W + (WINDOWS - 1), (False, n == 0, True))
                    dve.wait_ge(S["y_add"], L * WINDOWS + (WINDOWS + 1))
                    for b in range(BATCHES):
                        gg, h = divmod(b, 2)
                        src = Y[:, gg, :, :].rearrange("p w (j i) -> p w j i", i=WIN)
                        own = src[:, 1 + 4 * h:5 + 4 * h]
                        bef = src[:, 4 * h:4 * h + 4]
                        dst = xs[:, b, :].rearrange("p (w j i) -> p w j i", j=QUADS, i=WIN)
                        dve.tensor_copy(dst[0:64], own[0:64]).then_inc(S["xs_done"], 1)
                        dve.tensor_copy(dst[64:P, :, :, 1:WIN], own[64:P, :, :, 0:WIN - 1]).then_inc(S["xs_done"], 1)
                        dve.tensor_copy(dst[64:P, :, :, 0:1], bef[64:P, :, :, WIN - 1:WIN]).then_inc(S["xs_done"], 1)
                    dve.wait_ge(S["ff_ld"], (L + 1) * 160)

                    def staged(b):
                        dve.wait_ge(S["xs_done"], L * 12 + 3 * b + 3)
                    norm(N, lambda b: xs[:, b, :], staged, lambda b: cen[:, b, :],
                         lambda b: L * BATCHES + b + 1, None)
                    K = L * (BATCHES * 3) + CREDIT

                    def join(b):
                        dve.wait_ge(S["f_done"], L * BATCHES + b + 1)
                        dve.scalar_tensor_tensor(batch(b, Y), TB[b % 2][:, :], lnp[:, 2:3], batch(b, Y), ALU.add, ALU.add).then_inc(S["y_ready"], 1)

                    for i in range(3 * BATCHES):
                        b, c = divmod(i, 3)
                        dve.wait_ge(S["h_done"], L * (BATCHES * 6) + 2 * i + 2)
                        dve.wait_ge(S["gelu_done"], K + i + 1)
                        if c == 0 and b >= 2:
                            dve.wait_ge(S["f_done"], L * BATCHES + b - 1)
                        r = slice(0, FFC[c])
                        dve.scalar_tensor_tensor(hh[r, b % 2, c, :], FFB[(2 * i + 1) % 4][r, :], b1[r, c:c + 1], gl[r, i % 2, :],
                                                 ALU.add, ALU.mult).then_inc(S["hm_done"], 1)
                        if c == 2 and b >= 1:
                            join(b - 1)
                    join(BATCHES - 1)
                for b in range(BATCHES):
                    dve.wait_ge(S["y_ready"], (DEPTH * (p + 1) + p) * BATCHES + b + 1)
                    dve.scalar_tensor_tensor(batch(b, X), batch(b, Y), 0.5, batch(b, X), ALU.mult, ALU.add).then_inc(S["x_done"], 1)

            run(stack, attention, ffn)


INPUTS = ["L0_attn_Wq", "L0_attn_Wk", "L0_attn_Wv", "L0_attn_norm_w", "L0_attn_Wo", "L0_attn_bo",
          "L0_attn_diff_weight", "L0_ffn_Wqkv", "L0_ffn_q_scale", "L0_ffn_k_scale", "L0_ffn_Wo", "L0_ffn_ln_g",
          "L0_ffn_ln_b", "L0_ffn_W1", "L0_ffn_b1", "L0_ffn_W2", "L0_ffn_b2", "L1_attn_Wk", "L1_attn_Wq",
          "L1_attn_Wo", "L1_attn_bo", "L1_ffn_w_gate", "L1_ffn_w_up", "L1_ffn_w_down"]


def build_program(nc, inputs, stop_after=99):
    fp32 = mybir.dt.float32
    arrays, aps = {}, {}
    for name in ["L0_attn_x"] + INPUTS:
        a = np.ascontiguousarray(inputs[name])
        if a.ndim == 0:
            a = a.reshape(1)
        arrays[name] = a
        aps[name] = nc.dram_tensor(name, a.shape, mybir.dt.from_np(a.dtype), kind="ExternalInput").ap()
    cst = []
    for name, a in zip(("rotary", "mask", "identity"), shape_constants()):
        arrays[name] = a
        cst.append(nc.dram_tensor(name, a.shape, fp32, kind="ExternalInput").ap())
    out = nc.dram_tensor("out", (SEQS, TOKENS, P), fp32, kind="ExternalOutput").ap()
    macaron(nc, aps["L0_attn_x"], aps, cst, out, stop_after)
    return arrays


def kernel(**inputs):
    import concourse.bacc as bacc
    from concourse.bass_utils import run_bass_kernel_spmd

    nc = bacc.Bacc("TRN2", target_bir_lowering=False, num_devices=1)
    arrays = build_program(nc, inputs)
    r = run_bass_kernel_spmd(nc, [arrays], core_ids=[0])
    return r.results[0]["out"]
```

```python
import numpy as np
from contextlib import ExitStack

import concourse.bass as bass
from concourse import mybir

P = 128
GROUPS, QUADS, WINDOWS, WIN = 2, 4, 8, 32
SEQS, TOKENS = GROUPS * QUADS, WINDOWS * WIN
TILES = GROUPS * WINDOWS
BATCH = 512
BATCHES = SEQS * TOKENS // BATCH
DEPTH, HEADS, DH = 6, 16, 64
PAIRS = HEADS // 2
INNER = HEADS * DH
FF = int(P * 4 * 2 / 3)
FFC = [128, 128, FF - 256]
QK_SCALE = 8.0
HID = 384
PASSES = 2
MASKED = -1e30


def shape_constants():
    half = np.arange(0, DH, 2, dtype=np.float32)
    inv_freq = (1.0 / 10000.0 ** (half / DH)).astype(np.float32)
    t = np.arange(TOKENS, dtype=np.float32)
    freqs = t[:, None] * inv_freq[None, :]
    freqs = np.concatenate([freqs, freqs], -1).astype(np.float64)
    base = ((half + np.float32(0.4 * DH)) / np.float32(1.4 * DH)).astype(np.float64)
    power = (t.astype(np.float64) - TOKENS // 2) / (WIN // 2)
    scale = base[None, :] ** power[:, None]
    scale = np.concatenate([scale, scale], -1)
    sign = np.where(np.arange(DH) < DH // 2, -1.0, 1.0)[None, :]
    cos, sin = np.cos(freqs), np.sin(freqs) * sign
    tabs = np.stack([cos * scale, sin * scale, cos / scale, sin / scale])
    tabs = tabs.reshape(4, WINDOWS, 1, WIN, DH)
    tabs = np.broadcast_to(tabs, (4, WINDOWS, QUADS, WIN, DH))
    tabs = tabs.reshape(4, WINDOWS, P, DH).transpose(2, 0, 1, 3)
    i = np.arange(P)[:, None] % WIN
    j = np.arange(WIN)[None, :]
    own, prev = np.where(j <= i, 0.0, MASKED), np.where(j >= i, 0.0, MASKED)
    none = np.full((P, WIN), MASKED)
    mask = np.stack([np.concatenate(x, 1) for x in ([own, none], [prev, own], [own, prev])], 1)
    return (np.ascontiguousarray(tabs, np.float32), np.ascontiguousarray(mask, np.float32),
            np.eye(P, dtype=np.float32))


def macaron(nc, x, w, cst, out):
    fp32, bf16, i32 = mybir.dt.float32, mybir.dt.bfloat16, mybir.dt.int32
    ALU, ACT, AX = mybir.AluOpType, mybir.ActivationFunctionType, mybir.AxisListType

    with ExitStack() as ctx:
        ctx.enter_context(nc.allow_non_contiguous_dma(reason="a layer's vectors, one element a partition"))

        def sb(name, shape, dt=fp32):
            return ctx.enter_context(nc.sbuf_tensor(name, shape, dt))

        def sem(name):
            return ctx.enter_context(nc.semaphore(name))

        X = sb("X", [P, GROUPS, WINDOWS + 1, P])
        Y = sb("Y", [P, GROUPS, WINDOWS + 1, P])
        ident = sb("ident", [P, P])
        ident_bf = sb("ident_bf", [P, P], bf16)
        ones = sb("ones", [P, P])
        mean_w = sb("mean_w", [P, P])
        mhalf = sb("mhalf", [P, 1])
        mask_bf = sb("mask_bf", [P, 3, DH], bf16)
        tabs = sb("tabs", [P, 4, WINDOWS, DH])
        wqkv = sb("wqkv", [P, 3 * INNER])
        wo = sb("wo", [P, PAIRS, P])
        w1 = sb("w1", [P, 2 * FF])
        w2 = sb("w2", [P, 3, P])
        b1 = sb("b1", [P, 6])
        lnp = sb("lnp", [P, 3])
        qks = sb("qks", [P, 2, DH])
        rot = sb("rot", [P, 4, WINDOWS, DH])
        xst = sb("xst", [P, 2, P])
        sq = sb("sq", [P, 2, BATCH])
        t1 = sb("t1", [P, 2, 4, BATCH])
        t2 = sb("t2", [P, 2, BATCH])
        ss = sb("ss", [P, 2, 32])
        rn = sb("rn", [P, 2, 2, 32])
        qT = sb("qT", [P, PAIRS, P])
        kT = [sb(f"kT{g}", [P, PAIRS, QUADS, 2, 2, WIN]) for g in range(2)]
        mx = sb("mx", [P, 2, HEADS])
        pr = sb("pr", [P, 2, PAIRS, 2, DH])
        sm = sb("sm", [P, 2, HEADS])
        rs = sb("rs", [P, 2, HEADS])
        pT = sb("pT", [P, PAIRS, P])
        vj = [sb(f"vj{g}", [P, QUADS, 2, BATCH]) for g in range(2)]
        osb = sb("osb", [P, PAIRS, 2, DH])
        oT = sb("oT", [P, PAIRS, 2, P])
        xs = sb("xs", [P, BATCHES, BATCH])
        vs = xs[:, :, :].rearrange("p (g a) n -> p g a n", g=2)
        cen = sb("cen", [P, BATCHES, BATCH])
        sqd = sb("sqd", [P, BATCHES, BATCH])
        ve = sb("ve", [P, TILES])
        rstd = sb("rstd", [P, TILES])

        wraw = sb("wraw", [P, 7, P])
        iraw = tabs[:, :, :, :].rearrange("p a w d -> p (a w d)")[:, 0:3 * HID].rearrange("p (m n) -> p m n", m=3).bitcast(i32)
        wi = vj[0][:, :, :, :].rearrange("p j a n -> p (j a n)")[:, 0:3 * HID].rearrange("p (m n) -> p m n", m=3)
        vec = sb("vec", [P, 8])
        t1f = t1[:, :, :, :].rearrange("p g c n -> p (g c) n")
        pe_ring = pr[:, :, :, :, :].rearrange("p g m a k -> p (g m a k)").rearrange("p (r t k) -> p r t k", r=4, k=TOKENS)
        pn_ring = t1f[:, 0:2, :].rearrange("p r (t k) -> p r t k", t=2)
        pnT = t1f[:, 2:4, :].rearrange("p r (t k) -> p r t k", t=2)
        qz = kT[0][:, :, :, :, :, :].rearrange("p m j a s k -> p (m j a s k)").rearrange("p (r a k) -> p r a k", r=4, a=4)
        kp = t1f[:, 6:8, :].rearrange("p c (r k) -> p (c r) k", k=TOKENS)
        vpad = osb[:, :, :, :].rearrange("p m a d -> p (m a d)").rearrange("p (t h d) -> p t h d", t=2, d=32)
        oTf = oT[:, :, :, :].rearrange("p m g c -> p (m g c)").rearrange("p (n k) -> p n k", k=TOKENS)
        ys, on, osq, on2, odg, ott = (oTf[:, k, :] for k in range(6))
        rotf = rot[:, :, :, :].rearrange("p a w d -> p (a w d)")
        wqp, wkp = (rotf[:, 512 * k:512 * k + 512].rearrange("p (n d) -> p n d", d=32) for k in range(2))
        wv, wot = (rotf[:, 1024 + P * k:1152 + P * k] for k in range(2))
        nm = sb("nm", [P, HEADS, 2])
        dsum = sb("dsum", [P, HEADS, 2])
        drc = sb("drc", [P, 2, HEADS, 2])
        ave = sb("ave", [P, 2])
        ars = sb("ars", [P, 2])

        gl = sq
        hh = t1[:, :, 0:3, :]

        QB = [ctx.enter_context(nc.psum_tensor(f"QB{i}", [P, BATCH], fp32)) for i in range(2)]
        TB = [ctx.enter_context(nc.psum_tensor(f"TB{i}", [P, BATCH], fp32)) for i in range(2)]
        SB = [ctx.enter_context(nc.psum_tensor(f"SB{i}", [P, BATCH], fp32)) for i in range(2)]
        OB = [ctx.enter_context(nc.psum_tensor(f"OB{i}", [P, BATCH], fp32)) for i in range(2)]
        LNB = [QB[0], QB[1], TB[0], TB[1]]
        FFB = [SB[0], SB[1], OB[0], OB[1]]

        names = """cst_ld cst_done mask_done ln_xn x_ld xt_done xt_ev
            ln_mean ln_cen ln_sqd ln_ss ln_ve ln_rs ln_dg ln_bc ln_out
            wqkv_ld wo_ld ff_ld qs_ld tab_done xst_done
            qkv_done sq_done ss_done rot_done add_done nrm_max nrm_pow qn_done kn_done v_done vj_ld0 vj_ld1
            qkt_done qkt_ev sc_done mx_done sub_done exp_done sum_done rs_done
            pt_done pt_ev pv_done on_done ot_done ot_ev y_done y_add
            xs_done h_done gelu_done hm_done f_done y_ready x_done
            raw_ld int_ld vec_done wt_done wt_ev wdup_done wi_cv wi_done wi_ev n_out
            ys_done aqk_done aqk_ev aq_ev av_done av_ev as_done am_done ae_done ac_done ad_done an_half an_done at_done at_ev apv_done
            a_on a_sq a_ss a_ve a_rs a_dg a_bc a_on2 a_y a_yt
            on_T on_ev out_st""".split()
        S = {n: sem(n) for n in names}

        def batch(b, t):
            h, g = divmod(b, 2)
            return t[:, g, 1 + 4 * h:5 + 4 * h, :].rearrange("p w c -> p (w c)")

        def natural(ap):
            return [ap[s].rearrange("(w i) e -> i w e", i=WIN) for s in range(SEQS)]

        PHASES = [("stack", 0), ("attend", 0), ("stack", 1), ("ffn", 0), ("attend", 1), ("ffn", 1)]
        X_BEFORE = [0, 4, 12, 16, 20, 28, 32]
        NORM_NO = [0, 1 + DEPTH, 2 + DEPTH, 3 + 2 * DEPTH, 4 + 2 * DEPTH, 5 + 2 * DEPTH]

        def run(stack, attention, ffn):
            for k, (kind, p) in enumerate(PHASES):
                {"stack": stack, "attend": attention, "ffn": ffn}[kind](p, NORM_NO[k], X_BEFORE[k])

        X_TOTAL = X_BEFORE[-1]

        DIFF = 0
        DHS = [16, 8]
        QS = [8.0 ** -0.5, float(P) ** -0.5]
        UNITS = [8, 16]
        ROWS = 16

        def unit_ready(kind, i):
            if not 0 <= i < ROWS:
                return None
            return i if kind else (i // 2 if i % 2 else None)

        def seq_cols(t, gq, jq):
            return t[:, bass.ds(gq, 1), 1:1 + WINDOWS, bass.ds(jq * WIN, WIN)].rearrange("p g w i -> p (g w) i")

        nat = xs[:, :, :].rearrange("p b (t e) -> p (b t) e", e=P)

        def nat_tile(b, t):
            return b % 2 * WINDOWS + b // 2 * 4 + t

        block = ctx.enter_context(nc.Block())

        CREDIT = 2

        def tile0(p, l):
            return l * TILES + (CREDIT + p * DEPTH * TILES)

        def layer0(p, l):
            return l + p * DEPTH

        def ln_no(p, l):
            return l + ((DEPTH + 2) * p + 1)

        @block.sync
        def _(sp):
            sp.sem_inc(S["vj_ld0"], 128)
            sp.sem_inc(S["vj_ld1"], 128)
            for k, (dst, src) in enumerate(((tabs[:, :, :, :], cst[0]), (ident[:, :], cst[2]))):
                sp.dma_start(dst, src).then_inc(S["cst_ld"], 16)
            sp.dma_start(xs[:, 3, 0:3 * DH], cst[1].rearrange("p a b -> p (a b)")).then_inc(S["cst_ld"], 16)
            sp.wait_ge(S["mask_done"], 1)
            for s, src in enumerate(natural(x)):
                g, j = divmod(s, QUADS)
                sp.dma_start(nat[32 * j:32 * j + 32, g * WINDOWS:(g + 1) * WINDOWS, :], src).then_inc(S["x_ld"], 16)

            for k, n in enumerate(("L0_attn_Wq", "L0_attn_Wk", "L0_attn_Wv", "L0_attn_Wo", "L1_attn_Wq", "L1_attn_Wk", "L1_attn_Wo")):
                sp.dma_start(wraw[:, k, :], w[n]).then_inc(S["raw_ld"], 16)
            for k, src in ((0, w["L0_attn_diff_weight"].unsqueeze(0).to_broadcast([P, 1])),
                           (3, w["L0_attn_norm_w"].rearrange("h (d o) -> (h d) o", o=1)),
                           (4, w["L0_attn_bo"].rearrange("(p o) -> p o", o=1)), (6, w["L1_attn_bo"].rearrange("(p o) -> p o", o=1))):
                sp.dma_start(vec[:, k:k + 1], src).then_inc(S["raw_ld"], 16)

            def stack(p, N0, xb):
                with sp.Fori(0, DEPTH) as l:
                    G, L = tile0(p, l), layer0(p, l)
                    sp.wait_ge(S["qkv_done"], G * 6)
                    sp.dma_start(wqkv[:, :], w["L0_ffn_Wqkv"][bass.ds(l, 1), :, :].rearrange("a p n -> p (a n)"),
                                 max_dma_last_dim=16384).then_inc(S["wqkv_ld"], 16)
                    sp.wait_ge(S["tab_done"], L * 4 + 4)
                    for k, n in enumerate(("L0_ffn_q_scale", "L0_ffn_k_scale")):
                        sp.dma_start(qks[:, k, :], w[n][bass.ds(l, 1), :].to_broadcast([P, DH])).then_inc(S["qs_ld"], 16)
                    sp.wait_ge(S["y_done"], L * WINDOWS + 1)
                    sp.dma_start(wo[:, :, :], w["L0_ffn_Wo"][bass.ds(l, 1), :, :].rearrange("a (m p) n -> p (a m) n", p=P)).then_inc(S["wo_ld"], 16)
                    sp.wait_ge(S["y_ready"], (L + (p + 1)) * BATCHES)
                    sp.dma_start(w1[:, :], w["L0_ffn_W1"][bass.ds(l, 1), :, :].rearrange("a p n -> p (a n)")).then_inc(S["ff_ld"], 16)
                    sp.dma_start(w2[:, 0:2, :], w["L0_ffn_W2"][bass.ds(l, 1), 0:256, :].rearrange("a (m p) n -> p (a m) n", p=P)).then_inc(S["ff_ld"], 16)
                    sp.dma_start(w2[0:FFC[2], 2, :], w["L0_ffn_W2"][bass.ds(l, 1), 256:FF, :].rearrange("a p n -> p (a n)")).then_inc(S["ff_ld"], 16)
                    for half in range(2):
                        o = half * FF
                        sp.dma_start(b1[:, 3 * half:3 * half + 2], w["L0_ffn_b1"][bass.ds(l, 1), o:o + 256].rearrange("a (m p) -> p (a m)", p=P)).then_inc(S["ff_ld"], 16)
                        sp.dma_start(b1[0:FFC[2], 3 * half + 2:3 * half + 3], w["L0_ffn_b1"][bass.ds(l, 1), o + 256:o + FF].rearrange("a p -> p a")).then_inc(S["ff_ld"], 16)
                    for k, n in enumerate(("L0_ffn_ln_g", "L0_ffn_ln_b", "L0_ffn_b2")):
                        sp.dma_start(lnp[:, k:k + 1], w[n][bass.ds(l, 1), :].rearrange("a p -> p a")).then_inc(S["ff_ld"], 16)

                    def spread(G, w_par, g):
                        sp.wait_ge(S["v_done"], G * 2 + 2)
                        for j in range(QUADS):
                            for h2 in range(2):
                                sp.dma_start(vj[g][64 * h2 + 32 * w_par:64 * h2 + 32 * w_par + 32, j, h2, :],
                                             vs[32 * j:32 * j + 32, g, h2, :]).then_inc(S[f"vj_ld{g}"], 16)

                    with sp.Fori(0, WINDOWS // 2) as wp:
                        for k in range(4):
                            spread(G + wp * 4 + k, k // 2, k % 2)

            run(stack, lambda *a: None, lambda *a: None)
            sp.wait_ge(S["tab_done"], 4 * DEPTH * PASSES + 4)
            for k, n in enumerate(("L1_ffn_w_gate", "L1_ffn_w_up")):
                sp.dma_start(iraw[:, k, :].rearrange("p (c d) -> p c d", d=P), w[n].rearrange("(c p) d -> p c d", p=P)).then_inc(S["int_ld"], 16)
            sp.dma_start(iraw[:, 2, :], w["L1_ffn_w_down"]).then_inc(S["int_ld"], 16)
            sp.wait_ge(S["on_ev"], 4)
            for s, dst in enumerate(natural(out)):
                g, j = divmod(s, QUADS)
                sp.dma_start(dst, nat[32 * j:32 * j + 32, g * WINDOWS:(g + 1) * WINDOWS, :]).then_inc(S["out_st"], 16)
            sp.wait_ge(S["out_st"], 16 * SEQS)

        @block.gpsimd
        def _(gp):
            gp.memset(ones[:, :], 1.0).then_inc(S["cst_done"], 1)

            gp.wait_ge(S["cst_done"], 5)

            def power(N):
                for h in range(2):
                    gp.wait_ge(S["ln_ve"], N * 2 + h + 1)
                    gp.tensor_tensor(rstd[:, 8 * h:8 * h + 8], ve[:, 8 * h:8 * h + 8], mhalf[:, 0:1].to_broadcast([P, 8]), ALU.pow).then_inc(S["ln_rs"], 1)

            def project(G, g):
                for k in range(2):
                    for c in (2 * k, 2 * k + 1):
                        gp.wait_ge(S["rot_done"], G * 8 + 2 * c + 2)
                        gp.tensor_tensor(t1[:, g, c, :], t1[:, g, c, :], t2[:, c % 2, :], ALU.add).then_inc(S["add_done"], 1)
                    gp.wait_ge(S["nrm_max"], G * 2 + k + 1)
                    if k == 0:
                        gp.wait_ge(S["qn_done"], G - 1)
                    else:
                        gp.wait_ge(S["kn_done"], G - 1)
                    gp.tensor_tensor(rn[:, g, 1, 16 * k:16 * k + 16], rn[:, g, 0, 16 * k:16 * k + 16],
                                     mhalf[:, 0:1].to_broadcast([P, 16]), ALU.pow).then_inc(S["nrm_pow"], 1)
                gp.wait_ge(S["nrm_pow"], G * 2 + 2)
                gp.wait_ge(S["add_done"], G * 4 + 4)
                t = t1[:, g, 2:4, :].rearrange("p c (h d) -> p (c h) d", d=DH)
                r = rn[:, g, 1, 16:32].unsqueeze(2).to_broadcast([P, 16, DH])
                gp.tensor_tensor(t, t, r, ALU.mult).then_inc(S["kn_done"], 1)

            gp.sem_inc(S["nrm_pow"], 2 * CREDIT)
            gp.sem_inc(S["tab_done"], 4)
            gp.sem_inc(S["a_rs"], 1)
            gp.sem_inc(S["add_done"], 4 * CREDIT)
            gp.sem_inc(S["kn_done"], CREDIT)

            def attention(kind, N0, xb):
                power(N0)
                if kind == DIFF:
                    with gp.Fori(0, SEQS) as q:
                        gp.wait_ge(S["a_ve"], q + 2)
                        gp.tensor_tensor(ars[:, :], ave[:, :], mhalf[:, 0:1].to_broadcast([P, 2]), ALU.pow).then_inc(S["a_rs"], 1)

            def ffn(q, N0, xb):
                power(N0)

            def stack(p, N0, xb):
                power(N0)
                with gp.Fori(0, DEPTH) as l:
                    G, L = tile0(p, l), layer0(p, l)
                    gp.wait_ge(S["qs_ld"], L * 32 + 32)
                    gp.wait_ge(S["rot_done"], G * 8)
                    gp.wait_ge(S["cst_ld"], 48)
                    for k in range(4):
                        s = qks[:, k // 2, :].rearrange("p (w t d) -> p w t d", w=1, t=2)
                        if k % 2:
                            s = s[:, :, ::-1, :]
                        gp.tensor_tensor(rot[:, k, :, :].rearrange("p w (t d) -> p w t d", t=2),
                                         tabs[:, k, :, :].rearrange("p w (t d) -> p w t d", t=2),
                                         s.to_broadcast([P, WINDOWS, 2, DH // 2]), ALU.mult).then_inc(S["tab_done"], 1)
                    with gp.Fori(0, WINDOWS) as v:
                        for g in range(2):
                            project(G + v * 2 + g, g)
                    power(ln_no(p, l))

            run(stack, attention, ffn)

        @block.tensor
        def _(pe):
            for n, k in (("qkv_done", 6), ("qkt_done", 4), ("sc_done", 2), ("pt_done", 2), ("pv_done", 2), ("ot_done", 2)):
                pe.sem_inc(S[n], k * CREDIT)
            for n, k in (("y_done", 1), ("aqk_done", 4), ("av_done", 1), ("as_done", ROWS), ("at_done", UNITS[0]), ("apv_done", 1),
                         ("a_ss", 1), ("a_bc", 1), ("a_y", 1)):
                pe.sem_inc(S[n], k)
            pe.wait_ge(S["cst_ld"], 48)
            pe.wait_ge(S["cst_done"], 5)
            pe.wait_ge(S["mask_done"], 1)
            pe.wait_ge(S["x_ld"], 16 * SEQS)

            def to_features():
                for b in range(BATCHES):
                    for t in range(4):
                        last = pe.transpose(LNB[b][:, P * t:P * t + P], nat[:, nat_tile(b, t), :], ident[:, :])
                    last.then_inc(S["xt_done"], 1)

            def means(N, h, src, ready):
                for b in (2 * h, 2 * h + 1):
                    ready(b)
                    pe.matmul(LNB[b][:, :], mean_w[:, :], src(b), start=True, stop=True).then_inc(S["ln_mean"], 1)

            def variances(N, h):
                for b in (2 * h, 2 * h + 1):
                    pe.wait_ge(S["ln_sqd"], N * BATCHES + b + 1)
                    for t in range(4):
                        last = pe.matmul(LNB[2 * h][:, 4 * (b % 2) + t:4 * (b % 2) + t + 1], sqd[:, b, P * t:P * t + P], mean_w[:, 0:1],
                                         start=(b % 2 == 0 and t == 0), stop=True, skip_group_check=True)
                    last.then_inc(S["ln_ss"], 1)

            def spread(N, h):
                for b in (2 * h, 2 * h + 1):
                    pe.wait_ge(S["ln_dg"], N * BATCHES + b + 1)
                    pe.matmul(LNB[b][:, :], ones[:, :], sqd[:, b, :], start=True, stop=True).then_inc(S["ln_bc"], 1)

            def norm(N, src, ready):
                for h in range(2):
                    means(N, h, src, ready)
                for h in range(2):
                    variances(N, h)
                for h in range(2):
                    spread(N, h)

            def qkv(G, g, chunks, y_no=None):
                for c in chunks:
                    if c < 2:
                        pe.wait_ge(S["v_done"], G * 2 - 1 + c)
                        if y_no is not None:
                            pe.wait_ge(S["y_ready"], y_no + c)
                    else:
                        pe.wait_ge(S["rot_done"], G * 8 + 2 * c - 2)
                    pe.matmul(QB[c % 2][:, :], xst[:, g, :], wqkv[:, BATCH * c:BATCH * c + BATCH],
                              start=True, stop=True).then_inc(S["qkv_done"], 1)

            def transposes(src, free, done):
                for k in range(2):
                    free(k)
                    for m in range(4):
                        last = pe.transpose(TB[k][:, P * m:P * m + P], src(4 * k + m), ident[:, :])
                    last.then_inc(S[done], 1)

            def q_transposes(G, g):
                pe.wait_ge(S["qn_done"], G + 1)
                transposes(lambda m: t1[:, g, m // 4, P * (m % 4):P * (m % 4) + P],
                           lambda k: pe.wait_ge(S["pt_ev"], G * 2 - 1 + k), "qkt_done")

            def k_transposes(G, g):
                pe.wait_ge(S["kn_done"], G + 1)
                transposes(lambda m: t1[:, g, 2 + m // 4, P * (m % 4):P * (m % 4) + P],
                           lambda k: pe.wait_ge(S["qkt_ev"], G * 6 + k + 1), "qkt_done")

            def scores(G, g, mask):
                pe.wait_ge(S["sub_done"], G * 2)
                for k in range(2):
                    if k:
                        pe.wait_ge(S["qkt_ev"], G * 6 + 6)
                    pe.matmul(SB[k][:, :].rearrange("p (m k) -> p m k", k=DH), ident_bf[:, :],
                              mask_bf[:, mask:mask + 1, :].to_broadcast([P, 8, DH]), start=True, stop=True)
                for m in range(PAIRS):
                    for j in range(QUADS):
                        last = pe.matmul(SB[m // 4][32 * j:32 * j + 32, P * (m % 4):P * (m % 4) + P],
                                         qT[:, m, 32 * j:32 * j + 32],
                                         kT[g][:, m, j, :, :, :].rearrange("p a s k -> p (a s k)"),
                                         start=False, stop=True, skip_group_check=True)
                    if m % 4 == 3:
                        last.then_inc(S["sc_done"], 1)

            def p_transposes(G, g):
                def free(k):
                    pe.wait_ge(S["exp_done"], G * 2 + k + 1)
                    pe.wait_ge(S["ot_ev"], G * 2 - 1 + k)
                transposes(lambda m: pr[:, g, m, :, :].rearrange("p a b -> p (a b)"), free, "pt_done")

            def values(G, g, v_no, y_no, k):
                if k == 0:
                    pe.wait_ge(S["y_add"], y_no)
                    pe.wait_ge(S[f"vj_ld{g}"], v_no * 128)
                    pe.wait_ge(S["pt_ev"], G * 2 + 2)
                pe.wait_ge(S["on_done"], G * 2 - 1 + k)
                for m in range(4 * k, 4 * k + 4):
                    for j in range(QUADS):
                        last = pe.matmul(OB[m // 4][32 * j:32 * j + 32, P * (m % 4):P * (m % 4) + P],
                                         pT[:, m, 32 * j:32 * j + 32], vj[g][:, j, :, DH * m:DH * m + DH],
                                         start=True, stop=True, skip_group_check=True)
                    if m % 4 == 3:
                        last.then_inc(S["pv_done"], 1)

            def o_transposes(G, b):
                def free(k):
                    pe.wait_ge(S["on_done"], G * 2 + k + 1)
                    if b:
                        pe.wait_ge(S["qkt_ev"], G * 6 + 10 + 2 * k)
                transposes(lambda m: osb[:, m, :, :].rearrange("p a b -> p (a b)"), free, "ot_done")

            def output(G):
                pe.wait_ge(S["ot_ev"], G * 2 + 2)
                for m in range(PAIRS):
                    last = pe.matmul(OB[0][:, 0:2 * P], wo[:, m, :], oT[:, m, :, :].rearrange("p g c -> p (g c)"),
                                     start=(m == 0), stop=(m == PAIRS - 1))
                last.then_inc(S["y_done"], 1)

            def attend(base, L, W, n, p, parts=(True, True, True), beside=None):
                a, b, c = parts
                g = n % 2
                G = base + n
                if a:
                    if n == 0:
                        pe.wait_ge(S["wqkv_ld"], L * 16 + 16)
                    pe.wait_ge(S["xst_done"], G * 3 + 3)
                    qkv(G, g, (0, 1), (L + p) * BATCHES + 3 if n == 0 else None)
                if c and g == 0 and n > 2:
                    pe.wait_ge(S["wo_ld"], L * 16 + 16)
                    output(G - 3)
                if c:
                    p_transposes(G - 2, g)
                if a and g == 0:
                    qkv(G, g, (2,))
                if b:
                    q_transposes(G - 1, 1 - g)
                if a and g == 1:
                    qkv(G, g, (2,))
                if c:
                    values(G - 2, g, W + (n - 2) // 2 + 2, W + (n - 2) // 2 + 1, 0)
                if b:
                    k_transposes(G - 1, 1 - g)
                if c:
                    values(G - 2, g, W + (n - 2) // 2 + 2, W + (n - 2) // 2 + 1, 1)
                if beside:
                    beside()
                if a:
                    qkv(G, g, (3,))
                if c:
                    o_transposes(G - 2, b)
                if b:
                    mask = 0 if n < 3 else (1 if (n - 1) // 2 % 2 else 2)
                    scores(G - 1, 1 - g, mask)
                if g == 1 and not a:
                    output(G - 2)
                if a:
                    qkv(G, g, (4, 5))

            def feed_forward(p, L, N, staged):
                pe.wait_ge(S["ff_ld"], (L + 1) * 160)
                K = L * (BATCHES * 3) + CREDIT

                def up(b, chunks=range(6)):
                    pe.wait_ge(S["ln_out"], L * BATCHES + b + 1)
                    for k in chunks:
                        i, c = 6 * b + k, k // 2
                        pe.wait_ge(S["hm_done" if k % 2 else "gelu_done"], K + (i // 2 - 2 + 1))
                        col = P * c + (0 if k % 2 else FF)
                        pe.matmul(FFB[i % 4][0:FFC[c], :], w1[:, col:col + FFC[c]], cen[:, b, :],
                                  start=True, stop=True).then_inc(S["h_done"], 1)

                def down(b):
                    pe.wait_ge(S["hm_done"], K + 3 * b + 3)
                    if b >= 2:
                        pe.wait_ge(S["y_ready"], (L + p + 1) * BATCHES + b - 1)
                    for c in range(3):
                        last = pe.matmul(QB[b % 2][:, :], w2[0:FFC[c], c, :], hh[0:FFC[c], b % 2, c, :],
                                         start=(c == 0), stop=(c == 2))
                    last.then_inc(S["f_done"], 1)

                up(0)
                means(N, 1, lambda b: xs[:, b, :], staged)
                up(1, range(2))
                variances(N, 1)
                up(1, range(2, 6))
                down(0)
                down(1)
                spread(N, 1)
                up(2)
                up(3)
                down(2)
                down(3)

            def x_ready(xb):
                if xb == 0:
                    return lambda b: pe.wait_ge(S["xt_ev"], b + 1)
                return lambda b: pe.wait_ge(S["x_done"], xb)

            def ffn(q, N0, xb):
                if q == 0:
                    pe.wait_ge(S["wi_cv"], 3)
                    for m in range(3):
                        for c in range(3):
                            last = pe.transpose(FFB[m][:, P * c:P * c + P], wqkv[:, HID * m + P * c:HID * m + P * c + P], ident[:, :])
                        last.then_inc(S["wi_done"], 1)
                    pe.wait_ge(S["wi_ev"], 3)
                norm(N0, lambda b: batch(b, X), x_ready(xb))
                L = PASSES * DEPTH + q
                K = L * (BATCHES * 3) + CREDIT

                def up(b):
                    pe.wait_ge(S["n_out"], (1 + 2 * q) * BATCHES + b + 1)
                    for k in range(6):
                        i, c = 6 * b + k, k // 2
                        pe.wait_ge(S["hm_done" if k % 2 else "gelu_done"], K + (i // 2 - 2 + 1))
                        pe.matmul(FFB[i % 4][:, :], wi[:, k % 2, P * c:P * c + P], cen[:, b, :], start=True, stop=True).then_inc(S["h_done"], 1)

                def down(b):
                    pe.wait_ge(S["hm_done"], K + 3 * b + 3)
                    pe.wait_ge(S["n_out"], (1 + 2 * q) * BATCHES + BATCHES)
                    if b >= 2:
                        pe.wait_ge(S["x_done"], xb + b - 1)
                    for c in range(3):
                        last = pe.matmul(TB[b % 2][:, :], wi[:, 2, P * c:P * c + P], hh[:, b % 2, c, :], start=(c == 0), stop=(c == 2))
                    last.then_inc(S["f_done"], 1)

                up(0)
                for b in range(1, BATCHES):
                    up(b)
                    down(b - 1)
                down(BATCHES - 1)

            def attention(kind, N0, xb):
                if kind == DIFF:
                    pe.wait_ge(S["raw_ld"], 16 * 11)
                    for k in range(4):
                        last = pe.transpose(SB[0][:, P * k:P * k + P], wraw[:, k, :], ident[:, :])
                    last.then_inc(S["wt_done"], 1)
                    pe.wait_ge(S["wt_ev"], 2)
                pe.wait_ge(S["wdup_done"], 5 * kind + 5)
                norm(N0, lambda b: batch(b, X), x_ready(xb))
                wvv = wv if kind == DIFF else wraw[:, 5, :]
                woo = wot if kind == DIFF else wraw[:, 6, :]
                dh = DHS[kind]
                per = 32 // dh
                units = UNITS[kind]
                with pe.Fori(0, SEQS) as s:
                    Q = s + (SEQS * kind + 1)
                    U = s * units + (SEQS * UNITS[0] * kind + UNITS[0])
                    pe.wait_ge(S["ys_done"], Q + 1)
                    pe.wait_ge(S["ae_done"], Q * ROWS)
                    for k, wp in enumerate((wqp, wkp)):
                        for h in range(2):
                            for r_ in range(2):
                                c = 4 * (2 * h + r_)
                                last = pe.matmul(LNB[2 * k + h][:, TOKENS * r_:TOKENS * r_ + TOKENS],
                                                 wp[:, c:c + 4, :].rearrange("p n d -> p (n d)"), ys, start=True, stop=True, skip_group_check=True)
                            last.then_inc(S["aqk_done"], 1)
                    pe.wait_ge(S["at_ev"], U)
                    for t in range(2):
                        last = pe.matmul(SB[0][:, P * t:P * t + P], ys[:, P * t:P * t + P], wvv, start=True, stop=True, skip_group_check=True)
                    last.then_inc(S["av_done"], 1)
                    pe.wait_ge(S["aqk_ev"], Q * 6 + 6)
                    pe.wait_ge(S["aq_ev"], Q * 4 + 4)
                    for i in range(ROWS + 5):
                        if i < ROWS:
                            a, r_ = i % 4, i // 4
                            if i >= 4:
                                pe.wait_ge(S["ae_done"], Q * ROWS + i - 3)
                            for t in range(2):
                                last = pe.matmul(LNB[a][:, TOKENS * t:TOKENS * t + TOKENS],
                                                 qz[:, r_, a, P * t:P * t + P], kp[:, r_, :],
                                                 start=True, stop=True, skip_group_check=True)
                            last.then_inc(S["as_done"], 1)
                        u = unit_ready(kind, i - 5)
                        if u is not None:
                            if u == 0:
                                pe.wait_ge(S["x_done"], xb + s)
                            pe.wait_ge(S["at_ev"], U + u + 1)
                            c = 32 * (u // per)
                            for kb in range(2):
                                pv = pe.matmul(OB[0][c:c + 32, 0:TOKENS], vpad[:, kb, u, :], pnT[:, u % 2, kb, :],
                                                 start=(u % per == 0 and kb == 0), stop=(u % per == per - 1 and kb == 1))
                        u = unit_ready(kind, i - 3)
                        if u is not None:
                            pe.wait_ge(S["an_done"], U + u + 1)
                            if u < 2:
                                pe.wait_ge(S["av_ev"], Q + 1)
                            else:
                                pe.wait_ge(S["at_ev"], U + u - 1)
                            for kb in range(2):
                                for t in range(2):
                                    last = pe.transpose(SB[u % 2][:, TOKENS * kb + P * t:TOKENS * kb + P * t + P],
                                                        pn_ring[:, u % 2, t, P * kb:P * kb + P], ident[:, :])
                            last.then_inc(S["at_done"], 1)
                    pv.then_inc(S["apv_done"], 1)
                    if kind == DIFF:
                        pe.wait_ge(S["a_sq"], Q + 1)
                        for t in range(2):
                            last = pe.matmul(OB[1][:, t:t + 1], osq[:, P * t:P * t + P], mean_w[:, 0:1], start=(t == 0), stop=True, skip_group_check=True)
                        last.then_inc(S["a_ss"], 1)
                        pe.wait_ge(S["a_dg"], Q * 2 + 2)
                        pe.matmul(OB[1][:, 0:TOKENS], ones[:, :], odg, start=True, stop=True).then_inc(S["a_bc"], 1)
                        pe.wait_ge(S["a_on2"], Q + 1)
                        pe.matmul(OB[0][:, 0:TOKENS], woo, on2, start=True, stop=True).then_inc(S["a_y"], 1)
                    else:
                        pe.wait_ge(S["a_on"], Q + 1)
                        pe.matmul(OB[0][:, 0:TOKENS], woo, on, start=True, stop=True).then_inc(S["a_y"], 1)

            def stack(p, N0, xb):
                norm(N0, lambda b: batch(b, X), x_ready(xb))
                with pe.Fori(0, DEPTH) as l:
                    G, L, N = tile0(p, l), layer0(p, l), ln_no(p, l)
                    W = L * WINDOWS
                    for n in range(3):
                        attend(G, L, W, n, p, (True, n >= 1, n >= 2))
                    with pe.Fori(0, 3) as v:
                        for n in range(3, 7):
                            attend(G + v * 4, L, W + v * 2, n, p)
                    attend(G, L, W, 15, p)
                    attend(G, L, W, 16, p, (False, True, True))

                    def staged(b):
                        pe.wait_ge(S["xs_done"], L * 12 + 3 * b + 3)
                    means(N, 0, lambda b: xs[:, b, :], staged)
                    attend(G, L, W, 17, p, (False, False, True), lambda: variances(N, 0))
                    spread(N, 0)
                    feed_forward(p, L, N, staged)

            to_features()
            run(stack, attention, ffn)

            def to_tokens():
                for b in range(BATCHES):
                    pe.wait_ge(S["x_done"], X_TOTAL)
                    for t in range(4):
                        last = pe.transpose(LNB[b][:, P * t:P * t + P], batch(b, X)[:, P * t:P * t + P], ident[:, :])
                    last.then_inc(S["on_T"], 1)
            to_tokens()

        @block.scalar
        def _(act):
            act.sem_inc(S["sq_done"], 4 * CREDIT)
            act.sem_inc(S["xst_done"], 3 * CREDIT)
            act.sem_inc(S["v_done"], 2 * CREDIT)
            act.sem_inc(S["qkt_ev"], 6 * CREDIT)
            act.sem_inc(S["exp_done"], 2 * CREDIT)
            act.sem_inc(S["pt_ev"], 2 * CREDIT)
            act.sem_inc(S["ot_ev"], 2 * CREDIT)
            act.sem_inc(S["gelu_done"], CREDIT)
            for n, k in (("aqk_ev", 6), ("ae_done", ROWS), ("at_ev", UNITS[0]), ("a_sq", 1)):
                act.sem_inc(S[n], k)
            for b in range(BATCHES):
                act.wait_ge(S["xt_done"], b + 1)
                act.activation(batch(b, X), LNB[b][:, :], ACT.Copy).then_inc(S["xt_ev"], 1)

            def squares(N, halves=(0, 1)):
                for h in halves:
                    for b in (2 * h, 2 * h + 1):
                        act.wait_ge(S["ln_cen"], N * BATCHES + b + 1)
                        act.activation(sqd[:, b, :], cen[:, b, :], ACT.Square).then_inc(S["ln_sqd"], 1)

            def stage(G, wx, g):
                act.wait_ge(S["qkv_done"], (G - 1) * 6)
                yt = Y[:, g, bass.ds(wx, 2), :].rearrange("p a (j i) -> p a j i", i=WIN)
                xt = xst[:, g, :].rearrange("p (a j i) -> p a j i", a=1, i=WIN)
                act.activation(xt[0:64], yt[0:64, 1:2], ACT.Copy).then_inc(S["xst_done"], 1)
                act.activation(xt[64:P, :, :, 1:WIN], yt[64:P, 1:2, :, 0:WIN - 1], ACT.Copy).then_inc(S["xst_done"], 1)
                act.activation(xt[64:P, :, :, 0:1], yt[64:P, 0:1, :, WIN - 1:WIN], ACT.Copy).then_inc(S["xst_done"], 1)

            def attend(base, n, w0, y_no, parts=(True, True, True), beside=None):
                a, b, c = parts
                g, G = n % 2, base + n

                def square(c4):
                    act.wait_ge(S["qkv_done"], G * 6 + c4 + 1)
                    act.wait_ge(S["ss_done"], G * 4 + c4 - 1)
                    act.activation(sq[:, c4 % 2, :], QB[c4 % 2][:, :], ACT.Square).then_inc(S["sq_done"], 1)

                if a:
                    if n == 0:
                        stage(G, 0, 0)
                    square(0)
                    square(1)
                if c:
                    act.wait_ge(S["pv_done"], G * 2 - 4)
                    for k in range(2):
                        act.wait_ge(S["pt_done"], (G - 2) * 2 + k + 1)
                        act.activation(pT[:, 4 * k:4 * k + 4, :].rearrange("p m q -> p (m q)"), TB[k][:, :], ACT.Copy).then_inc(S["pt_ev"], 1)
                if beside:
                    beside()
                if a and n < TILES - 1:
                    stage(G + 1, w0 + (n + 1) // 2, 1 - g)
                if b:
                    slot = ((n - 1) // 2) % 2
                    act.wait_ge(S["sc_done"], (G - 1) * 2)
                    for k in range(2):
                        act.wait_ge(S["qkt_done"], (G - 1) * 4 + k + 1)
                        act.activation(qT[:, 4 * k:4 * k + 4, :], TB[k][:, :].rearrange("p (m q) -> p m q", m=4), ACT.Copy).then_inc(S["qkt_ev"], 1)
                if a:
                    square(2)
                if b:
                    for k in range(2):
                        act.wait_ge(S["qkt_done"], (G - 1) * 4 + k + 3)
                        for h2 in range(2):
                            r = slice(64 * h2, 64 * h2 + 64)
                            act.activation(kT[1 - g][r, 4 * k:4 * k + 4, :, h2, slot, :],
                                           TB[k][r, :].rearrange("p (m j q) -> p m j q", m=4, q=WIN), ACT.Copy).then_inc(S["qkt_ev"], 1)
                if a:
                    square(3)
                if c:
                    act.wait_ge(S["y_done"], y_no + 1)
                    for k in range(2):
                        act.wait_ge(S["ot_done"], (G - 2) * 2 + k + 1)
                        act.activation(oT[:, 4 * k:4 * k + 4, g, :], TB[k][:, :].rearrange("p (m q) -> p m q", m=4), ACT.Copy).then_inc(S["ot_ev"], 1)
                if a:
                    act.wait_ge(S[f"vj_ld{g}"], (y_no + 2) * 128)
                    act.wait_ge(S["pv_done"], G * 2 - 2)
                    for k in range(2):
                        act.wait_ge(S["qkv_done"], G * 6 + 5 + k)
                        act.activation(vs[:, g, :, 256 * k:256 * k + 256].rearrange("p a (m d) -> p m a d", d=DH),
                                       QB[k][:, :].rearrange("p (m a d) -> p m a d", a=2, d=DH), ACT.Copy).then_inc(S["v_done"], 1)
                if b:
                    for k in range(2):
                        act.wait_ge(S["sub_done"], (G - 1) * 2 + k + 1)
                        t = pr[:, 1 - g, 4 * k:4 * k + 4, :, :].rearrange("p m a k -> p (m a k)")
                        act.activation(t, t, ACT.Exp, scale=QK_SCALE).then_inc(S["exp_done"], 1)

            def ffn(q, N0, xb):
                squares(N0)
                L = PASSES * DEPTH + q
                K = L * (BATCHES * 3) + CREDIT
                for i in range(3 * BATCHES):
                    act.wait_ge(S["h_done"], L * (BATCHES * 6) + 2 * i + 1)
                    act.wait_ge(S["hm_done"], K + (i - 2 + 1))
                    act.activation(gl[:, i % 2, :], FFB[(2 * i) % 4][:, :], ACT.Silu).then_inc(S["gelu_done"], 1)

            def attention(kind, N0, xb):
                squares(N0)
                units = UNITS[kind]
                with act.Fori(0, SEQS) as s:
                    Q = s + (SEQS * kind + 1)
                    U = s * units + (SEQS * UNITS[0] * kind + UNITS[0])
                    act.wait_ge(S["as_done"], Q * ROWS)
                    act.wait_ge(S["aqk_done"], Q * 4 + 1)
                    for a in range(4):
                        q = slice(32 * a, 32 * a + 32)
                        act.activation(qz[q, 0:2, a, :], LNB[0][q, :].rearrange("p (r n) -> p r n", n=TOKENS), ACT.Copy,
                                       scale=QS[kind]).then_inc(S["aqk_ev"], 1)
                    for k in range(2):
                        act.wait_ge(S["aqk_done"], Q * 4 + k + 3)
                        act.activation(kp[:, 2 * k:2 * k + 2, :], LNB[2 + k][:, :].rearrange("p (r n) -> p r n", n=TOKENS), ACT.Copy).then_inc(S["aqk_ev"], 1)
                    for i in range(ROWS + 3):
                        if i < ROWS:
                            act.wait_ge(S["am_done"], Q * ROWS + i + 1)
                            if i < 4:
                                act.wait_ge(S["an_done"], U)
                            elif kind != DIFF:
                                act.wait_ge(S["an_done"], U + i - 3)
                            else:
                                act.wait_ge(S["an_done" if i % 2 else "an_half"], U + (i - 4) // 2 + 1)
                            for t in range(2):
                                last = act.activation(pe_ring[:, i % 4, t, :], LNB[i % 4][:, TOKENS * t:TOKENS * t + TOKENS], ACT.Exp,
                                                      bias=nm[:, i, t:t + 1], accum_out=dsum[:, i, t:t + 1])
                            last.then_inc(S["ae_done"], 1)
                        u = unit_ready(kind, i - 3)
                        if u is not None:
                            act.wait_ge(S["at_done"], U + u + 1)
                            act.activation(pnT[:, u % 2, :, :], SB[u % 2][:, :].rearrange("p (t k) -> p t k", t=2), ACT.Copy).then_inc(S["at_ev"], 1)
                    if kind == DIFF:
                        act.wait_ge(S["a_on"], Q + 1)
                        act.activation(osq, OB[0][:, 0:TOKENS], ACT.Square).then_inc(S["a_sq"], 1)

            def stack(p, N0, xb):
                squares(N0)
                with act.Fori(0, DEPTH) as l:
                    G, L, N = tile0(p, l), layer0(p, l), ln_no(p, l)
                    act.wait_ge(S["y_ready"], (L + p) * BATCHES + 2)
                    W = L * WINDOWS
                    for n in range(3):
                        attend(G, n, 0, W + (n - 2) // 2, (True, n >= 1, n >= 2))
                    with act.Fori(0, 3) as v:
                        act.wait_ge(S["y_ready"], (L + p + 1) * BATCHES)
                        for n in range(3, 7):
                            attend(G + v * 4, n, v * 2, W + v * 2 + (n - 2) // 2)
                    attend(G, 15, 0, W + 6)
                    attend(G, 16, 0, W + 7, (False, True, True))
                    attend(G, 17, 0, W + 7, (False, False, True), lambda: squares(N, (0,)))
                    K = L * (BATCHES * 3) + CREDIT
                    act.wait_ge(S["ff_ld"], (L + 1) * 160)
                    for i in range(3 * BATCHES):
                        b, c = divmod(i, 3)
                        act.wait_ge(S["h_done"], L * (BATCHES * 6) + 2 * i + 1)
                        act.wait_ge(S["hm_done"], K + (i - 2 + 1))
                        r = slice(0, FFC[c])
                        act.activation(gl[r, i % 2, :], FFB[(2 * i) % 4][r, :], ACT.Gelu, bias=b1[r, 3 + c:4 + c]).then_inc(S["gelu_done"], 1)
                        if i == 2:
                            squares(N, (1,))

            run(stack, attention, ffn)
            for b in range(BATCHES):
                act.wait_ge(S["on_T"], b + 1)
                act.activation(nat[:, nat_tile(b, 0):nat_tile(b, 4), :].rearrange("p t e -> p (t e)"), LNB[b][:, :], ACT.Copy).then_inc(S["on_ev"], 1)

        @block.vector
        def _(dve):
            dve.sem_inc(S["rot_done"], 8 * CREDIT)
            dve.sem_inc(S["ss_done"], 4 * CREDIT)
            dve.sem_inc(S["mx_done"], 2 * CREDIT)
            dve.sem_inc(S["nrm_max"], 2 * CREDIT)
            dve.sem_inc(S["qn_done"], CREDIT)
            dve.sem_inc(S["sub_done"], 2 * CREDIT)
            dve.sem_inc(S["sum_done"], CREDIT)
            dve.sem_inc(S["rs_done"], CREDIT)
            dve.sem_inc(S["on_done"], 2 * CREDIT)
            dve.sem_inc(S["hm_done"], CREDIT)
            for n, k in (("y_add", 1), ("ys_done", 1), ("aq_ev", 4), ("av_ev", 1), ("am_done", ROWS), ("ac_done", ROWS), ("ad_done", UNITS[0]),
                         ("an_half", UNITS[0]), ("an_done", UNITS[0]), ("a_on", 1), ("a_ve", 1), ("a_dg", 2), ("a_on2", 1), ("a_yt", 1)):
                dve.sem_inc(S[n], k)
            dve.wait_ge(S["cst_ld"], 48)
            dve.tensor_copy(mask_bf[:, :, :].rearrange("p a b -> p (a b)"), xs[:, 3, 0:3 * DH]).then_inc(S["mask_done"], 1)
            dve.tensor_copy(ident_bf[:, :], ident[:, :]).then_inc(S["cst_done"], 1)
            dve.memset(mean_w[:, :], 1.0 / P).then_inc(S["cst_done"], 1)
            dve.memset(mhalf[:, :], -0.5).then_inc(S["cst_done"], 1)
            for g in range(2):
                dve.memset(kT[g][:, :, :, :, :, :], 0.0)
                dve.memset(vj[g][:, :, :, :], 0.0)
            dve.memset(Y[:, :, 0, :], 0.0).then_inc(S["cst_done"], 1)

            def centre(N, h, src, ready):
                for b in (2 * h, 2 * h + 1):
                    dve.wait_ge(S["ln_mean"], N * BATCHES + b + 1)
                    ready(b)
                    dve.tensor_tensor(cen[:, b, :], src(b), LNB[b][:, :], ALU.subtract).then_inc(S["ln_cen"], 1)

            def guarded(N, h):
                dve.wait_ge(S["ln_ss"], N * BATCHES + 2 * h + 2)
                dve.tensor_scalar(ve[:, 8 * h:8 * h + 8], LNB[2 * h][:, 0:8], 1e-5, None, ALU.add).then_inc(S["ln_ve"], 1)

            def diagonals(N, h):
                dve.wait_ge(S["ln_rs"], N * 2 + h + 1)
                for b in (2 * h, 2 * h + 1):
                    dve.tensor_tensor(sqd[:, b, :].rearrange("p (t k) -> p t k", k=P), ident[:, :].unsqueeze(1).to_broadcast([P, 4, P]),
                                      rstd[:, 4 * b:4 * b + 4].unsqueeze(2).to_broadcast([P, 4, P]), ALU.mult).then_inc(S["ln_dg"], 1)

            def scale(N, h, dst, done, affine=None):
                for b in (2 * h, 2 * h + 1):
                    dve.wait_ge(S["ln_bc"], N * BATCHES + b + 1)
                    dve.tensor_tensor(dst(b), cen[:, b, :], LNB[b][:, :], ALU.mult).then_inc(S["ln_xn" if affine else done], 1)
                    if affine:
                        dve.wait_ge(S["ln_xn"], affine(b))
                        dve.tensor_scalar(dst(b), dst(b), lnp[:, 0:1], lnp[:, 1:2], ALU.mult, ALU.add).then_inc(S[done], 1)

            def norm(N, src, ready, dst, done):
                for h in range(2):
                    centre(N, h, src, ready)
                for h in range(2):
                    guarded(N, h)
                for h in range(2):
                    diagonals(N, h)
                for h in range(2):
                    scale(N, h, dst, done)

            def attend(base, n, w_a, w_c, y_no, parts=(True, True, True), beside=None):
                a, b, c = parts
                g, G = n % 2, base + n

                def rotate(c4):
                    k = 2 * (c4 // 2)
                    dve.wait_ge(S["sq_done"], G * 4 + c4 + 1)
                    dve.wait_ge(S["add_done"], G * 4 + c4 - 1)
                    q = QB[c4 % 2][:, :].rearrange("p (h t d) -> p h t d", t=2, d=DH // 2)
                    cos = rot[:, k, bass.ds(w_a, 1), :]
                    sin = rot[:, k + 1, bass.ds(w_a, 1), :]
                    dve.tensor_tensor(t1[:, g, c4, :].rearrange("p (h d) -> p h d", d=DH), QB[c4 % 2][:, :].rearrange("p (h d) -> p h d", d=DH),
                                      cos.to_broadcast([P, 8, DH]), ALU.mult).then_inc(S["rot_done"], 1)
                    dve.tensor_tensor(t2[:, c4 % 2, :].rearrange("p (h t d) -> p h t d", t=2, d=DH // 2), q[:, :, ::-1, :],
                                      sin.rearrange("p w (t d) -> p w t d", t=2).to_broadcast([P, 8, 2, DH // 2]),
                                      ALU.mult).then_inc(S["rot_done"], 1)
                    dve.tensor_reduce(ss[:, g, 8 * c4:8 * c4 + 8], sq[:, c4 % 2, :].rearrange("p (h d) -> p h d", d=DH),
                                      AX.X, ALU.add).then_inc(S["ss_done"], 1)

                def guard(k):
                    dve.wait_ge(S["ss_done"], G * 4 + 2 * k + 2)
                    dve.wait_ge(S["nrm_pow"], G * 2 - 2)
                    dve.tensor_scalar(rn[:, g, 0, 16 * k:16 * k + 16], ss[:, g, 16 * k:16 * k + 16], 1e-24, None, ALU.max).then_inc(S["nrm_max"], 1)

                def residual(w_, y_):
                    dve.wait_ge(S["y_done"], y_ + 2)
                    y = Y[:, :, bass.ds(w_ + 1, 1), :]
                    dve.tensor_tensor(y, OB[0][:, 0:2 * P].rearrange("p (g w c) -> p g w c", g=2, w=1), y, ALU.add).then_inc(S["y_add"], 1)

                if a:
                    dve.wait_ge(S["qkt_done"], G * 4 - 4)
                    rotate(0)
                    rotate(1)
                    guard(0)
                if c and g == 0 and n > 2:
                    residual(w_c - 1, y_no - 1)
                if c:
                    Gc = G - 2
                    dve.wait_ge(S["exp_done"], Gc * 2 + 2)
                    dve.tensor_reduce(sm[:, g, :], pr[:, g, :, :, :].rearrange("p m a k -> p (m a) k"), AX.X, ALU.add).then_inc(S["sum_done"], 1)
                    dve.wait_ge(S["sum_done"], Gc + 1)
                    dve.reciprocal(rs[:, g, :], sm[:, g, :]).then_inc(S["rs_done"], 1)
                    dve.wait_ge(S["rs_done"], Gc + 1)
                    dve.wait_ge(S["ot_done"], Gc * 2)
                    for k in range(2):
                        dve.wait_ge(S["pv_done"], Gc * 2 + k + 1)
                        dve.tensor_tensor(osb[:, 4 * k:4 * k + 4, :, :].rearrange("p m a d -> p (m a) d"),
                                          OB[k][:, :].rearrange("p (h d) -> p h d", d=DH),
                                          rs[:, g, 8 * k:8 * k + 8].unsqueeze(2).to_broadcast([P, 8, DH]), ALU.mult).then_inc(S["on_done"], 1)
                if beside:
                    beside()
                if a:
                    rotate(2)
                    rotate(3)
                    guard(1)
                    dve.wait_ge(S["nrm_pow"], G * 2 + 1)
                    dve.wait_ge(S["add_done"], G * 4 + 2)
                    t = t1[:, g, 0:2, :].rearrange("p c (h d) -> p (c h) d", d=DH)
                    dve.tensor_tensor(t, t, rn[:, g, 1, 0:16].unsqueeze(2).to_broadcast([P, 16, DH]), ALU.mult).then_inc(S["qn_done"], 1)
                if b:
                    Gb, gb = G - 1, 1 - g
                    dve.wait_ge(S["pt_done"], (Gb - 1) * 2)
                    dve.wait_ge(S["sum_done"], Gb)
                    for k in range(2):
                        dve.wait_ge(S["sc_done"], Gb * 2 + k + 1)
                        dve.tensor_reduce(mx[:, gb, 8 * k:8 * k + 8], SB[k][:, :].rearrange("p (h k) -> p h k", k=DH), AX.X, ALU.max).then_inc(S["mx_done"], 1)
                    for k in range(2):
                        dve.wait_ge(S["mx_done"], Gb * 2 + k + 1)
                        dve.tensor_tensor(pr[:, gb, 4 * k:4 * k + 4, :, :].rearrange("p m a k -> p (m a) k"),
                                          SB[k][:, :].rearrange("p (h k) -> p h k", k=DH),
                                          mx[:, gb, 8 * k:8 * k + 8].unsqueeze(2).to_broadcast([P, 8, DH]), ALU.subtract).then_inc(S["sub_done"], 1)
                if g == 1 and not a:
                    residual(w_c, y_no)

            def x_ready(xb):
                if xb == 0:
                    return lambda b: dve.wait_ge(S["xt_ev"], b + 1)
                return lambda b: dve.wait_ge(S["x_done"], xb)

            def ffn(q, N0, xb):
                if q == 0:
                    dve.wait_ge(S["int_ld"], 48)
                    for m in range(3):
                        dve.tensor_scalar(wqkv[:, HID * m:HID * m + HID], iraw[:, m, :], float(np.float32(1.0 / 127.0)), None, ALU.mult).then_inc(S["wi_cv"], 1)
                    for m in range(3):
                        dve.wait_ge(S["wi_done"], m + 1)
                        dve.tensor_copy(wi[:, m, :], FFB[m][:, 0:HID]).then_inc(S["wi_ev"], 1)
                norm(N0, lambda b: batch(b, X), x_ready(xb), lambda b: cen[:, b, :], "n_out")
                L = PASSES * DEPTH + q
                K = L * (BATCHES * 3) + CREDIT

                def join(b):
                    dve.wait_ge(S["f_done"], L * BATCHES + b + 1)
                    dve.scalar_tensor_tensor(batch(b, X), TB[b % 2][:, :], 0.5, batch(b, X), ALU.mult, ALU.add).then_inc(S["x_done"], 1)

                for i in range(3 * BATCHES):
                    b, c = divmod(i, 3)
                    dve.wait_ge(S["h_done"], L * (BATCHES * 6) + 2 * i + 2)
                    dve.wait_ge(S["gelu_done"], K + i + 1)
                    if c == 0 and b >= 2:
                        dve.wait_ge(S["f_done"], L * BATCHES + b - 1)
                    dve.tensor_tensor(hh[:, b % 2, c, :], FFB[(2 * i + 1) % 4][:, :], gl[:, i % 2, :], ALU.mult).then_inc(S["hm_done"], 1)
                    if c == 2 and b >= 1:
                        join(b - 1)
                join(BATCHES - 1)

            def attention(kind, N0, xb):
                dh = DHS[kind]
                units = UNITS[kind]
                if kind == DIFF:
                    dve.wait_ge(S["raw_ld"], 16 * 11)
                    dve.tensor_scalar(vec[:, 1:2], vec[:, 0:1], -1.0, None, ALU.mult).then_inc(S["vec_done"], 1)
                    dve.tensor_scalar(vec[:, 2:3], vec[:, 0:1], -1.0, 1.0, ALU.mult, ALU.add).then_inc(S["vec_done"], 1)
                    dve.wait_ge(S["vec_done"], 2)
                    dve.tensor_tensor(vec[:, 5:6], vec[:, 4:5], vec[:, 2:3], ALU.mult).then_inc(S["vec_done"], 1)
                    dve.wait_ge(S["vec_done"], 3)
                    dve.wait_ge(S["wt_done"], 1)
                    for k, dst in ((2, wv), (3, wot)):
                        dve.tensor_copy(dst, SB[0][:, P * k:P * k + P]).then_inc(S["wt_ev"], 1)
                dve.memset(qz[:, :, :, :], 0.0).then_inc(S["wdup_done"], 1)
                dve.memset(rotf[:, 0:1024], 0.0).then_inc(S["wdup_done"], 1)
                dve.memset(vpad[:, :, :, :], 0.0).then_inc(S["wdup_done"], 1)
                dve.wait_ge(S["wdup_done"], 5 * kind + 3)
                for k, dst in ((0, wqp), (1, wkp)):
                    src = SB[0][:, P * k:P * k + P] if kind == DIFF else wraw[:, 4 + k, :]
                    dve.tensor_copy(dst[:, :, 0:8], src.rearrange("p (n d) -> p n d", d=8)).then_inc(S["wdup_done"], 1)
                norm(N0, lambda b: batch(b, X), x_ready(xb), lambda b: cen[:, b, :], "n_out")
                norms = (1 if kind == DIFF else 3)
                dve.wait_ge(S["n_out"], norms * BATCHES)
                ycen = cen[:, :, :].rearrange("p (h g) (w c) -> p g h w c", g=GROUPS, w=4)
                per = 32 // dh
                with dve.Fori(0, GROUPS) as gq, dve.Fori(0, QUADS) as jq:
                    s = gq * QUADS + jq
                    Q = s + (SEQS * kind + 1)
                    U = s * units + (SEQS * UNITS[0] * kind + UNITS[0])
                    dve.wait_ge(S["av_done"], Q)
                    dve.tensor_copy(ys.rearrange("p (h w i) -> p h w i", h=2, i=WIN),
                                    ycen[:, bass.ds(gq, 1), :, :, bass.ds(jq * WIN, WIN)].rearrange("p g h w i -> p (g h) w i")).then_inc(S["ys_done"], 1)
                    dve.wait_ge(S["as_done"], Q * ROWS)
                    dve.wait_ge(S["aqk_done"], Q * 4 + 2)
                    for a in range(4):
                        q = slice(32 * a, 32 * a + 32)
                        dve.tensor_scalar(qz[q, 2:4, a, :], LNB[1][q, :].rearrange("p (r n) -> p r n", n=TOKENS), QS[kind], None, ALU.mult).then_inc(S["aq_ev"], 1)
                    dve.wait_ge(S["av_done"], Q + 1)
                    dve.wait_ge(S["apv_done"], Q)
                    for h in range(per):
                        src = SB[0][:, 0:TOKENS].rearrange("p (t c h d) -> p t c h d", t=2, h=per, d=dh)
                        dst = vpad[:, :, 0:units, :].rearrange("p t (c h) d -> p t c h d", h=per)
                        o = dve.tensor_copy(dst[:, :, :, h, dh * h:dh * h + dh], src[:, :, :, h, :])
                    o.then_inc(S["av_ev"], 1)

                    def finish(i):
                        dve.wait_ge(S["ae_done"], Q * ROWS + i + 1)
                        dve.reciprocal(drc[:, 0, i, :], dsum[:, i, :]).then_inc(S["ac_done"], 1)
                        dve.wait_ge(S["ac_done"], Q * ROWS + i + 1)
                        u = i if kind else i // 2
                        if kind or i % 2 == 0:
                            if u >= 2:
                                dve.wait_ge(S["at_done"], U + u - 1)
                            for t in range(2):
                                o = dve.tensor_scalar(pn_ring[:, u % 2, t, :], pe_ring[:, i % 4, t, :], drc[:, 0, i, t:t + 1], None, ALU.mult)
                            o.then_inc(S["an_done" if kind else "an_half"], 1)
                        else:
                            dve.tensor_scalar(drc[:, 1, i, :], drc[:, 0, i, :], vec[:, 1:2], None, ALU.mult).then_inc(S["ad_done"], 1)
                            dve.wait_ge(S["ad_done"], U + u + 1)
                            dve.wait_ge(S["an_half"], U + u + 1)
                            for t in range(2):
                                o = dve.scalar_tensor_tensor(pn_ring[:, u % 2, t, :], pe_ring[:, i % 4, t, :], drc[:, 1, i, t:t + 1],
                                                             pn_ring[:, u % 2, t, :], ALU.mult, ALU.add)
                            o.then_inc(S["an_done"], 1)

                    for i in range(ROWS + 2):
                        if i < ROWS:
                            dve.wait_ge(S["as_done"], Q * ROWS + i + 1)
                            dve.tensor_reduce(nm[:, i, :], LNB[i % 4][:, :].rearrange("p (t k) -> p t k", t=2), AX.X, ALU.max, negate=True).then_inc(S["am_done"], 1)
                        if i >= 2:
                            finish(i - 2)
                    dve.wait_ge(S["apv_done"], Q + 1)
                    o = seq_cols(X, gq, jq)
                    if kind == DIFF:
                        dve.tensor_scalar(on, OB[0][:, 0:TOKENS], vec[:, 3:4], None, ALU.mult).then_inc(S["a_on"], 1)
                        dve.wait_ge(S["a_ss"], Q + 1)
                        dve.tensor_scalar(ave[:, :], OB[1][:, 0:2], float(np.finfo(np.float32).eps), None, ALU.add).then_inc(S["a_ve"], 1)
                        dve.wait_ge(S["a_rs"], Q + 1)
                        for t in range(2):
                            dve.tensor_scalar(odg[:, P * t:P * t + P], ident[:, :], ars[:, t:t + 1], None, ALU.mult).then_inc(S["a_dg"], 1)
                        dve.wait_ge(S["a_bc"], Q + 1)
                        dve.tensor_tensor(on2, on, OB[1][:, 0:TOKENS], ALU.mult).then_inc(S["a_on2"], 1)
                        dve.wait_ge(S["a_y"], Q + 1)
                        dve.tensor_scalar(ott, OB[0][:, 0:TOKENS], vec[:, 2:3], vec[:, 5:6], ALU.mult, ALU.add).then_inc(S["a_yt"], 1)
                        dve.wait_ge(S["a_yt"], Q + 1)
                        dve.tensor_tensor(o, ott.rearrange("p (w i) -> p w i", i=WIN), o, ALU.add).then_inc(S["x_done"], 1)
                    else:
                        dve.tensor_copy(on, OB[0][:, 0:TOKENS]).then_inc(S["a_on"], 1)
                        dve.wait_ge(S["a_y"], Q + 1)
                        dve.scalar_tensor_tensor(o, OB[0][:, 0:TOKENS].rearrange("p (w i) -> p w i", i=WIN), vec[:, 6:7], o, ALU.add, ALU.add).then_inc(S["x_done"], 1)

            def stack(p, N0, xb):
                if p:
                    dve.wait_ge(S["as_done"], (SEQS + 1) * ROWS)
                    dve.memset(qz[:, :, :, :], 0.0)
                norm(N0, lambda b: batch(b, X), x_ready(xb), lambda b: batch(b, Y), "y_ready")
                with dve.Fori(0, DEPTH) as l:
                    G, L, N = tile0(p, l), layer0(p, l), ln_no(p, l)
                    dve.wait_ge(S["tab_done"], L * 4 + 8)
                    dve.wait_ge(S["y_ready"], (L + p + 1) * BATCHES)
                    W = L * WINDOWS
                    for n in range(3):
                        attend(G, n, n // 2, (n - 2) // 2, W + (n - 2) // 2, (True, n >= 1, n >= 2))
                    with dve.Fori(0, 3) as v:
                        for n in range(3, 7):
                            wc = v * 2 + (n - 2) // 2
                            attend(G + v * 4, n, v * 2 + n // 2, wc, W + wc)
                    attend(G, 15, 7, 6, W + 6)

                    def stage(h):
                        for b in (2 * h, 2 * h + 1):
                            src = Y[:, b % 2, :, :].rearrange("p w (j i) -> p w j i", i=WIN)
                            own = src[:, 1 + 4 * h:5 + 4 * h]
                            bef = src[:, 4 * h:4 * h + 4]
                            dst = xs[:, b, :].rearrange("p (w j i) -> p w j i", j=QUADS, i=WIN)
                            dve.tensor_copy(dst[0:64], own[0:64]).then_inc(S["xs_done"], 1)
                            dve.tensor_copy(dst[64:P, :, :, 1:WIN], own[64:P, :, :, 0:WIN - 1]).then_inc(S["xs_done"], 1)
                            dve.tensor_copy(dst[64:P, :, :, 0:1], bef[64:P, :, :, WIN - 1:WIN]).then_inc(S["xs_done"], 1)

                    def staged(b):
                        dve.wait_ge(S["xs_done"], L * 12 + 3 * b + 3)

                    def first_half():
                        dve.wait_ge(S["y_add"], W + 5)
                        dve.wait_ge(S["vj_ld0"], (W + (WINDOWS + 1)) * 128)
                        stage(0)

                    def first_scale():
                        guarded(N, 0)
                        diagonals(N, 0)

                    attend(G, 16, 0, 7, W + 7, (False, True, True), first_half)
                    centre(N, 0, lambda b: xs[:, b, :], staged)
                    attend(G, 17, 0, 7, W + 7, (False, False, True), first_scale)
                    dve.wait_ge(S["y_add"], W + (WINDOWS + 1))
                    dve.wait_ge(S["vj_ld1"], (W + (WINDOWS + 1)) * 128)
                    dve.wait_ge(S["ff_ld"], (L + 1) * 160)
                    scale(N, 0, lambda b: cen[:, b, :], "ln_out", lambda b: L * BATCHES + b + 1)
                    stage(1)
                    K = L * (BATCHES * 3) + CREDIT

                    def join(b):
                        dve.wait_ge(S["f_done"], L * BATCHES + b + 1)
                        dve.scalar_tensor_tensor(batch(b, Y), QB[b % 2][:, :], lnp[:, 2:3], batch(b, Y), ALU.add, ALU.add).then_inc(S["y_ready"], 1)

                    for i in range(3 * BATCHES):
                        b, c = divmod(i, 3)
                        dve.wait_ge(S["h_done"], L * (BATCHES * 6) + 2 * i + 2)
                        dve.wait_ge(S["gelu_done"], K + i + 1)
                        if c == 0 and b >= 2:
                            dve.wait_ge(S["f_done"], L * BATCHES + b - 1)
                        r = slice(0, FFC[c])
                        dve.scalar_tensor_tensor(hh[r, b % 2, c, :], FFB[(2 * i + 1) % 4][r, :], b1[r, c:c + 1], gl[r, i % 2, :],
                                                 ALU.add, ALU.mult).then_inc(S["hm_done"], 1)
                        if i == 2:
                            centre(N, 1, lambda b: xs[:, b, :], staged)
                        elif i == 3:
                            guarded(N, 1)
                        elif i == 5:
                            diagonals(N, 1)
                            join(0)
                            join(1)
                            scale(N, 1, lambda b: cen[:, b, :], "ln_out", lambda b: L * BATCHES + b + 1)
                    join(2)
                    join(3)
                for b in range(BATCHES):
                    dve.wait_ge(S["y_ready"], (DEPTH * (p + 1) + p) * BATCHES + b + 1)
                    dve.scalar_tensor_tensor(batch(b, X), batch(b, Y), 0.5, batch(b, X), ALU.mult, ALU.add).then_inc(S["x_done"], 1)

            run(stack, attention, ffn)


INPUTS = ["L0_attn_Wq", "L0_attn_Wk", "L0_attn_Wv", "L0_attn_norm_w", "L0_attn_Wo", "L0_attn_bo",
          "L0_attn_diff_weight", "L0_ffn_Wqkv", "L0_ffn_q_scale", "L0_ffn_k_scale", "L0_ffn_Wo", "L0_ffn_ln_g",
          "L0_ffn_ln_b", "L0_ffn_W1", "L0_ffn_b1", "L0_ffn_W2", "L0_ffn_b2", "L1_attn_Wk", "L1_attn_Wq",
          "L1_attn_Wo", "L1_attn_bo", "L1_ffn_w_gate", "L1_ffn_w_up", "L1_ffn_w_down"]


def build_program(nc, inputs):
    fp32 = mybir.dt.float32
    arrays, aps = {}, {}
    for name in ["L0_attn_x"] + INPUTS:
        a = np.ascontiguousarray(inputs[name])
        if a.ndim == 0:
            a = a.reshape(1)
        arrays[name] = a
        aps[name] = nc.dram_tensor(name, a.shape, mybir.dt.from_np(a.dtype), kind="ExternalInput").ap()
    cst = []
    for name, a in zip(("rotary", "mask", "identity"), shape_constants()):
        arrays[name] = a
        cst.append(nc.dram_tensor(name, a.shape, fp32, kind="ExternalInput").ap())
    out = nc.dram_tensor("out", (SEQS, TOKENS, P), fp32, kind="ExternalOutput").ap()
    macaron(nc, aps["L0_attn_x"], aps, cst, out)
    return arrays


def kernel(**inputs):
    import concourse.bacc as bacc
    from concourse.bass_utils import run_bass_kernel_spmd

    nc = bacc.Bacc("TRN2", target_bir_lowering=False, num_devices=1)
    arrays = build_program(nc, inputs)
    r = run_bass_kernel_spmd(nc, [arrays], core_ids=[0])
    return r.results[0]["out"]
```
